# Optimizing a Trainium2 kernel written in Bass

```python
import numpy as np
import jax
import jax.numpy as jnp

def _softmax(x, axis=-1):
    return jax.nn.softmax(x, axis=axis)

def _gelu(x):
    return jax.nn.gelu(x, approximate=True)

def _silu(x):
    return jax.nn.silu(x)

def _sigmoid(x):
    return jax.nn.sigmoid(x)

def _layernorm(x, axis=-1, eps=1e-05):
    m = jnp.mean(x, axis=axis, keepdims=True)
    v = jnp.var(x, axis=axis, keepdims=True)
    return (x - m) / jnp.sqrt(v + eps)

def _scatter_add(tgt, idx, src, axis=0):
    return tgt.at[idx].add(src)

def _segment_sum(src, seg, n):
    return jax.ops.segment_sum(src, seg, n)
kernel_name = 'mk_xattn_ffn_d1_seqx_r4_112bde'

def setup_inputs(seed: int=0):
    np.random.seed(seed)
    _w = jnp.asarray

    def _rec_inputs():
        import jax
        import jax.numpy as jnp
        _rk = jax.random.key(seed)
        x = -0.0005207 + 1.001 * jax.random.normal(jax.random.fold_in(_rk, 1), (32, 128, 256), jnp.float32)
        _lenS = 128 - jax.random.randint(jax.random.fold_in(_rk, 7), (32,), 0, max(1, 128 // 4) + 1, jnp.int32)
        _lenS2 = 128 - jax.random.randint(jax.random.fold_in(_rk, 8), (32,), 0, max(1, 128 // 4) + 1, jnp.int32)
        _ctx_1024P = jax.random.normal(jax.random.fold_in(_rk, 11), (32, 16, 256), jnp.float32)
        _ctx_1024c = jax.random.dirichlet(jax.random.fold_in(_rk, 511), 0.3 * jnp.ones((16,), jnp.float32), (32, 128))
        _ctx_1024t = jnp.einsum('bsk,bkd->bsd', _ctx_1024c, _ctx_1024P)
        _ctx_1024t = _ctx_1024t * jax.lax.rsqrt(jnp.mean(jnp.square(_ctx_1024t)) + 1e-12) * 0.953939
        ctx_1024 = -0.000514642 + 1.00011 * (_ctx_1024t + 0.3 * jax.random.normal(jax.random.fold_in(_rk, 611), (32, 128, 256), jnp.float32))
        return (x, ctx_1024)
    x, ctx_1024 = _rec_inputs()

    def _L0_xattn_setup():
        import jax, jax.numpy as jnp
        import numpy as np
        B, S, E, NH = (1, 512, 256, 8)
        DH = E // NH
        EPS = 1e-06
        LN_EPS = 1e-05
        key = jax.random.key(seed)
        ks = jax.random.split(key, 8)
        q = jax.random.normal(ks[0], (B, S, E), dtype=jnp.float32)
        k = jax.random.normal(ks[1], (B, S, E), dtype=jnp.float32)
        v = jax.random.normal(ks[2], (B, S, E), dtype=jnp.float32)
        scale = 1.0 / np.sqrt(3 * E)
        igate_w = jax.random.normal(ks[3], (NH, 3 * E), dtype=jnp.float32) * scale
        igate_b = jax.random.normal(ks[4], (NH,), dtype=jnp.float32) * 0.1
        fgate_w = jax.random.normal(ks[5], (NH, 3 * E), dtype=jnp.float32) * scale
        fgate_b = jnp.linspace(3.0, 6.0, NH, dtype=jnp.float32)
        out_w = 1.0 + 0.1 * jax.random.normal(ks[6], (E,), dtype=jnp.float32)
        return {'q': q, 'k': k, 'v': v, 'igate_w': igate_w, 'igate_b': igate_b, 'fgate_w': fgate_w, 'fgate_b': fgate_b, 'out_w': out_w}
    _L0_xattn_all = _L0_xattn_setup()
    _L0_xattn_in = {k: v for k, v in _L0_xattn_all.items() if k in ('igate_w', 'igate_b', 'fgate_w', 'fgate_b', 'out_w')}
    del _L0_xattn_all

    def _L0_ffn_setup():
        import jax, jax.numpy as jnp
        import numpy as np
        TOP_K = 2
        key = jax.random.key(seed)
        ks = jax.random.split(key, 6)
        B, S, D, F, E = (2, 512, 256, 1024, 8)
        sd = 1.0 / np.sqrt(D)
        sf = 1.0 / np.sqrt(F)
        return {'x': jax.random.normal(ks[0], (B, S, D), jnp.float32), 'gate_w': jax.random.normal(ks[1], (D, E), jnp.float32) * sd, 'w1': jax.random.normal(ks[2], (E, D, F), jnp.float32) * sd, 'b1': jax.random.normal(ks[3], (E, F), jnp.float32) * 0.01, 'w2': jax.random.normal(ks[4], (E, F, D), jnp.float32) * sf, 'b2': jax.random.normal(ks[5], (E, D), jnp.float32) * 0.01}
    _L0_ffn_all = _L0_ffn_setup()
    _L0_ffn_in = {k: v for k, v in _L0_ffn_all.items() if k in ('gate_w', 'w1', 'b1', 'w2', 'b2')}
    del _L0_ffn_all
    return {'x': x, 'ctx_1024': ctx_1024, 'L0_xattn_igate_w': _L0_xattn_in['igate_w'], 'L0_xattn_igate_b': _L0_xattn_in['igate_b'], 'L0_xattn_fgate_w': _L0_xattn_in['fgate_w'], 'L0_xattn_fgate_b': _L0_xattn_in['fgate_b'], 'L0_xattn_out_w': _L0_xattn_in['out_w'], 'L0_ffn_gate_w': _L0_ffn_in['gate_w'], 'L0_ffn_w1': _L0_ffn_in['w1'], 'L0_ffn_b1': _L0_ffn_in['b1'], 'L0_ffn_w2': _L0_ffn_in['w2'], 'L0_ffn_b2': _L0_ffn_in['b2']}

def reference(x, ctx_1024, L0_xattn_igate_w, L0_xattn_igate_b, L0_xattn_fgate_w, L0_xattn_fgate_b, L0_xattn_out_w, L0_ffn_gate_w, L0_ffn_w1, L0_ffn_b1, L0_ffn_w2, L0_ffn_b2):
    import jax
    import jax.numpy as jnp

    def _L0_xattn_ref(q, k, v, igate_w, igate_b, fgate_w, fgate_b, out_w):
        import jax, jax.numpy as jnp
        import numpy as np
        B, S, E, NH = (1, 512, 256, 8)
        DH = E // NH
        EPS = 1e-06
        LN_EPS = 1e-05
        Bq, Sq, Eq = q.shape
        nh = igate_b.shape[0]
        dh = Eq // nh
        gi = jnp.concatenate([q, k, v], axis=-1)
        ig = (gi @ igate_w.T + igate_b).transpose(0, 2, 1)
        fg = (gi @ fgate_w.T + fgate_b).transpose(0, 2, 1)
        qh = q.reshape(Bq, Sq, nh, dh).transpose(0, 2, 1, 3)
        kh = k.reshape(Bq, Sq, nh, dh).transpose(0, 2, 1, 3)
        vh = v.reshape(Bq, Sq, nh, dh).transpose(0, 2, 1, 3)
        log_f = jax.nn.log_sigmoid(fg)
        cs = jnp.cumsum(log_f, axis=-1)
        diff = cs[..., :, None] - cs[..., None, :]
        mask = jnp.tril(jnp.ones((Sq, Sq), dtype=bool))
        log_fg_mat = jnp.where(mask, diff, -jnp.inf)
        log_D = log_fg_mat + ig[..., None, :]
        max_log_D = jnp.max(log_D, axis=-1, keepdims=True)
        D = jnp.exp(log_D - max_log_D)
        qk = jnp.einsum('bhsd,bhtd->bhst', qh, kh) / jnp.sqrt(jnp.float32(dh))
        C = qk * D
        normalizer = jnp.maximum(jnp.abs(C.sum(-1, keepdims=True)), jnp.exp(-max_log_D))
        h = jnp.einsum('bhst,bhtd->bhsd', C / (normalizer + EPS), vh)
        mean = h.mean(-1, keepdims=True)
        var = ((h - mean) ** 2).mean(-1, keepdims=True)
        hn = (h - mean) / jnp.sqrt(var + LN_EPS)
        hn = hn * out_w.reshape(nh, dh)[None, :, None, :]
        return hn.transpose(0, 2, 1, 3).reshape(Bq, Sq, Eq)

    def _L0_ffn_ref(x, gate_w, w1, b1, w2, b2):
        import jax, jax.numpy as jnp
        import numpy as np
        TOP_K = 2
        B, S, D = x.shape
        T = B * S
        xf = x.reshape(T, D)
        gate_scores = jax.nn.softmax(xf @ gate_w, axis=-1)
        topk_scores, topk_idx = jax.lax.top_k(gate_scores, TOP_K)
        topk_scores = topk_scores / jnp.sum(topk_scores, axis=-1, keepdims=True)
        h = jax.nn.gelu(jnp.einsum('td,edf->etf', xf, w1) + b1[:, None, :], approximate=False)
        y = jnp.einsum('etf,efd->etd', h, w2) + b2[:, None, :]
        tok = jnp.arange(T)
        y_sel = y[topk_idx.T, tok[None, :]]
        out = jnp.einsum('kt,ktd->td', topk_scores.T, y_sel)
        return out.reshape(B, S, D)
    x = x + _L0_xattn_ref(_layernorm(x, axis=-1), ctx_1024, ctx_1024, L0_xattn_igate_w, L0_xattn_igate_b, L0_xattn_fgate_w, L0_xattn_fgate_b, L0_xattn_out_w)
    x = x + _L0_ffn_ref(_layernorm(x, axis=-1), L0_ffn_gate_w, L0_ffn_w1, L0_ffn_b1, L0_ffn_w2, L0_ffn_b2)
    return x

_drawn_inputs = setup_inputs


def setup_inputs(seed=0):
    import zlib

    import numpy as np

    out = dict(_drawn_inputs(seed))
    spreads = {}
    factors = {'L0_xattn_igate_b': 64.0, 'L0_ffn_b1': 8.0, 'L0_ffn_b2': 8.0}
    for name, (base, spread) in spreads.items():
        noise = np.random.default_rng([zlib.crc32(name.encode()), seed]).standard_normal(out[name].shape)
        drawn = base * np.exp(spread * noise) if base else spread * noise
        out[name] = jnp.asarray(drawn.astype(out[name].dtype))
    for name, factor in factors.items():
        out[name] = (out[name] * factor).astype(out[name].dtype)
    return out
```

```python
from contextlib import ExitStack

import concourse.bass as bass
from concourse import mybir

ALU = mybir.AluOpType
ACT = mybir.ActivationFunctionType
AX = mybir.AxisListType.X
F32 = mybir.dt.float32
F16 = mybir.dt.float16
BF16 = mybir.dt.bfloat16
I32 = mybir.dt.int32

P = 128
EPS = 1e-6
LN_EPS = 1e-5
BIG = 1e30
W_SCALE = 64.0


class Chain:

    def __init__(self, sem, per_step):
        self.sem, self.per_step, self.base, self.n = sem, per_step, 0, 0

    def begin(self, step):
        self.base, self.n = step * self.per_step, 0

    def inc(self, ins):
        self.n += 1
        ins.then_inc(self.sem, 1)

    def wait(self, eng):
        eng.wait_ge(self.sem, self.base + self.n)

    def link(self, eng, ins):
        self.inc(ins)
        self.wait(eng)

    def end(self):
        assert self.n == self.per_step, (self.n, self.per_step)


def build(nc, x, ctx_in, igate_w, igate_b, fgate_w, fgate_b, out_w, gate_w, w1, b1, w2, b2, out):
    NB, S, D = x.shape
    NH = igate_b.shape[0]
    DH = D // NH
    HG = P // DH
    KC = D // P
    NE, _, F = w1.shape
    FC = F // P
    SB = 4
    NSTEP = NB // SB
    T = NB * S
    G = SB * NH
    QK_SCALE = float(DH) ** -0.5
    assert S == P and D == KC * P and NH == KC * HG and NSTEP % 2 == 0
    NT = (2 * T + NE * (P - 1)) // P
    NL = NT + 2
    PAD_ROW = NE * T
    TABLE = NE * T + P
    TB = TABLE // P
    LOOP_TURNS = (NT - 3) // 4
    assert 4 * LOOP_TURNS + 3 == NT

    DVE_NEXT, DVE_HERE, ACT_NEXT, ACT_HERE = 14, 47, 2, 2

    xs_dram = x.rearrange("(g j) s d -> g s j d", j=SB)
    ctx_dram = ctx_in.rearrange("(g j) s d -> g s j d", j=SB)
    out_dram = out.rearrange("(g j) s d -> g s j d", j=SB)
    out_rows = out.rearrange("b s d -> (b s) d")
    xf_dram = nc.dram_tensor("xf_rows", (T, D), F32, kind="Internal").ap()
    xf_step = xf_dram.rearrange("(g j s) d -> g s j d", j=SB, s=S)
    scan_dram = nc.dram_tensor("scan_rows", (NSTEP, G, P), F32, kind="Internal").ap()
    table = nc.dram_tensor("expert_table", (TABLE, 2), I32, kind="Internal").ap()
    w1_dram = w1.rearrange("e (k p) f -> (e k) p f", p=P)
    w2_dram = w2.rearrange("e (h c p) d -> (e h) p c d", h=2, p=P)
    NPIECE = NE * 4
    PW = 1024
    assert NPIECE == NB and F == PW and FC * D == 2 * PW

    with ExitStack() as ctx:
        def sb(name, shape, dt=F32):
            return ctx.enter_context(nc.sbuf_tensor(name, shape, dt))

        def sem(name):
            return ctx.enter_context(nc.semaphore(name))

        w1s = sb("w1_halves", [P, NE, 2, KC, F], F16)
        w2s = sb("w2_halves", [P, NE, 2, FC, D], F16)
        xbuf = sb("x_slots", [P, 2, SB, D])
        ctxb = sb("ctx_slots", [P, SB, D])
        normed = sb("normed", [P, SB, D])
        vaug = sb("v_centred_and_one", [P, 2, SB, NH, DH + 1])
        qkT = sb("q_and_k_transposed", [P, 2, SB, 2 * KC, P])
        E = sb("decay_slots", [P, SB, NH, P])
        Hs = sb("h_slots", [P, SB, NH, DH + 1])
        work = sb("work", [P, SB, D])
        stage = sb("weight_stage", [P, 2, PW])
        ident = sb("ident", [P, P])
        tri = sb("tri", [P, P])
        tri_s = sb("tri_strict", [P, P], BF16)
        ones = sb("ones", [P, P], BF16)
        low = sb("low", [G, P])
        outw = sb("out_w_rows", [P, D])
        gbias = sb("gate_bias_rows", [P, 2, NH])
        wraw = E[0:2 * NH, 0, :, :].rearrange("p a c -> p (a c)")[:, 0:3 * D]
        wgr = E[:, 2, 0, 0:6 * KC * NH].rearrange("p (c o) -> p c o", c=3 * KC)
        graw = E[:, 3, 0, 0:2 * NH].rearrange("p (a h) -> p a h", a=2)
        b1raw = E[0:NE * FC, 1, 0, :]
        wg = sb("gate_w_sum", [P, 2 * KC, 2 * NH])
        gw = sb("router_w", [P, KC, NE])
        b1T = sb("b1_turned", [P, NE, FC])
        revidx = sb("rev_index", [P, SB, NE])
        ebase = sb("expert_base", [P, NE])
        tok = sb("token_ids", [P, SB])
        h_flat = Hs[:, :, :, :].rearrange("p j h e -> p (j h e)")
        dl, key, oh1, oh2, dl2, rsum, tmp1, tmp2 = (
            h_flat[:, n * SB * NE:(n + 1) * SB * NE].rearrange("p (j e) -> p j e", j=SB) for n in range(8))
        it_rev = dl.bitcast(I32)
        it_base = h_flat[:, 64:64 + NE].bitcast(I32)
        it_tok = h_flat[:, 96:96 + SB].bitcast(I32)
        v_flat = vaug[0:1, :, :, :, :].rearrange("p a j h e -> p (a j h e)")
        exf, pastf, rowf, jf, it_j, rowi, exi = (v_flat[:, n * NL:(n + 1) * NL] for n in range(7))
        it_j, rowi, exi = (a.bitcast(I32) for a in (it_j, rowi, exi))
        st = sb("bn_parts", [P, SB, 6])
        mv = sb("mean_var", [P, SB, 2])
        ve = sb("var_eps", [P, SB])
        lnv = sb("ln_var", [P, SB])
        rs = sb("rstd", [P, SB])
        nt1 = sb("newton", [P, SB])
        vsum = sb("v_sum", [P, SB, NH])
        gs = sb("gates", [P, SB, 2, NH])
        nabs = sb("minus_abs_f", [P, SB, NH])
        ex1 = sb("exp_f", [P, SB, NH])
        lsg = sb("log_sigmoid", [P, SB, NH])
        csb = sb("log_f_sum", [P, G])
        acol = sb("i_minus_sum", [P, 2, G])
        arun = sb("running_max", [G, P])
        mld = sb("max_log_d", [P, G])
        en = sb("exp_minus_max", [P, 2, SB, NH])
        ssq = sb("square_sum", [P, G])
        nrm = sb("normalizer", [P, SB, NH])
        rn = sb("one_over_norm", [P, G])
        hv = sb("h_var", [P, G])
        hln = ssq
        ht = nabs[:, :, :].rearrange("p j h -> p (j h)")
        hy = sb("h_rstd", [P, G])
        m1 = sb("top1", [P, SB])
        kmax = sb("key_max", [P, SB])
        m2 = sb("top2", [P, SB])
        mask = sb("chosen", [P, SB, NE], BF16)
        p2 = sb("exp_top2", [P, SB])
        den = sb("gate_sum", [P, SB])
        slotf = sb("slot_f", [P, SB, 2])
        sloti = sb("slot_i", [P, SB, 2], I32)
        rec = sb("record", [P, SB, 2, 2], I32)
        fill = sb("expert_fill", [P, NE])
        ids_g = sb("ids_for_gather", [P, 4, 2], I32)
        ids_s = sb("ids_for_scatter", [P, 4, 2], I32)
        cntf = sb("count", [1, NE])
        cnti = sb("count_i", [1, NE], I32)
        ntf = sb("tiles_of", [1, NE])
        zer = sb("zeros", [1, NE])
        endf = sb("tiles_up_to", [1, NE])
        cmpf = Hs[0:1, :, :, :].rearrange("p j h e -> p (j h e)")[:, 0:NL * NE].rearrange(
            "p (t e) -> p t e", e=NE)

        psum = [ctx.enter_context(nc.psum_tensor(f"bank{i}", [P, 512], F32)) for i in range(1)]
        ps_s = ctx.enter_context(nc.psum_tensor("scores", [P, HG, 512], F32))
        ps_h = ctx.enter_context(nc.psum_tensor("pv", [P, 512], F32))
        ps_m = ctx.enter_context(nc.psum_tensor("gate_bank", [P, 512], F32))
        ps_x = ctx.enter_context(nc.psum_tensor("route_bank", [P, 512], F32))
        ps_t = psum[0]
        ps_gate = ps_m[:, 0:G * 2].rearrange("p (j a h) -> p j a h", j=SB, a=2)
        ps_cs = ps_m[:, 64:64 + G]
        ps_aT = ps_m[0:G, 128:128 + P]
        ps_ab = ps_m[:, 256:256 + G]
        ps_log = ps_x[:, 0:SB * NE].rearrange("p (j e) -> p j e", j=SB)
        ps_rank = ps_x[:, 64:64 + SB * NE]
        ps_tot = ps_x[:, 128:128 + NE]

        s_held = sem("held")
        s_const = sem("const_in")
        s_c0 = sem("zeroed")
        s_cp = sem("pool_consts")
        s_tab0 = sem("table_fill")
        s_tab = sem("table_written")
        s_wt = sem("gate_w_transposed")
        s_cd = sem("dve_consts")
        s_x = [sem(f"x_in{p}") for p in range(2)]
        s_ctx = sem("ctx_in")
        s_w = [sem(f"weights_in{p}") for p in range(2)]
        s_hi = sem("weights_high")
        s_lo = sem("weights_low")
        c_dn = Chain(sem("dve_next"), DVE_NEXT)
        c_dh = Chain(sem("dve_here"), DVE_HERE)
        c_an = Chain(sem("act_next"), ACT_NEXT)
        c_ah = Chain(sem("act_here"), ACT_HERE)
        s_ve = sem("var_ready")
        s_rs = sem("rstd_guess")
        s_qn = sem("q_normed")
        s_vc = sem("v_ready")
        s_tq = sem("qk_turned")
        s_te = sem("qk_in_sbuf")
        s_gt = sem("gates_summed")
        s_na = sem("f_abs_ready")
        s_ln = sem("ln_ready")
        s_ls = sem("log_sigmoid_ready")
        s_cs = sem("log_f_summed")
        s_a = sem("a_ready")
        s_aT = sem("a_turned")
        s_run = sem("running_max_ready")
        s_ab = sem("running_max_turned")
        s_mld = sem("max_log_d_ready")
        s_en = sem("exp_minus_max_ready")
        s_scan = sem("scan_written")
        s_e = [sem(f"running_max_in{j}") for j in range(SB)]
        s_em = sem("masked")
        s_ee = sem("decay_ready")
        s_s = sem("scores_ready")
        s_cm = sem("c_ready")
        s_pv = sem("pv_ready")
        s_hev = sem("h_in_sbuf")
        s_hve = sem("h_var_ready")
        s_hy = sem("h_rstd_guess")
        s_ve2 = sem("var2_ready")
        s_rs2 = sem("rstd2_guess")
        s_x1 = sem("x1_ready")
        s_xf = sem("xf_ready")
        s_xo = sem("x1_written")
        s_xfo = sem("xf_written")
        s_xt = sem("xf_turned")
        s_xe = sem("xf_turned_in_sbuf")
        s_lg = sem("logits_ready")
        s_m2 = sem("top2_ready")
        s_p2 = sem("exp_top2_ready")
        s_mk = sem("chosen_ready")
        s_rk = sem("rank_ready")
        s_rec = sem("records_ready")
        s_sc = sem("table_scattered")
        s_rf = sem("records_free")

        def number(step):
            return step[0] * 2 + step[1]

        def after(step):
            return (step[0] + step[1], 1 - step[1])

        def run_steps(eng, prologue, body):
            prologue((0, 0))
            with eng.Fori(0, NSTEP // 2 - 1) as i:
                body((i, 0), True)
                body((i, 1), True)
            body((NSTEP // 2 - 1, 0), True)
            body((NSTEP // 2 - 1, 1), False)

        with nc.Block() as block:

            @block.sync
            def _(sp):
                for o, gate in ((0, igate_w), (NH, fgate_w)):
                    for r in range(HG):
                        sp.dma_start(wraw[o + KC * r:o + KC * r + KC, :], gate[r::HG, :]).then_inc(s_const, 16)
                sp.dma_start(b1raw, b1.rearrange("e (c p) -> (e c) p", p=P)).then_inc(s_const, 16)
                sp.dma_start(xbuf[:, 0, :, :], xs_dram[0]).then_inc(s_x[0], 16)
                sp.dma_start(ctxb[:, :, :], ctx_dram[0]).then_inc(s_ctx, 16)
                sp.dma_start(xbuf[:, 1, :, :], xs_dram[1]).then_inc(s_x[1], 16)
                sp.dma_start(gw[:, :, :], gate_w.rearrange("(k p) e -> p k e", p=P)).then_inc(s_const, 16)
                sp.dma_start(outw[:, :], out_w.partition_broadcast(P)).then_inc(s_const, 16)
                for a, gate in ((0, igate_b), (1, fgate_b)):
                    sp.dma_start(graw[:, a, :], gate.partition_broadcast(P)).then_inc(s_const, 16)
                sp.wait_ge(s_tab0, 2)
                sp.dma_start(table.rearrange("(p n) w -> p n w", p=P),
                             stage[:, 0, 0:2 * TB].bitcast(I32).rearrange("p (n w) -> p n w", w=2)).then_inc(s_tab, 16)
                sp.wait_ge(s_tab, 16)

                def weights(n_half, half):
                    src = (w1_dram, w2_dram)[half]
                    dst = stage[:, half, :]
                    if half:
                        dst = dst.rearrange("p (c d) -> p c d", d=D)
                    sp.dma_start(dst, src[n_half]).then_inc(s_w[half], 16)

                def scans(step, free):
                    g = number(step)
                    sp.wait_ge(s_run, g + 1)
                    sp.dma_start(scan_dram[g], arun[:, :]).then_inc(s_scan, 16)
                    sp.wait_ge(s_scan, (g + 1) * 16)
                    for j in range(SB):
                        if free:
                            sp.wait_ge(s_pv, g * SB + (j + 1 - SB))
                        sp.dma_start(E[:, j, :, :],
                                     scan_dram[g, j * NH:j * NH + NH, :].partition_broadcast(P)).then_inc(s_e[j], 16)

                def prologue(step):
                    weights(0, 0)
                    weights(0, 1)
                    scans(step, False)

                def body(step, more):
                    g = number(step)
                    for half in range(2):
                        sp.wait_ge(s_lo, g * SB + half + 1)
                        weights(g * 2 + 1, half)
                    if more:
                        scans(after(step), True)
                        for half in range(2):
                            sp.wait_ge(s_lo, g * SB + half + 3)
                            weights(g * 2 + 2, half)
                    sp.wait_ge(s_x1, g + 1)
                    sp.dma_start(out_dram[g], xbuf[:, step[1], :, :]).then_inc(s_xo, 16)
                    sp.wait_ge(s_xf, (g + 1) * SB)
                    sp.dma_start(xf_step[g], normed[:, :, :]).then_inc(s_xfo, 16)
                    sp.wait_ge(s_xo, (g + 1) * 16)

                def body_and_loads(step, more, last_load):
                    body(step, more)
                    if last_load:
                        g = number(step)
                        sp.dma_start(xbuf[:, step[1], :, :], xs_dram[g + 2]).then_inc(s_x[step[1]], 16)
                        sp.wait_ge(s_tq, g * SB + 2 * SB)
                        sp.wait_ge(s_vc, g + 2)
                        sp.dma_start(ctxb[:, :, :], ctx_dram[g + 2]).then_inc(s_ctx, 16)

                prologue((0, 0))
                sp.wait_ge(s_tq, SB)
                sp.wait_ge(s_vc, 1)
                sp.dma_start(ctxb[:, :, :], ctx_dram[1]).then_inc(s_ctx, 16)
                with sp.Fori(0, NSTEP // 2 - 1) as i:
                    body_and_loads((i, 0), True, True)
                    body_and_loads((i, 1), True, True)
                body_and_loads((NSTEP // 2 - 1, 0), True, False)
                body_and_loads((NSTEP // 2 - 1, 1), False, False)
                sp.wait_ge(s_xo, 16 * NSTEP)
                sp.wait_ge(s_xfo, 16 * (NSTEP + 1))

            @block.gpsimd
            def _(pool):
                pool.sem_inc(s_rf, 1)
                pool.sem_inc(s_xfo, 16)
                tab0 = stage[:, 0, 0:2 * TB].rearrange("p (n w) -> p n w", w=2)
                pool.iota(tab0[:, :, 0:1].bitcast(I32), [[0, TB]], base=T, channel_multiplier=0).then_inc(s_tab0, 1)
                pool.memset(tab0[:, :, 1:2], 0.0).then_inc(s_tab0, 1)
                pool.memset(ident[:, :], 0.0).then_inc(s_c0, 1)
                pool.memset(tri[:, :], 1.0).then_inc(s_c0, 1)
                pool.memset(tri_s[:, :], 1.0).then_inc(s_c0, 1)
                pool.wait_ge(s_c0, 3)
                pool.affine_select(out=ident[:, :], in_=ident[:, :], compare_op=ALU.not_equal, fill=1.0,
                                   base=0, pattern=[[-1, P]], channel_multiplier=1).then_inc(s_cp, 1)
                pool.affine_select(out=tri[:, :], in_=tri[:, :], compare_op=ALU.is_ge, fill=0.0,
                                   base=0, pattern=[[1, P]], channel_multiplier=-1).then_inc(s_cp, 1)
                pool.affine_select(out=tri_s[:, :], in_=tri_s[:, :], compare_op=ALU.is_ge, fill=0.0,
                                   base=-1, pattern=[[1, P]], channel_multiplier=-1).then_inc(s_cp, 1)
                pool.memset(ones[:, :], 1.0).then_inc(s_cp, 1)
                pool.memset(low[:, :], -3e38).then_inc(s_cp, 1)
                for p in range(2):
                    pool.memset(vaug[:, p, :, :, DH:DH + 1], 1.0).then_inc(s_cp, 1)
                pool.iota(it_rev[:, :, :], [[0, SB], [-1, NE]], base=NE, channel_multiplier=0).then_inc(s_cp, 1)
                pool.iota(it_base[:, :], [[T, NE]], base=0, channel_multiplier=0).then_inc(s_cp, 1)
                pool.iota(it_tok[:, :], [[S, SB]], base=0, channel_multiplier=1).then_inc(s_cp, 1)
                pool.wait_ge(s_tab, 16)

                big = pool.to_reg(BIG)

                def masks(step):
                    g = number(step)
                    for j in range(SB):
                        pool.wait_ge(s_e[j], (g + 1) * 16)
                        pool.sem_inc(s_held, 1)
                        pool.affine_select(out=E[:, j, :, :], in_=E[:, j, :, :], compare_op=ALU.is_ge, fill=big,
                                           base=0, pattern=[[0, NH], [1, P]], channel_multiplier=-1).then_inc(s_em, 1)

                def prologue(step):
                    masks(step)

                def body(step, more):
                    g = number(step)
                    if more:
                        masks(after(step))
                    pool.wait_ge(s_rec, g + 1)
                    pool.sem_inc(s_held, 1)
                    for j in range(SB):
                        for k in range(2):
                            pool.indirect_dma_start(
                                table, bass.IndirectOffsetOnAxis(ap=sloti[:, j, k:k + 1], axis=0),
                                rec[:, j, k, :], None, bounds_check=TABLE - 1,
                                oob_is_err=False).then_inc(s_sc, 16)
                    pool.wait_ge(s_sc, (g + 1) * (2 * SB * 16))
                    pool.sem_inc(s_rf, 1)

                run_steps(pool, prologue, body)

            @block.scalar
            def _(act):
                act.preload_act_table_set("natural_log_exp_and_others")

                def rsqrt_guess(var, ln, y, chain, ready, done, count):
                    act.wait_ge(ready, count)
                    chain.link(act, act.activation(ln, var, ACT.Ln))
                    act.activation(y, ln, ACT.Exp, scale=-0.5).then_inc(done, 1)

                def next_guess(step):
                    c_an.begin(number(step))
                    rsqrt_guess(ve[:, :], lnv[:, :], rs[:, :], c_an, s_ve, s_rs, number(step) + 1)

                def turned(step, j):
                    g = number(step)
                    act.wait_ge(s_tq, g * SB + j + 1)
                    act.activation(qkT[:, step[1], j, :, :].rearrange("p c t -> p (c t)"), ps_t[:, :],
                                   ACT.Copy).then_inc(s_te, 1)

                def log_sigmoid(step):
                    g = number(step)
                    act.wait_ge(s_na, g + 1)
                    c_an.link(act, act.activation(ex1[:, :, :], nabs[:, :, :], ACT.Exp))
                    act.activation(lsg[:, :, :], ex1[:, :, :], ACT.Ln, bias=1.0).then_inc(s_ln, 1)
                    c_an.end()

                def exp_minus_max(step):
                    g = number(step)
                    act.wait_ge(s_mld, g + 1)
                    for j in range(SB):
                        ins = act.activation(
                            en[:, step[1], j, :].rearrange("p (u k) -> p k u", u=KC),
                            mld[:, j * NH:(j + 1) * NH].rearrange("p (k u) -> p k u", u=KC), ACT.Exp, scale=-1.0)
                    ins.then_inc(s_en, 1)

                def decay(step, j):
                    g = number(step)
                    act.wait_ge(s_em, g * SB + j + 1)
                    act.wait_ge(s_a, g + 1)
                    for c in range(NH):
                        ins = act.activation(E[:, j, c, :], E[:, j, c, :], ACT.Exp, scale=-1.0,
                                             bias=acol[:, step[1], j * NH + c:j * NH + c + 1])
                    ins.then_inc(s_ee, 1)

                def weights_high(step, n):
                    g, half, q = number(step), n % 2, n // 2
                    act.wait_ge(s_w[half], (g * 2 + (q + 1)) * 16)
                    if half == 0:
                        dst = w1s[:, bass.ds(g, 1), 0, q, :].rearrange("p a f -> p (a f)")
                    else:
                        dst = w2s[:, bass.ds(g, 1), 0, q * (FC // 2):(q + 1) * (FC // 2), :].rearrange(
                            "p a c d -> p (a c d)")
                    act.activation(dst, stage[:, half, :], ACT.Copy, scale=W_SCALE).then_inc(s_hi, 1)

                def h_out(step, j):
                    g = number(step)
                    act.wait_ge(s_pv, g * SB + j + 1)
                    h = ps_h[:, 0:NH * (DH + 1)].rearrange("p (h e) -> p h e", h=NH)
                    act.activation(Hs[:, j, :, :], h, ACT.Copy)
                    act.activation(work[:, j, :].rearrange("p (h e) -> p h e", h=NH), h[:, :, 0:DH],
                                   ACT.Square).then_inc(s_hev, 1)

                def prologue(step):
                    next_guess(step)
                    for j in range(SB):
                        turned(step, j)
                    log_sigmoid(step)
                    exp_minus_max(step)
                    for j in range(SB):
                        decay(step, j)

                def body(step, more):
                    g = number(step)
                    c_ah.begin(g)
                    if more:
                        nxt = after(step)
                        next_guess(nxt)
                    weights_high(step, 0)
                    h_out(step, 0)
                    if more:
                        turned(nxt, 0)
                        turned(nxt, 1)
                    weights_high(step, 1)
                    h_out(step, 1)
                    if more:
                        turned(nxt, 2)
                        turned(nxt, 3)
                    weights_high(step, 2)
                    h_out(step, 2)
                    if more:
                        log_sigmoid(nxt)
                    h_out(step, 3)
                    weights_high(step, 3)
                    if more:
                        exp_minus_max(nxt)
                        decay(nxt, 0)
                        decay(nxt, 1)
                    rsqrt_guess(hv[:, :], hln[:, :], hy[:, :], c_ah, s_hve, s_hy, g + 1)
                    if more:
                        decay(nxt, 2)
                    rsqrt_guess(ve[:, :], lnv[:, :], rs[:, :], c_ah, s_ve2, s_rs2, g + 1)
                    if more:
                        decay(nxt, 3)
                    act.wait_ge(s_m2, g + 1)
                    act.activation(p2[:, :], m2[:, :], ACT.Exp).then_inc(s_p2, 1)
                    c_ah.end()

                run_steps(act, prologue, body)

            @block.tensor
            def _(pe):
                pe.wait_ge(s_cp, 10)
                pe.wait_ge(s_const, 16 * (2 * HG + 5))
                for c in range(3 * KC):
                    ins = pe.transpose(ps_x[:, 16 * c:16 * c + 16], wraw[:, c * P:(c + 1) * P],
                                       ident[0:2 * NH, 0:2 * NH])
                ins = pe.transpose(ps_x[:, 256:256 + NE * FC], b1raw, ident[0:NE * FC, 0:NE * FC])
                ins.then_inc(s_wt, 1)

                def turn(step, j):
                    g = number(step)
                    pe.wait_ge(s_qn, g * SB + j + 1)
                    pe.wait_ge(s_te, g * SB + j + 1)
                    for c in range(KC):
                        pe.transpose(ps_t[:, c * P:(c + 1) * P], normed[:, j, c * P:(c + 1) * P], ident[:, :])
                    for c in range(KC):
                        ins = pe.transpose(ps_t[:, (KC + c) * P:(KC + c + 1) * P],
                                           ctxb[:, j, c * P:(c + 1) * P], ident[:, :])
                    ins.then_inc(s_tq, 1)

                def gates(step, first):
                    g = number(step)
                    if not first:
                        pe.wait_ge(s_mld, g)
                    pe.wait_ge(s_cd, 1)
                    pe.wait_ge(s_te, g * SB + SB + 1)
                    for j in range(SB):
                        for c in range(2 * KC):
                            ins = pe.matmul(ps_m[:, j * 2 * NH:(j + 1) * 2 * NH], qkT[:, step[1], j, c, :], wg[:, c, :],
                                            start=(c == 0), stop=(c == 2 * KC - 1))
                    ins.then_inc(s_gt, 1)

                def log_f_sum(step):
                    g = number(step)
                    pe.wait_ge(s_ls, g + 1)
                    pe.matmul(ps_cs, tri[:, :], lsg[:, :, :].rearrange("p j h -> p (j h)"),
                              start=True, stop=True).then_inc(s_cs, 1)
                    pe.wait_ge(s_a, g + 1)
                    pe.transpose(ps_aT, acol[:, step[1], :], ident[:, :]).then_inc(s_aT, 1)
                    pe.wait_ge(s_run, g + 1)
                    pe.sem_inc(s_held, 1)
                    pe.transpose(ps_ab, arun[:, :], ident[0:G, 0:G]).then_inc(s_ab, 1)

                def scores(step, j):
                    g = number(step)
                    pe.wait_ge(s_cm, g * SB + j + 1)
                    for u in range(KC):
                        for k in range(HG):
                            r = slice(DH * k, DH * k + DH)
                            ins = pe.matmul(ps_s[:, k, u * P:(u + 1) * P], qkT[r, step[1], j, KC + u, :],
                                            qkT[r, step[1], j, u, :], start=True, stop=True)
                    ins.then_inc(s_s, 1)

                def times_v(step, j):
                    g = number(step)
                    pe.wait_ge(s_cm, g * SB + j + 2)
                    pe.wait_ge(s_hev, g * SB + j + 1)
                    for u in range(KC):
                        for k in range(HG):
                            h = u * HG + k
                            ins = pe.matmul(ps_h[:, h * (DH + 1):(h + 1) * (DH + 1)], E[:, j, k * KC + u, :],
                                            vaug[:, step[1], j, h, :], start=True, stop=True)
                    ins.then_inc(s_pv, 1)

                def route(step):
                    g = number(step)
                    pe.wait_ge(s_xf, (g + 1) * SB)
                    for r in range(SB // 2):
                        pe.wait_ge(s_xe, g * (SB // 2) + r + 1)
                        for j in range(2):
                            for c in range(KC):
                                ins = pe.transpose(ps_x[:, (j * KC + c) * P:(j * KC + c + 1) * P],
                                                   normed[:, 2 * r + j, c * P:(c + 1) * P], ident[:, :])
                        ins.then_inc(s_xt, 1)
                    pe.wait_ge(s_xe, g * (SB // 2) + SB // 2 + 1)
                    xT = work[:, :, :].rearrange("p j (c t) -> p j c t", c=KC)
                    for j in range(SB):
                        for c in range(KC):
                            ins = pe.matmul(ps_log[:, j, :], xT[:, j, c, :], gw[:, c, :],
                                            start=(c == 0), stop=(c == KC - 1))
                    ins.then_inc(s_lg, 1)
                    pe.wait_ge(s_mk, g + 1)
                    chosen = mask[:, :, :].rearrange("p j e -> p (j e)")
                    pe.matmul(ps_rank, tri_s[:, :], chosen, start=True, stop=False)
                    for d in range(1, SB):
                        pe.matmul(ps_rank[:, d * NE:], ones[:, :], chosen[:, 0:(SB - d) * NE], start=False,
                                  stop=(d == SB - 1))
                    for j in range(SB):
                        ins = pe.matmul(ps_tot, ones[:, :], mask[:, j, :], start=(j == 0), stop=(j == SB - 1))
                    ins.then_inc(s_rk, 1)

                def prologue(step):
                    for j in range(SB):
                        turn(step, j)
                    gates(step, True)
                    log_f_sum(step)

                def body(step, more):
                    nxt = after(step)
                    scores(step, 0)
                    scores(step, 1)
                    times_v(step, 0)
                    if more:
                        turn(nxt, 0)
                        turn(nxt, 1)
                    scores(step, 2)
                    times_v(step, 1)
                    if more:
                        turn(nxt, 2)
                        turn(nxt, 3)
                    scores(step, 3)
                    times_v(step, 2)
                    if more:
                        gates(nxt, False)
                    times_v(step, 3)
                    if more:
                        log_f_sum(nxt)
                    route(step)

                run_steps(pe, prologue, body)

            @block.vector
            def _(dve):
                for s, n in ((s_te, 1), (s_cm, 1), (s_hev, 1), (s_xe, 1)):
                    dve.sem_inc(s, n)
                dve.wait_ge(s_cp, 10)
                dve.wait_ge(s_wt, 1)
                c_cd = Chain(sem("dve_setup"), 0)
                c_cd.inc(dve.tensor_copy(wgr[:, :, :], ps_x[:, 0:16 * 3 * KC].rearrange("p (c o) -> p c o", c=3 * KC)))
                for a in range(2):
                    c_cd.inc(dve.tensor_copy(gbias[:, a, :].rearrange("p (k u) -> p k u", u=KC),
                                             graw[:, a, :].rearrange("p (u k) -> p k u", u=KC)))
                c_cd.inc(dve.tensor_copy(b1T[:, :, :], ps_x[:, 256:256 + NE * FC].rearrange("p (e c) -> p e c", e=NE)))
                c_cd.inc(dve.tensor_copy(revidx[:, :, :], it_rev[:, :, :]))
                c_cd.inc(dve.tensor_copy(ebase[:, :], it_base[:, :]))
                c_cd.inc(dve.tensor_copy(fill[:, :], it_base[:, :]))
                c_cd.inc(dve.tensor_copy(tok[:, :], it_tok[:, :]))
                c_cd.wait(dve)
                c_cd.inc(dve.tensor_copy(wg[:, 0:KC, :], wgr[:, 0:KC, :]))
                c_cd.link(dve, dve.tensor_tensor(wg[:, KC:2 * KC, :], wgr[:, KC:2 * KC, :], wgr[:, 2 * KC:3 * KC, :], ALU.add))
                dve.sem_inc(s_cd, 1)

                def refine(c, var, y, t):
                    c.link(dve, dve.tensor_tensor(t, y, y, ALU.mult))
                    c.link(dve, dve.scalar_tensor_tensor(out=t, in0=t, scalar=-0.5, in1=var, op0=ALU.mult, op1=ALU.mult))
                    c.link(dve, dve.scalar_tensor_tensor(out=y, in0=t, scalar=1.5, in1=y, op0=ALU.add, op1=ALU.mult))

                def stats(c, src, parts, mean_var, var_eps, ready):
                    for j in range(SB):
                        c.inc(dve.bn_stats(parts[:, j, :], src[:, j, :]))
                    c.wait(dve)
                    dve.sem_inc(s_held, 1)
                    for j in range(SB):
                        c.inc(dve.bn_aggr(mean_var[:, j, :], parts[:, j, :]))
                    c.wait(dve)
                    dve.tensor_scalar(var_eps[:, :], mean_var[:, :, 1], LN_EPS, None, ALU.add).then_inc(ready, 1)

                def next_stats(step):
                    c_dn.begin(number(step))
                    dve.wait_ge(s_x[step[1]], (step[0] + 1) * 16)
                    stats(c_dn, xbuf[:, step[1], :, :], st, mv, ve, s_ve)

                def next_norm(step, first):
                    g = number(step)
                    dve.wait_ge(s_rs, g + 1)
                    refine(c_dn, ve[:, :], rs[:, :], nt1[:, :])
                    if not first:
                        dve.wait_ge(s_xfo, g * 16)
                    dve.wait_ge(s_ctx, (g + 1) * 16)
                    for j in range(SB):
                        dve.tensor_scalar(normed[:, j, :], xbuf[:, step[1], j, :], mv[:, j, 0:1], rs[:, j:j + 1],
                                          ALU.subtract, ALU.mult).then_inc(s_qn, 1)

                def centre_v(step):
                    ctx_h = ctxb[:, :, :].rearrange("p j (h e) -> p (j h) e", h=NH)
                    vs = vsum[:, :, :].rearrange("p j h -> p (j h)")
                    c_dn.link(dve, dve.tensor_reduce(vs, ctx_h, AX, ALU.add))
                    v = vaug[:, step[1], :, :, :].rearrange("p j h e -> p (j h) e")[:, :, 0:DH]
                    dve.scalar_tensor_tensor(out=v, in0=vs.unsqueeze(2).broadcast_to([P, G, DH]), scalar=-1.0 / DH,
                                             in1=ctx_h, op0=ALU.mult, op1=ALU.add).then_inc(s_vc, 1)

                def next_gates(step, first):
                    g = number(step)
                    f = gs[:, :, 1, :]
                    dve.wait_ge(s_gt, g + 1)
                    bias = gbias[:, :, :].rearrange("p a h -> p (a h)").unsqueeze(1).broadcast_to([P, SB, 2 * NH])
                    c_dn.link(dve, dve.tensor_tensor(gs[:, :, :, :].rearrange("p j a h -> p j (a h)"),
                                                     ps_gate.rearrange("p j a h -> p j (a h)"), bias, ALU.add))
                    dve.scalar_tensor_tensor(out=nabs[:, :, :], in0=f, scalar=-1.0, in1=f, op0=ALU.mult,
                                             op1=ALU.min).then_inc(s_na, 1)
                    dve.wait_ge(s_ln, g + 1)
                    dve.scalar_tensor_tensor(out=lsg[:, :, :], in0=f, scalar=0.0, in1=lsg[:, :, :], op0=ALU.min,
                                             op1=ALU.subtract).then_inc(s_ls, 1)
                    dve.wait_ge(s_cs, g + 1)
                    c_dn.inc(dve.tensor_copy(csb[:, :], ps_cs))
                    dve.tensor_tensor(acol[:, step[1], :].rearrange("p (j h) -> p j h", j=SB), gs[:, :, 0, :],
                                      ps_cs.rearrange("p (j h) -> p j h", j=SB), ALU.subtract).then_inc(s_a, 1)
                    dve.wait_ge(s_aT, g + 1)
                    if not first:
                        dve.wait_ge(s_scan, g * 16)
                        dve.wait_ge(s_en, g)
                    dve.tensor_tensor_scan(arun[:, :], ps_aT, low[:, :], -3e38, ALU.max, ALU.max).then_inc(s_run, 1)
                    dve.wait_ge(s_ab, g + 1)
                    c_dn.wait(dve)
                    dve.tensor_tensor(mld[:, :], csb[:, :], ps_ab, ALU.add).then_inc(s_mld, 1)

                def weights_low(step, n):
                    g, half, q = number(step), n % 2, n // 2
                    dve.wait_ge(s_hi, g * 4 + n + 1)
                    e, k = g, q
                    if half == 0:
                        hi, lo = (w1s[:, bass.ds(e, 1), a, k, :].rearrange("p a f -> p (a f)") for a in range(2))
                    else:
                        hi, lo = (w2s[:, bass.ds(e, 1), a, k * (FC // 2):(k + 1) * (FC // 2), :].rearrange("p a c d -> p (a c d)")
                                  for a in range(2))
                    dve.scalar_tensor_tensor(out=lo, in0=stage[:, half, :], scalar=W_SCALE, in1=hi, op0=ALU.mult,
                                             op1=ALU.subtract).then_inc(s_lo, 1)

                def c_of(step, j):
                    g = number(step)
                    dve.wait_ge(s_s, g * SB + j + 1)
                    dve.wait_ge(s_ee, g * SB + j + 1)
                    c = E[:, j, :, :].rearrange("p (k u) s -> p k (u s)", u=KC)
                    dve.scalar_tensor_tensor(out=c, in0=ps_s[:, :, 0:KC * P], scalar=QK_SCALE, in1=c,
                                             op0=ALU.mult, op1=ALU.mult).then_inc(s_cm, 1)

                def h_norm(step):
                    g, c = number(step), c_dh
                    dve.wait_ge(s_hev, g * SB + SB + 1)
                    dve.wait_ge(s_en, g + 1)
                    sq = work[:, :, :].rearrange("p j (h e) -> p (j h) e", h=NH)
                    c.inc(dve.tensor_reduce(ssq[:, :], sq, AX, ALU.add))
                    rows = Hs[:, :, :, DH]
                    c.link(dve, dve.scalar_tensor_tensor(out=nrm[:, :, :], in0=rows, scalar=-1.0, in1=rows,
                                                         op0=ALU.mult, op1=ALU.max))
                    c.link(dve, dve.tensor_tensor(nrm[:, :, :], nrm[:, :, :], en[:, step[1], :, :], ALU.max))
                    n = nrm[:, :, :].rearrange("p j h -> p (j h)")
                    c.link(dve, dve.tensor_scalar(n, n, EPS, None, ALU.add))
                    c.link(dve, dve.reciprocal(rn[:, :], n))
                    c.link(dve, dve.tensor_tensor(hv[:, :], ssq[:, :], rn[:, :], ALU.mult))
                    c.link(dve, dve.scalar_tensor_tensor(out=hv[:, :], in0=hv[:, :], scalar=1.0 / DH, in1=rn[:, :],
                                                         op0=ALU.mult, op1=ALU.mult))
                    dve.tensor_scalar(hv[:, :], hv[:, :], LN_EPS, None, ALU.add).then_inc(s_hve, 1)
                    dve.wait_ge(s_hy, g + 1)
                    refine(c, hv[:, :], hy[:, :], ht[:, :])
                    c.link(dve, dve.tensor_tensor(hy[:, :], hy[:, :], rn[:, :], ALU.mult))
                    h = Hs[:, :, :, :].rearrange("p j h e -> p (j h) e")[:, :, 0:DH]
                    c.link(dve, dve.tensor_tensor(sq, h, hy[:, :].unsqueeze(2).broadcast_to([P, G, DH]), ALU.mult))
                    c.link(dve, dve.tensor_tensor(work[:, :, :], work[:, :, :],
                                                  outw[:, :].unsqueeze(1).broadcast_to([P, SB, D]), ALU.mult))
                    xs = xbuf[:, step[1], :, :]
                    dve.tensor_tensor(xs, xs, work[:, :, :], ALU.add).then_inc(s_x1, 1)
                    dve.wait_ge(s_x1, g + 1)

                def x1_norm(step):
                    g, c = number(step), c_dh
                    stats(c, xbuf[:, step[1], :, :], st, mv, ve, s_ve2)
                    dve.wait_ge(s_rs2, g + 1)
                    refine(c, ve[:, :], rs[:, :], nt1[:, :])
                    for j in range(SB):
                        dve.tensor_scalar(normed[:, j, :], xbuf[:, step[1], j, :], mv[:, j, 0:1],
                                          rs[:, j:j + 1], ALU.subtract, ALU.mult).then_inc(s_xf, 1)

                def wide(ap):
                    return ap.unsqueeze(2).broadcast_to([P, SB, NE])

                def route(step):
                    g, c = number(step), c_dh
                    for r in range(SB // 2):
                        dve.wait_ge(s_xt, g * (SB // 2) + r + 1)
                        dve.tensor_copy(work[:, 2 * r:2 * r + 2, :].rearrange("p j d -> p (j d)"),
                                        ps_x[:, :]).then_inc(s_xe, 1)
                    dve.wait_ge(s_lg, g + 1)
                    c.link(dve, dve.tensor_reduce(m1[:, :], ps_log, AX, ALU.max))
                    c.link(dve, dve.tensor_tensor(dl[:, :, :], ps_log, wide(m1[:, :]), ALU.subtract))
                    c.link(dve, dve.scalar_tensor_tensor(out=key[:, :, :], in0=dl[:, :, :], scalar=0.0,
                                                         in1=revidx[:, :, :], op0=ALU.is_equal, op1=ALU.mult))
                    c.link(dve, dve.tensor_reduce(kmax[:, :], key[:, :, :], AX, ALU.max))
                    c.link(dve, dve.tensor_tensor(oh1[:, :, :], key[:, :, :], wide(kmax[:, :]), ALU.is_equal))
                    c.link(dve, dve.scalar_tensor_tensor(out=dl2[:, :, :], in0=oh1[:, :, :], scalar=-BIG,
                                                         in1=dl[:, :, :], op0=ALU.mult, op1=ALU.add))
                    dve.tensor_reduce(m2[:, :], dl2[:, :, :], AX, ALU.max).then_inc(s_m2, 1)
                    dve.wait_ge(s_m2, g + 1)
                    c.link(dve, dve.tensor_tensor(key[:, :, :], dl2[:, :, :], wide(m2[:, :]), ALU.is_equal))
                    c.link(dve, dve.tensor_tensor(key[:, :, :], key[:, :, :], revidx[:, :, :], ALU.mult))
                    c.link(dve, dve.tensor_reduce(kmax[:, :], key[:, :, :], AX, ALU.max))
                    c.link(dve, dve.tensor_tensor(oh2[:, :, :], key[:, :, :], wide(kmax[:, :]), ALU.is_equal))
                    dve.tensor_tensor(mask[:, :, :], oh1[:, :, :], oh2[:, :, :], ALU.add).then_inc(s_mk, 1)
                    dve.wait_ge(s_rf, g + 1)
                    recf = rec[:, :, :, :].bitcast(F32)
                    dve.wait_ge(s_p2, g + 1)
                    c.link(dve, dve.tensor_scalar(den[:, :], p2[:, :], 1.0, None, ALU.add))
                    c.link(dve, dve.reciprocal(den[:, :], den[:, :]))
                    c.inc(dve.tensor_copy(recf[:, :, 0, 1], den[:, :]))
                    c.inc(dve.tensor_tensor(recf[:, :, 1, 1], den[:, :], p2[:, :], ALU.mult))
                    for k in range(2):
                        c.inc(dve.tensor_copy(rec[:, :, k, 0], tok[:, :]))
                    c.wait(dve)
                    dve.wait_ge(s_rk, g + 1)
                    c.inc(dve.tensor_scalar(tok[:, :], tok[:, :], float(SB * S), None, ALU.add))
                    c.link(dve, dve.tensor_tensor(rsum[:, :, :], ps_rank.rearrange("p (j e) -> p j e", j=SB),
                                                  fill[:, :].unsqueeze(1).broadcast_to([P, SB, NE]), ALU.add))
                    c.inc(dve.tensor_tensor(fill[:, :], fill[:, :], ps_tot, ALU.add))
                    for oh, t in ((oh1, tmp1), (oh2, tmp2)):
                        c.inc(dve.tensor_tensor(t[:, :, :], oh[:, :, :], rsum[:, :, :], ALU.mult))
                    c.wait(dve)
                    for k, t in enumerate((tmp1, tmp2)):
                        c.inc(dve.tensor_reduce(slotf[:, :, k], t[:, :, :], AX, ALU.add))
                    c.wait(dve)
                    dve.tensor_copy(sloti[:, :, :], slotf[:, :, :]).then_inc(s_rec, 1)

                def prologue(step):
                    next_stats(step)
                    next_norm(step, True)
                    centre_v(step)
                    next_gates(step, True)
                    c_dn.end()

                def body(step, more):
                    nxt = after(step)
                    c_dh.begin(number(step))
                    if more:
                        next_stats(nxt)
                    c_of(step, 0)
                    if more:
                        next_norm(nxt, False)
                    weights_low(step, 0)
                    c_of(step, 1)
                    if more:
                        centre_v(nxt)
                    weights_low(step, 1)
                    c_of(step, 2)
                    weights_low(step, 2)
                    c_of(step, 3)
                    if more:
                        next_gates(nxt, False)
                        c_dn.end()
                    weights_low(step, 3)
                    h_norm(step)
                    x1_norm(step)
                    route(step)
                    c_dh.end()

                run_steps(dve, prologue, body)

        b2r = xbuf[:, :, :, :].rearrange("p a j d -> p (a j) d")
        xg = ctxb
        hf = E[:, 0:2, :, :].rearrange("p a c t -> p a (c t)")
        hh = E[:, 2:4, :, :].rearrange("p a c t -> p a (c t)").bitcast(F16).rearrange(
            "p a (w c t) -> p a w c t", w=2, c=FC)
        xh = normed[:, 0:2, :].bitcast(F16).rearrange("p a (w c t) -> p a w c t", w=2, c=KC)
        yo = work
        ps_xt = ps_t
        ps_l1 = ps_s[:, :, :].rearrange("p (a b) n -> p a b n", a=2)
        ps_y = (ps_h, ps_m)

        s_b2 = sem("b2_in")
        s_tl = sem("tiles_listed")
        s_ij = sem("tile_numbers")
        c_tl = Chain(sem("tile_list_steps"), 0)
        s_ig = [sem(f"gather_ids_in{k}") for k in range(4)]
        s_is = [sem(f"scatter_ids_in{k}") for k in range(4)]
        s_xg0 = sem("rows_cleared")
        s_gx = [sem(f"rows_in{k}") for k in range(4)]
        s_xT = sem("rows_turned")
        s_xhi = sem("rows_high")
        s_xh = sem("row_halves")
        s_l1 = sem("layer1_half")
        s_ge = sem("gelu_half")
        s_hhi = sem("gelu_high")
        s_hh = sem("gelu_halves")
        s_l2 = sem("layer2")
        s_yb = sem("rows_with_bias")
        s_y = sem("rows_gated")
        s_add = sem("rows_added")
        s_af = sem("scatter_ids_free")
        GE0, HH0, L20, Y0, FREE0 = 1, 1, 1, 4, 3

        class Turn:

            def __init__(self, i, u):
                self.i, self.u = i, u
                self.t = u if isinstance(i, int) and i == 0 else i * 4 + u

            def slot(self, ahead):
                return (self.u + ahead) % 4

            def landed(self, ahead):
                return (self.i + ((self.u + ahead) // 4 + 1)) * 16

        def run_turns(eng, turn):
            turn(Turn(0, 0), True, NT)
            with eng.Fori(0, LOOP_TURNS) as i:
                for u in range(1, 5):
                    turn(Turn(i, u), False, NT)
            for t in range(4 * LOOP_TURNS + 1, NT + 1):
                turn(Turn(0, t), False, NT - t)

        with nc.Block() as block:

            @block.sync
            def _(sp):
                sp.dma_start(b2r, b2.partition_broadcast(P)).then_inc(s_b2, 16)
                sp.wait_ge(s_tl, 2)

                def ids(tr, ahead, dst, sems, wait=None):
                    row = sp.value_load(rowi[0:1, bass.ds(tr.t + ahead, 1)], min_val=0, max_val=PAD_ROW)
                    if wait is not None:
                        wait()
                    sp.dma_start(dst[:, tr.slot(ahead), :], table[bass.ds(row, P), :])\
                      .then_inc(sems[tr.slot(ahead)], 16)

                def turn(tr, first, left):
                    if first:
                        for k in range(4):
                            ids(tr, k, ids_g, s_ig)
                        ids(tr, 0, ids_s, s_is)
                    if left > 4:
                        ids(tr, 4, ids_g, s_ig, lambda: sp.wait_ge(s_gx[tr.slot(0)], tr.landed(0)))
                    if left > 1:
                        ids(tr, 1, ids_s, s_is, None if first else
                            lambda: sp.wait_ge(s_af, tr.t + (FREE0 - 2)))

                run_turns(sp, turn)
                for n in (NT, NT + 1):
                    sp.wait_ge(s_ig[n % 4], (n // 4 + 1) * 16)

            @block.gpsimd
            def _(pool):
                pool.sem_inc(s_af, FREE0)
                pool.iota(it_j, [[1, NL]], base=0, channel_multiplier=0).then_inc(s_ij, 1)
                pool.memset(xg[:, :, :], 0.0).then_inc(s_xg0, 1)
                pool.wait_ge(s_xg0, 1)

                def gather(tr, ahead):
                    k = tr.slot(ahead)
                    pool.wait_ge(s_ig[k], tr.landed(ahead))
                    pool.sem_inc(s_held, 1)
                    pool.indirect_dma_start(xg[:, k, :], None, xf_dram,
                                            bass.IndirectOffsetOnAxis(ap=ids_g[:, k, 0:1], axis=0),
                                            bounds_check=T - 1, oob_is_err=False).then_inc(s_gx[k], 16)

                def add_rows(tr):
                    k = tr.slot(-1)
                    pool.wait_ge(s_y, tr.t + Y0)
                    pool.sem_inc(s_held, 1)
                    pool.indirect_dma_start(out_rows, bass.IndirectOffsetOnAxis(ap=ids_s[:, k, 0:1], axis=0),
                                            yo[:, k, :], None, bounds_check=T - 1, oob_is_err=False,
                                            compute_op=ALU.add).then_inc(s_add, 16)
                    pool.wait_ge(s_add, tr.t * 16)
                    pool.sem_inc(s_af, 1)

                def turn(tr, first, left):
                    if first:
                        for ahead in range(3):
                            gather(tr, ahead)
                    if left > 3:
                        if not first:
                            pool.wait_ge(s_xT, tr.t)
                        gather(tr, 3)
                    if not first:
                        add_rows(tr)

                run_turns(pool, turn)
                pool.wait_ge(s_gx[NT % 4], (NT // 4 + 1) * 16)

            @block.tensor
            def _(pe):
                def turn_rows(tr, ahead):
                    pe.wait_ge(s_gx[tr.slot(ahead)], tr.landed(ahead))
                    for c in range(KC):
                        ins = pe.transpose(ps_xt[:, c * P:(c + 1) * P], xg[:, tr.slot(ahead), c * P:(c + 1) * P],
                                           ident[:, :])
                    ins.then_inc(s_xT, 1)

                def layer1(tr, expert):
                    half = FC // 2
                    for f in range(FC):
                        o = ps_l1[:, tr.slot(0) % 2, f // half, (f % half) * P:(f % half + 1) * P]
                        parts = [(a, b, k) for a, b in ((0, 0), (0, 1), (1, 0)) for k in range(KC)]
                        for n, (a, b, k) in enumerate(parts):
                            w = w1s[:, bass.ds(expert, 1), a, k, f * P:(f + 1) * P].rearrange("p a f -> p (a f)")
                            ins = pe.matmul(o, w, xh[:, tr.slot(0) % 2, b, k, :], start=(n == 0),
                                            stop=(n == len(parts) - 1))
                        if f % half == half - 1:
                            ins.then_inc(s_l1, 1)

                def layer2(tr, expert):
                    k = tr.slot(-1)
                    for f in range(FC):
                        if f % (FC // 2) == 0:
                            pe.wait_ge(s_hh, tr.t * 2 + (f // (FC // 2) + HH0 - 1))
                        for n, (a, b) in enumerate(((0, 0), (0, 1), (1, 0))):
                            w = w2s[:, bass.ds(expert, 1), b, f, :].rearrange("p a d -> p (a d)")
                            ins = pe.matmul(ps_y[k % 2][:, 0:D], hh[:, k % 2, a, f, :], w,
                                            start=(f == 0 and n == 0), stop=(f == FC - 1 and n == 2))
                    ins.then_inc(s_l2, 1)

                pe.sem_inc(s_l2, L20)
                pe.wait_ge(s_tl, 2)

                def turn(tr, first, left):
                    if first:
                        turn_rows(tr, 0)
                    else:
                        last = pe.value_load(exi[0:1, bass.ds(tr.t - 1, 1)], min_val=0, max_val=NE - 1)
                    if left > 0:
                        expert = pe.value_load(exi[0:1, bass.ds(tr.t, 1)], min_val=0, max_val=NE - 1)
                        pe.wait_ge(s_xh, tr.t + 1)
                        if left > 1:
                            turn_rows(tr, 1)
                        if not first:
                            pe.wait_ge(s_ge, tr.t * 2 + (GE0 - 2))
                        layer1(tr, expert)
                    if not first:
                        pe.wait_ge(s_y, tr.t + (Y0 - 2))
                        layer2(tr, last)

                run_turns(pe, turn)

            @block.scalar
            def _(act):
                act.sem_inc(s_ge, GE0)
                act.wait_ge(s_tl, 2)

                def turn(tr, first, left):
                    if not left > 0:
                        return
                    expert = act.value_load(exi[0:1, bass.ds(tr.t, 1)], min_val=0, max_val=NE - 1)
                    k, w = tr.slot(0) % 2, FC // 2
                    if not first:
                        act.wait_ge(s_hh, tr.t * 2 + (HH0 - 2))
                    for half in range(2):
                        act.wait_ge(s_l1, tr.t * 2 + (half + 1))
                        for q in range(w):
                            f = half * w + q
                            ins = act.activation(hf[:, k, f * P:(f + 1) * P], ps_l1[:, k, half, q * P:(q + 1) * P],
                                                 ACT.Gelu, bias=b1T[:, bass.ds(expert, 1), f], scale=1.0 / W_SCALE)
                        ins.then_inc(s_ge, 1)

                run_turns(act, turn)

            @block.vector
            def _(dve):
                dve.sem_inc(s_y, Y0)
                dve.sem_inc(s_hh, HH0)
                one, c, NJ = slice(0, 1), c_tl, NL
                dve.wait_ge(s_ij, 1)
                c.inc(dve.tensor_copy(jf, it_j))
                c.inc(dve.memset(zer[:, :], 0.0))
                c.link(dve, dve.tensor_tensor(cntf[:, :], fill[one, :], ebase[one, :], ALU.subtract))
                c.link(dve, dve.tensor_scalar(cnti[:, :], cntf[:, :], float(P - 1), None, ALU.add))
                c.link(dve, dve.tensor_scalar(cnti[:, :], cnti[:, :], P.bit_length() - 1, None,
                                              ALU.logical_shift_right))
                c.link(dve, dve.tensor_copy(ntf[:, :], cnti[:, :]))
                c.link(dve, dve.tensor_tensor_scan(endf[:, :], ntf[:, :], zer[:, :], 0.0, ALU.add, ALU.add))
                jw = jf[:, :].unsqueeze(2).broadcast_to([1, NJ, NE])
                ew = endf[:, :].unsqueeze(1).broadcast_to([1, NJ, NE])
                nw = ntf[:, :].unsqueeze(1).broadcast_to([1, NJ, NE])
                c.link(dve, dve.tensor_tensor(cmpf[:, :, :], jw, ew, ALU.is_ge))
                c.link(dve, dve.tensor_reduce(exf[:, :], cmpf[:, :, :], AX, ALU.add))
                c.link(dve, dve.tensor_tensor(cmpf[:, :, :], cmpf[:, :, :], nw, ALU.mult))
                c.link(dve, dve.tensor_reduce(pastf[:, :], cmpf[:, :, :], AX, ALU.add))
                c.link(dve, dve.tensor_tensor(rowf[:, :], jf[:, :], pastf[:, :], ALU.subtract))
                c.link(dve, dve.tensor_scalar(pastf[:, :], exf[:, :], float(NE), float(P), ALU.is_lt, ALU.mult))
                c.link(dve, dve.tensor_tensor(rowf[:, :], rowf[:, :], pastf[:, :], ALU.mult))
                c.link(dve, dve.scalar_tensor_tensor(out=rowf[:, :], in0=exf[:, :], scalar=float(T), in1=rowf[:, :],
                                                     op0=ALU.mult, op1=ALU.add))
                dve.tensor_copy(rowi[:, :], rowf[:, :]).then_inc(s_tl, 1)
                dve.tensor_scalar(exi[:, :], exf[:, :], float(NE - 1), None, ALU.min).then_inc(s_tl, 1)
                dve.wait_ge(s_tl, 2)
                dve.wait_ge(s_b2, 16)

                def split_rows(tr, ahead):
                    dve.wait_ge(s_xT, tr.t + (ahead + 1))
                    src = ps_xt[:, 0:D].rearrange("p (c t) -> p c t", c=KC)
                    hi, lo = (xh[:, tr.slot(ahead) % 2, w, :, :] for w in range(2))
                    dve.tensor_copy(hi, src).then_inc(s_xhi, 1)
                    dve.wait_ge(s_xhi, tr.t + (ahead + 1))
                    dve.tensor_tensor(lo, src, hi, ALU.subtract).then_inc(s_xh, 1)

                def split_gelu(tr, half):
                    w, k = FC // 2, tr.slot(0) % 2
                    dve.wait_ge(s_ge, tr.t * 2 + (half + 1 + GE0))
                    src = hf[:, k, half * w * P:(half + 1) * w * P].rearrange("p (c t) -> p c t", c=w)
                    hi, lo = (hh[:, k, a, half * w:(half + 1) * w, :] for a in range(2))
                    dve.tensor_copy(hi, src).then_inc(s_hhi, 1)
                    dve.wait_ge(s_hhi, tr.t * 2 + (half + 1))
                    dve.tensor_tensor(lo, src, hi, ALU.subtract).then_inc(s_hh, 1)

                def gate_rows(tr, expert):
                    k = tr.slot(-1)
                    dve.wait_ge(s_is[k], tr.landed(-1))
                    dve.wait_ge(s_l2, tr.t + L20)
                    dve.scalar_tensor_tensor(
                        out=yo[:, k, :], in0=ps_y[k % 2][:, 0:D], scalar=1.0 / W_SCALE,
                        in1=b2r[:, bass.ds(expert, 1), :].rearrange("p a d -> p (a d)"), op0=ALU.mult,
                        op1=ALU.add).then_inc(s_yb, 1)
                    dve.wait_ge(s_yb, tr.t)
                    dve.tensor_scalar(yo[:, k, :], yo[:, k, :], ids_s[:, k, 1:2].bitcast(F32), None,
                                      ALU.mult).then_inc(s_y, 1)

                def turn(tr, first, left):
                    if first:
                        split_rows(tr, 0)
                    else:
                        expert = dve.value_load(exi[0:1, bass.ds(tr.t - 1, 1)], min_val=0, max_val=NE - 1)
                    if left > 1:
                        if not first:
                            dve.wait_ge(s_l1, tr.t * 2)
                        split_rows(tr, 1)
                    if left > 0:
                        if not first:
                            dve.wait_ge(s_l2, tr.t + (L20 - 1))
                        split_gelu(tr, 0)
                        split_gelu(tr, 1)
                    if not first:
                        gate_rows(tr, expert)

                run_turns(dve, turn)


_INS = ["x", "ctx_1024", "L0_xattn_igate_w", "L0_xattn_igate_b", "L0_xattn_fgate_w", "L0_xattn_fgate_b",
        "L0_xattn_out_w", "L0_ffn_gate_w", "L0_ffn_w1", "L0_ffn_b1", "L0_ffn_w2", "L0_ffn_b2"]


def kernel(**inputs):
    import numpy as np
    import concourse.bacc as bacc
    from concourse.bass_utils import run_bass_kernel_spmd

    nc = bacc.Bacc("TRN2", target_bir_lowering=False, num_devices=1)
    arrays, args = {}, []
    for name in _INS:
        a = np.ascontiguousarray(inputs[name])
        arrays[f"in_{name}"] = a
        args.append(nc.dram_tensor(f"in_{name}", a.shape, mybir.dt.from_np(a.dtype), kind="ExternalInput").ap())
    shape = arrays["in_x"].shape
    args.append(nc.dram_tensor("out_rows", shape, F32, kind="ExternalOutput").ap())
    build(nc, *args)
    r = run_bass_kernel_spmd(nc, [arrays], core_ids=[0])
    return r.results[0]["out_rows"]
```

```python
from contextlib import ExitStack

import concourse.bass as bass
from concourse import mybir

ALU = mybir.AluOpType
ACT = mybir.ActivationFunctionType
AX = mybir.AxisListType.X
F32 = mybir.dt.float32
F16 = mybir.dt.float16
BF16 = mybir.dt.bfloat16
I32 = mybir.dt.int32

P = 128
EPS = 1e-6
LN_EPS = 1e-5
BIG = 1e30
W_SCALE = 64.0


class Chain:

    def __init__(self, sem, per_step):
        self.sem, self.per_step, self.base, self.n = sem, per_step, 0, 0

    def begin(self, step):
        self.base, self.n = step * self.per_step, 0

    def inc(self, ins):
        self.n += 1
        ins.then_inc(self.sem, 1)

    def wait(self, eng):
        eng.wait_ge(self.sem, self.base + self.n)

    def link(self, eng, ins):
        self.inc(ins)
        self.wait(eng)

    def end(self):
        assert self.n == self.per_step, (self.n, self.per_step)


def build(nc, x, ctx_in, igate_w, igate_b, fgate_w, fgate_b, out_w, gate_w, w1, b1, w2, b2, out):
    NB, S, D = x.shape
    NH = igate_b.shape[0]
    DH = D // NH
    HG = P // DH
    KC = D // P
    NE, _, F = w1.shape
    FC = F // P
    SB = 4
    NSTEP = NB // SB
    T = NB * S
    G = SB * NH
    QK_SCALE = float(DH) ** -0.5
    assert S == P and D == KC * P and NH == KC * HG and NSTEP % 2 == 0
    NT = (2 * T + NE * (P - 1)) // P
    NL = NT + 2
    PAD_ROW = NE * T
    TABLE = NE * T + P
    TB = TABLE // P
    LOOP_TURNS = (NT - 3) // 4
    assert 4 * LOOP_TURNS + 3 == NT

    HALVES = ((0, 0), (0, 1), (1, 0))

    DVE_NEXT, DVE_GATES, DVE_HERE, DVE_LAST, ACT_NEXT, ACT_HERE, ACT_LAST = 11, 2, 11, 31, 1, 1, 1

    xs_dram = x.rearrange("(g j) s d -> g s j d", j=SB)
    ctx_dram = ctx_in.rearrange("(g j) s d -> g s j d", j=SB)
    out_dram = out.rearrange("(g j) s d -> g s j d", j=SB)
    out_rows = out.rearrange("b s d -> (b s) d")
    xf_dram = nc.dram_tensor("xf_rows", (T, D), F32, kind="Internal").ap()
    xf_step = xf_dram.rearrange("(g j s) d -> g s j d", j=SB, s=S)
    scan_dram = nc.dram_tensor("scan_rows", (NSTEP, G, P), F32, kind="Internal").ap()
    table = nc.dram_tensor("expert_table", (TABLE, 2), I32, kind="Internal").ap()
    w1_dram = w1.rearrange("e (k p) f -> (e k) p f", p=P)
    w2_dram = w2.rearrange("e (h c p) d -> (e h) p c d", h=2, p=P)
    NPIECE = NE * 4
    PW = 1024
    assert NPIECE == NB and F == PW and FC * D == 2 * PW

    with ExitStack() as ctx:
        def sb(name, shape, dt=F32):
            return ctx.enter_context(nc.sbuf_tensor(name, shape, dt))

        def sem(name):
            return ctx.enter_context(nc.semaphore(name))

        w1s = sb("w1_halves", [P, NE, 2, KC, F], F16)
        w2s = sb("w2_halves", [P, NE, 2, FC, D], F16)
        xin = sb("x_to_norm", [P, SB, D])
        xres = sb("x_residual", [P, SB, D])
        ctxb = sb("ctx_slots", [P, SB, D])
        normed = sb("normed", [P, SB, D])
        vaug = sb("v_centred_and_one", [P, 2, SB, NH, DH + 1])
        qkT = sb("q_and_k_halves", [P, 2, SB, 2, 2 * KC, P], F16)
        E = sb("decay_slots", [P, SB, NH, P])
        Hs = sb("h_slots", [P, SB, NH, DH + 1])
        work = sb("work", [P, SB, D])
        stage = sb("weight_stage", [P, 2, PW])
        ident = sb("ident", [P, P])
        tri = sb("tri", [P, P])
        tri_s = sb("tri_strict", [P, P], BF16)
        ones = sb("ones", [P, P], BF16)
        low = sb("low", [G, 1])
        outw = sb("out_w_rows", [P, D])
        gbias = sb("gate_bias_rows", [P, 2, NH])
        wraw = E[0:2 * NH, 0, :, :].rearrange("p a c -> p (a c)")[:, 0:3 * D]
        wgr = E[:, 2, 0, 0:6 * KC * NH].rearrange("p (c o) -> p c o", c=3 * KC)
        graw = E[:, 3, 0, 0:2 * NH].rearrange("p (a h) -> p a h", a=2)
        b1raw = E[0:NE * FC, 1, 0, :]
        wg = sb("gate_w_halves", [P, 2, 2 * KC, 2 * NH], F16)
        gw = sb("router_w", [P, KC, NE])
        b1T = sb("b1_turned", [P, NE, FC])
        revidx = sb("rev_index", [P, SB, NE])
        ebase = sb("expert_base", [P, NE])
        tok = sb("token_ids", [P, SB])
        h_flat = sb("routing_work", [P, 5 * SB * NE])
        dl, key, oh1, oh2, dl2 = (
            h_flat[:, n * SB * NE:(n + 1) * SB * NE].rearrange("p (j e) -> p j e", j=SB) for n in range(5))
        rsum, tmp1, tmp2 = dl, key, dl2
        it_rev, it_base, it_tok = dl.bitcast(I32), key[:, 0, :].bitcast(I32), oh1[:, 0, 0:SB].bitcast(I32)
        v_flat = vaug[0:1, :, :, :, :].rearrange("p a j h e -> p (a j h e)")
        exf, pastf, rowf, jf, it_j, rowi, exi = (v_flat[:, n * NL:(n + 1) * NL] for n in range(7))
        it_j, rowi, exi = (a.bitcast(I32) for a in (it_j, rowi, exi))
        xT = ctxb[:, :, :].rearrange("p j (c t) -> p j c t", c=KC)
        st = sb("bn_parts", [P, SB, 6])
        mv = sb("mean_var", [P, SB, 2])
        ve = sb("var_eps", [P, SB])
        lnv = sb("ln_var", [P, SB])
        rs = sb("rstd", [P, SB])
        nt1 = sb("newton", [P, SB])
        nb = sb("minus_mean_rstd", [P, SB])
        vsum = sb("v_sum", [P, SB, NH])
        gs = sb("gates", [P, SB, 2, NH])
        nabs = sb("minus_abs_f", [P, SB, NH])
        ex1 = sb("exp_f", [P, SB, NH])
        lsg = sb("log_sigmoid", [P, SB, NH])
        csb = sb("log_f_sum", [P, G])
        acol = sb("i_minus_sum", [P, 2, G])
        arun = sb("running_max", [G, P])
        mld = sb("max_log_d", [P, G])
        en = sb("exp_minus_max", [P, 2, SB, NH])
        ssq = sb("square_sum", [P, G])
        nrm = sb("normalizer", [P, SB, NH])
        rn = sb("one_over_norm", [P, G])
        hv = sb("h_var", [P, G])
        hln = ssq
        ht = nabs[:, :, :].rearrange("p j h -> p (j h)")
        hy = sb("h_rstd", [P, G])
        m1 = sb("top1", [P, SB])
        kmax = sb("key_max", [P, SB])
        m2 = sb("top2", [P, SB])
        mask = sb("chosen", [P, SB, NE], BF16)
        p2 = sb("exp_top2", [P, SB])
        den = sb("gate_sum", [P, SB])
        slotf = sb("slot_f", [P, SB, 2])
        sloti = sb("slot_i", [P, SB, 2], I32)
        rec = sb("record", [P, SB, 2, 2], I32)
        fill = sb("expert_fill", [P, NE])
        ids_g = sb("ids_for_gather", [P, 4, 2], I32)
        ids_s = sb("ids_for_scatter", [P, 4, 2], I32)
        cntf = sb("count", [1, NE])
        cnti = sb("count_i", [1, NE], I32)
        ntf = sb("tiles_of", [1, NE])
        zer = sb("zeros", [1, NE])
        endf = sb("tiles_up_to", [1, NE])
        cmpf = Hs[0:1, :, :, :].rearrange("p j h e -> p (j h e)")[:, 0:NL * NE].rearrange(
            "p (t e) -> p t e", e=NE)

        ps_s = ctx.enter_context(nc.psum_tensor("scores", [P, HG, 512], F32))
        ps_h = ctx.enter_context(nc.psum_tensor("pv", [P, 512], F32))
        ps_m = ctx.enter_context(nc.psum_tensor("gate_bank", [P, 512], F32))
        ps_x = ctx.enter_context(nc.psum_tensor("route_bank", [P, 512], F32))
        ps_t = ctx.enter_context(nc.psum_tensor("pv_odd", [P, 512], F32))
        ps_pv = (ps_h, ps_t)
        ps_gate = ps_m[:, 0:G * 2].rearrange("p (j a h) -> p j a h", j=SB, a=2)
        ps_cs = ps_m[:, 64:64 + G]
        ps_aT = ps_m[0:G, 128:128 + P]
        ps_ab = ps_m[:, 256:256 + G]
        ps_log = ps_x[:, 0:SB * NE].rearrange("p (j e) -> p j e", j=SB)
        ps_rank = ps_x[:, 64:64 + SB * NE]
        ps_tot = ps_x[:, 128:128 + NE]

        s_held = sem("held")
        s_const = sem("const_in")
        s_c0 = sem("zeroed")
        s_cp = sem("pool_consts")
        s_tab0 = sem("table_fill")
        s_tab = sem("table_written")
        s_wt = sem("gate_w_transposed")
        s_cd = sem("dve_consts")
        s_x = sem("x_in")
        s_xr = sem("x_residual_in")
        s_ctx = sem("ctx_in")
        s_w = [sem(f"weights_in{p}") for p in range(2)]
        s_hi = sem("weights_high")
        s_lo = sem("weights_low")
        c_dn = Chain(sem("dve_next"), DVE_NEXT)
        c_dh = Chain(sem("dve_here"), DVE_HERE)
        c_an = Chain(sem("act_next"), ACT_NEXT)
        c_ah = Chain(sem("act_here"), ACT_HERE)
        c_dl = Chain(sem("dve_last"), DVE_LAST)
        c_al = Chain(sem("act_last"), ACT_LAST)
        c_ax = Chain(sem("act_log_f"), 1)
        c_dg = Chain(sem("dve_gates"), DVE_GATES)
        s_ve = sem("var_ready")
        s_rs = sem("rstd_guess")
        s_nb = sem("q_scale_ready")
        s_vs = sem("v_summed")
        s_xb = sem("xf_scale_ready")
        s_ho = sem("h_scaled")
        s_hw = sem("h_weighted")
        s_qn = sem("q_normed")
        s_vc = sem("v_ready")
        s_tq = sem("qk_turned")
        s_te = sem("qk_high")
        s_ql = sem("qk_halves")
        s_gt = sem("gates_summed")
        s_na = sem("f_abs_ready")
        s_ln = sem("ln_ready")
        s_ls = sem("log_sigmoid_ready")
        s_cs = sem("log_f_summed")
        s_a = sem("a_ready")
        s_aT = sem("a_turned")
        s_run = sem("running_max_ready")
        s_ab = sem("running_max_turned")
        s_mld = sem("max_log_d_ready")
        s_en = sem("exp_minus_max_ready")
        s_scan = sem("scan_written")
        s_e = [sem(f"running_max_in{j}") for j in range(SB)]
        s_em = sem("masked")
        s_ee = sem("decay_ready")
        s_s = sem("scores_ready")
        s_cm = sem("c_ready")
        s_pv = sem("pv_ready")
        s_hev = sem("h_in_sbuf")
        s_hve = sem("h_var_ready")
        s_hy = sem("h_rstd_guess")
        s_ve2 = sem("var2_ready")
        s_rs2 = sem("rstd2_guess")
        s_x1 = sem("x1_ready")
        s_xf = sem("xf_ready")
        s_xo = sem("x1_written")
        s_xfo = sem("xf_written")
        s_xt = sem("xf_turned")
        s_xe = sem("xf_turned_in_sbuf")
        s_lg = sem("logits_ready")
        s_m2 = sem("top2_ready")
        s_p2 = sem("exp_top2_ready")
        s_mk = sem("chosen_ready")
        s_rk = sem("rank_ready")
        s_rec = sem("records_ready")
        s_sc = sem("table_scattered")
        s_rf = sem("records_free")

        def number(step):
            return step[0] * 2 + step[1]

        def run_steps(eng, prologue, body, epilogue):
            end = NSTEP // 2 - 1
            prologue((0, 0), (0, 1))
            body(None, (0, 0), (0, 1), (1, 0))
            with eng.Fori(0, end - 1) as i:
                body((i, 0), (i, 1), (i + 1, 0), (i + 1, 1))
                body((i, 1), (i + 1, 0), (i + 1, 1), (i + 2, 0))
            body((end - 1, 0), (end - 1, 1), (end, 0), (end, 1))
            body((end - 1, 1), (end, 0), (end, 1), None)
            body((end, 0), (end, 1), None, None)
            epilogue((end, 1))

        with nc.Block() as block:

            @block.sync
            def _(sp):
                for o, gate in ((0, igate_w), (NH, fgate_w)):
                    for r in range(HG):
                        sp.dma_start(wraw[o + KC * r:o + KC * r + KC, :], gate[r::HG, :]).then_inc(s_const, 16)
                sp.dma_start(b1raw, b1.rearrange("e (c p) -> (e c) p", p=P)).then_inc(s_const, 16)
                sp.dma_start(xin[:, :, :], xs_dram[0]).then_inc(s_x, 16)
                sp.dma_start(ctxb[:, :, :], ctx_dram[0]).then_inc(s_ctx, 16)
                sp.dma_start(xres[:, :, :], xs_dram[0]).then_inc(s_xr, 16)
                sp.dma_start(gw[:, :, :], gate_w.rearrange("(k p) e -> p k e", p=P)).then_inc(s_const, 16)
                sp.dma_start(outw[:, :], out_w.partition_broadcast(P)).then_inc(s_const, 16)
                for a, gate in ((0, igate_b), (1, fgate_b)):
                    sp.dma_start(graw[:, a, :], gate.partition_broadcast(P)).then_inc(s_const, 16)
                sp.wait_ge(s_tab0, 2)
                sp.sem_inc(s_held, 1)
                sp.dma_start(table.rearrange("(p n) w -> p n w", p=P),
                             stage[:, 0, 0:2 * TB].bitcast(I32).rearrange("p (n w) -> p n w", w=2)).then_inc(s_tab, 16)
                sp.wait_ge(s_tab, 16)

                def weights(n_half, half):
                    src = (w1_dram, w2_dram)[half]
                    dst = stage[:, half, :]
                    if half:
                        dst = dst.rearrange("p (c d) -> p c d", d=D)
                    sp.dma_start(dst, src[n_half]).then_inc(s_w[half], 16)

                def write_scan(step):
                    g = number(step)
                    sp.wait_ge(s_run, g + 1)
                    sp.sem_inc(s_held, 1)
                    sp.dma_start(scan_dram[g], arun[:, :]).then_inc(s_scan, 16)

                def read_scan(step, free, places):
                    g = number(step)
                    sp.wait_ge(s_scan, (g + 1) * 16)
                    sp.sem_inc(s_held, 1)
                    for j in places:
                        if free:
                            sp.wait_ge(s_pv, g * SB + (j + 1 - SB))
                        sp.sem_inc(s_held, 1)
                        sp.dma_start(E[:, j, :, :],
                                     scan_dram[g, j * NH:j * NH + NH, :].partition_broadcast(P)).then_inc(s_e[j], 16)

                def load_x(step):
                    g = number(step)
                    sp.wait_ge(s_qn, g * SB)
                    sp.sem_inc(s_held, 1)
                    sp.dma_start(xin[:, :, :], xs_dram[g]).then_inc(s_x, 16)

                def load_ctx(step, first):
                    g = number(step)
                    sp.wait_ge(s_tq, g * SB)
                    sp.sem_inc(s_held, 1)
                    sp.wait_ge(s_vc, g)
                    sp.sem_inc(s_held, 1)
                    if not first:
                        sp.wait_ge(s_lg, g - 1)
                    sp.sem_inc(s_held, 1)
                    sp.dma_start(ctxb[:, :, :], ctx_dram[g]).then_inc(s_ctx, 16)

                def write_xf(step):
                    g = number(step)
                    sp.wait_ge(s_xf, (g + 1) * SB)
                    sp.sem_inc(s_held, 1)
                    sp.dma_start(xf_step[g], normed[:, :, :]).then_inc(s_xfo, 16)

                def write_x1(step):
                    g = number(step)
                    sp.wait_ge(s_x1, g + 1)
                    sp.sem_inc(s_held, 1)
                    sp.dma_start(out_dram[g], xres[:, :, :]).then_inc(s_xo, 16)

                def prologue(step, nxt):
                    weights(0, 0)
                    weights(0, 1)
                    load_x(nxt)
                    load_ctx(nxt, True)
                    write_scan(step)
                    read_scan(step, False, range(SB))
                    load_x((1, 0))

                def body(last, step, nxt, after_next):
                    g = number(step)
                    if last is not None:
                        write_xf(last)
                        sp.wait_ge(s_xo, g * 16)
                        sp.sem_inc(s_held, 1)
                        sp.dma_start(xres[:, :, :], xs_dram[g]).then_inc(s_xr, 16)
                    if last is not None:
                        sp.wait_ge(s_lo, g * SB)
                        sp.sem_inc(s_held, 1)
                        weights(g * 2, 1)
                    sp.wait_ge(s_lo, g * SB + 1)
                    sp.sem_inc(s_held, 1)
                    weights(g * 2 + 1, 0)
                    if nxt is not None:
                        write_scan(nxt)
                        read_scan(nxt, True, range(2))
                    sp.wait_ge(s_lo, g * SB + 2)
                    sp.sem_inc(s_held, 1)
                    weights(g * 2 + 1, 1)
                    if after_next is not None:
                        load_ctx(after_next, False)
                    if nxt is not None:
                        read_scan(nxt, True, range(2, SB))
                        sp.wait_ge(s_lo, g * SB + 3)
                        sp.sem_inc(s_held, 1)
                        weights(g * 2 + 2, 0)
                    write_x1(step)
                    if after_next is not None and not (isinstance(g, int) and g + 3 == NSTEP):
                        load_x((after_next[0] + after_next[1], 1 - after_next[1]))

                run_steps(sp, prologue, body, write_xf)
                sp.wait_ge(s_xo, 16 * NSTEP)
                sp.wait_ge(s_xfo, 16 * (NSTEP + 1))

            @block.gpsimd
            def _(pool):
                pool.sem_inc(s_rf, 1)
                pool.sem_inc(s_xfo, 16)
                tab0 = stage[:, 0, 0:2 * TB].rearrange("p (n w) -> p n w", w=2)
                pool.iota(tab0[:, :, 0:1].bitcast(I32), [[0, TB]], base=T, channel_multiplier=0).then_inc(s_tab0, 1)
                pool.memset(tab0[:, :, 1:2], 0.0).then_inc(s_tab0, 1)
                pool.memset(ident[:, :], 0.0).then_inc(s_c0, 1)
                pool.memset(tri[:, :], 1.0).then_inc(s_c0, 1)
                pool.memset(tri_s[:, :], 1.0).then_inc(s_c0, 1)
                pool.wait_ge(s_c0, 3)
                pool.affine_select(out=ident[:, :], in_=ident[:, :], compare_op=ALU.not_equal, fill=1.0,
                                   base=0, pattern=[[-1, P]], channel_multiplier=1).then_inc(s_cp, 1)
                pool.affine_select(out=tri[:, :], in_=tri[:, :], compare_op=ALU.is_ge, fill=0.0,
                                   base=0, pattern=[[1, P]], channel_multiplier=-1).then_inc(s_cp, 1)
                pool.affine_select(out=tri_s[:, :], in_=tri_s[:, :], compare_op=ALU.is_ge, fill=0.0,
                                   base=-1, pattern=[[1, P]], channel_multiplier=-1).then_inc(s_cp, 1)
                pool.memset(ones[:, :], 1.0).then_inc(s_cp, 1)
                pool.memset(low[:, :], -3e38).then_inc(s_cp, 1)
                for p in range(2):
                    pool.memset(vaug[:, p, :, :, DH:DH + 1], 1.0).then_inc(s_cp, 1)
                pool.iota(it_rev[:, :, :], [[0, SB], [-1, NE]], base=NE, channel_multiplier=0).then_inc(s_cp, 1)
                pool.iota(it_base[:, :], [[T, NE]], base=0, channel_multiplier=0).then_inc(s_cp, 1)
                pool.iota(it_tok[:, :], [[S, SB]], base=0, channel_multiplier=1).then_inc(s_cp, 1)
                pool.wait_ge(s_tab, 16)

                big = pool.to_reg(BIG)

                def masks(step):
                    g = number(step)
                    for j in range(SB):
                        pool.wait_ge(s_e[j], (g + 1) * 16)
                        pool.sem_inc(s_held, 1)
                        pool.affine_select(out=E[:, j, :, :], in_=E[:, j, :, :], compare_op=ALU.is_ge, fill=big,
                                           base=0, pattern=[[0, NH], [1, P]], channel_multiplier=-1).then_inc(s_em, 1)

                def prologue(step, nxt):
                    masks(step)

                def x1_of(step):
                    g = number(step)
                    pool.wait_ge(s_ho, g + 1)
                    pool.sem_inc(s_held, 1)
                    pool.tensor_tensor(work[:, :, :], work[:, :, :],
                                       outw[:, :].unsqueeze(1).broadcast_to([P, SB, D]), ALU.mult).then_inc(s_hw, 1)
                    pool.wait_ge(s_hw, g + 1)
                    pool.wait_ge(s_xr, (g + 1) * 16)
                    pool.sem_inc(s_held, 1)
                    pool.tensor_tensor(xres[:, :, :], xres[:, :, :], work[:, :, :], ALU.add).then_inc(s_x1, 1)

                def scatter(step):
                    g = number(step)
                    pool.wait_ge(s_rec, g + 1)
                    pool.sem_inc(s_held, 1)
                    for j in range(SB):
                        for k in range(2):
                            pool.indirect_dma_start(
                                table, bass.IndirectOffsetOnAxis(ap=sloti[:, j, k:k + 1], axis=0),
                                rec[:, j, k, :], None, bounds_check=TABLE - 1,
                                oob_is_err=False).then_inc(s_sc, 16)
                    pool.wait_ge(s_sc, (g + 1) * (2 * SB * 16))
                    pool.sem_inc(s_rf, 1)

                def body(last, step, nxt, after_next):
                    if nxt is not None:
                        masks(nxt)
                    x1_of(step)
                    if last is not None:
                        scatter(last)

                run_steps(pool, prologue, body, scatter)

            @block.scalar
            def _(act):
                act.preload_act_table_set("natural_log_exp_and_others")

                def rsqrt_guess(var, ln, y, chain, ready, done, count):
                    act.wait_ge(ready, count)
                    chain.link(act, act.activation(ln, var, ACT.Ln))
                    act.activation(y, ln, ACT.Exp, scale=-0.5).then_inc(done, 1)

                def next_guess(step):
                    c_an.begin(number(step))
                    rsqrt_guess(ve[:, :], lnv[:, :], rs[:, :], c_an, s_ve, s_rs, number(step) + 1)

                def normalize(src, done):
                    for j in range(SB):
                        act.activation(normed[:, j, :], src[:, j, :], ACT.Identity, scale=rs[:, j:j + 1],
                                       bias=nb[:, j:j + 1]).then_inc(done, 1)

                def next_normed(step, first):
                    g = number(step)
                    act.wait_ge(s_nb, g + 1)
                    if not first:
                        act.wait_ge(s_xfo, (g - 1) * 16)
                        act.wait_ge(s_lg, g - 1)
                    act.wait_ge(s_ctx, (g + 1) * 16)
                    normalize(xin, s_qn)

                def x1_normed(step, last):
                    g = number(step)
                    act.wait_ge(s_xb, g + 1)
                    if not last:
                        act.wait_ge(s_tq, (g + 3) * SB)
                    normalize(xres, s_xf)

                def turned(step, j):
                    g = number(step)
                    act.wait_ge(s_tq, g * SB + j + 1)
                    act.activation(qkT[:, step[1], j, 0, :, :].rearrange("p c t -> p (c t)"), ps_s[:, j, :],
                                   ACT.Copy).then_inc(s_te, 1)

                def log_sigmoid(step):
                    g = number(step)
                    act.wait_ge(s_na, g + 1)
                    c_ax.begin(g)
                    c_ax.link(act, act.activation(ex1[:, :, :], nabs[:, :, :], ACT.Exp))
                    act.activation(lsg[:, :, :], ex1[:, :, :], ACT.Ln, bias=1.0).then_inc(s_ln, 1)
                    c_ax.end()

                def exp_minus_max(step):
                    g = number(step)
                    act.wait_ge(s_mld, g + 1)
                    for j in range(SB):
                        ins = act.activation(
                            en[:, step[1], j, :].rearrange("p (u k) -> p k u", u=KC),
                            mld[:, j * NH:(j + 1) * NH].rearrange("p (k u) -> p k u", u=KC), ACT.Exp, scale=-1.0)
                    ins.then_inc(s_en, 1)

                def decay(step, j):
                    g = number(step)
                    act.wait_ge(s_em, g * SB + j + 1)
                    act.wait_ge(s_a, g + 1)
                    for c in range(NH):
                        ins = act.activation(E[:, j, c, :], E[:, j, c, :], ACT.Exp, scale=-1.0,
                                             bias=acol[:, step[1], j * NH + c:j * NH + c + 1])
                    ins.then_inc(s_ee, 1)

                def weights_high(step, n):
                    g, half, q = number(step), n % 2, n // 2
                    act.wait_ge(s_w[half], (g * 2 + (q + 1)) * 16)
                    if half == 0:
                        dst = w1s[:, bass.ds(g, 1), 0, q, :].rearrange("p a f -> p (a f)")
                    else:
                        dst = w2s[:, bass.ds(g, 1), 0, q * (FC // 2):(q + 1) * (FC // 2), :].rearrange(
                            "p a c d -> p (a c d)")
                    act.activation(dst, stage[:, half, :], ACT.Copy, scale=W_SCALE).then_inc(s_hi, 1)

                def h_out(step, j, first=False):
                    g = number(step)
                    act.wait_ge(s_pv, g * SB + j + 1)
                    if j == 0 and not first:
                        act.wait_ge(s_x1, g)
                    h = ps_pv[j % 2][:, 0:NH * (DH + 1)].rearrange("p (h e) -> p h e", h=NH)
                    act.activation(Hs[:, j, :, :], h, ACT.Copy)
                    act.activation(work[:, j, :].rearrange("p (h e) -> p h e", h=NH), h[:, :, 0:DH],
                                   ACT.Square).then_inc(s_hev, 1)

                def h_guess(step):
                    c_ah.begin(number(step))
                    rsqrt_guess(hv[:, :], hln[:, :], hy[:, :], c_ah, s_hve, s_hy, number(step) + 1)
                    c_ah.end()

                def x1_guess(step):
                    c_al.begin(number(step))
                    rsqrt_guess(ve[:, :], lnv[:, :], rs[:, :], c_al, s_ve2, s_rs2, number(step) + 1)
                    c_al.end()

                def xf_turned(step, r, last=False):
                    g = number(step)
                    vc = NSTEP if last else g + 3
                    act.wait_ge(s_xt, g * (SB // 2) + r + 1)
                    if r == 0:
                        act.wait_ge(s_vc, vc)
                    act.activation(xT[:, 2 * r:2 * r + 2, :, :].rearrange("p j c t -> p (j c t)"), ps_x[:, :],
                                   ACT.Copy).then_inc(s_xe, 1)

                def second_gate(step):
                    act.wait_ge(s_m2, number(step) + 1)
                    act.activation(p2[:, :], m2[:, :], ACT.Exp).then_inc(s_p2, 1)

                def prologue(step, nxt):
                    next_guess(step)
                    next_normed(step, True)
                    for j in range(SB):
                        turned(step, j)
                    c_an.end()
                    next_guess(nxt)
                    next_normed(nxt, True)
                    for j in range(SB):
                        turned(nxt, j)
                    c_an.end()
                    log_sigmoid(step)
                    exp_minus_max(step)
                    for j in range(SB - 1):
                        decay(step, j)

                def body(last, step, nxt, after_next):
                    if nxt is not None:
                        log_sigmoid(nxt)
                    if last is not None:
                        weights_high(last, 3)
                    weights_high(step, 0)
                    if last is not None:
                        x1_guess(last)
                        x1_normed(last, nxt is None)
                    decay(step, 3)
                    h_out(step, 0, last is None)
                    if last is not None:
                        xf_turned(last, 0, nxt is None)
                    weights_high(step, 1)
                    if last is not None:
                        xf_turned(last, 1)
                    h_out(step, 1)
                    if nxt is not None:
                        exp_minus_max(nxt)
                    weights_high(step, 2)
                    if after_next is not None:
                        next_guess(after_next)
                        c_an.end()
                    if after_next is not None:
                        next_normed(after_next, False)
                    h_out(step, 2)
                    if nxt is not None:
                        decay(nxt, 0)
                    h_out(step, 3)
                    if last is not None:
                        second_gate(last)
                    if after_next is not None:
                        turned(after_next, 0)
                        turned(after_next, 1)
                    h_guess(step)
                    if after_next is not None:
                        turned(after_next, 2)
                        turned(after_next, 3)
                    if nxt is not None:
                        decay(nxt, 1)
                        decay(nxt, 2)

                def epilogue(step):
                    weights_high(step, 3)
                    x1_guess(step)
                    x1_normed(step, True)
                    xf_turned(step, 0, True)
                    xf_turned(step, 1)
                    second_gate(step)

                run_steps(act, prologue, body, epilogue)

            @block.tensor
            def _(pe):
                pe.wait_ge(s_cp, 10)
                pe.wait_ge(s_const, 16 * (2 * HG + 5))
                for c in range(3 * KC):
                    ins = pe.transpose(ps_x[:, 16 * c:16 * c + 16], wraw[:, c * P:(c + 1) * P],
                                       ident[0:2 * NH, 0:2 * NH])
                ins = pe.transpose(ps_x[:, 256:256 + NE * FC], b1raw, ident[0:NE * FC, 0:NE * FC])
                ins.then_inc(s_wt, 1)

                def turn(step, j, first):
                    g = number(step)
                    pe.wait_ge(s_qn, g * SB + j + 1)
                    if not first:
                        pe.wait_ge(s_cm, (g - 1) * SB + 1)
                    for c in range(KC):
                        pe.transpose(ps_s[:, j, c * P:(c + 1) * P], normed[:, j, c * P:(c + 1) * P], ident[:, :])
                    for c in range(KC):
                        ins = pe.transpose(ps_s[:, j, (KC + c) * P:(KC + c + 1) * P],
                                           ctxb[:, j, c * P:(c + 1) * P], ident[:, :])
                    ins.then_inc(s_tq, 1)

                def gates(step, first):
                    g = number(step)
                    if not first:
                        pe.wait_ge(s_mld, g)
                    pe.wait_ge(s_cd, 1)
                    pe.wait_ge(s_ql, g * SB + SB)
                    for j in range(SB):
                        for c in range(2 * KC):
                            for n, (a, b) in enumerate(HALVES):
                                ins = pe.matmul(ps_m[:, j * 2 * NH:(j + 1) * 2 * NH], qkT[:, step[1], j, a, c, :],
                                                wg[:, b, c, :], start=(c == 0 and n == 0),
                                                stop=(c == 2 * KC - 1 and n == 2))
                    ins.then_inc(s_gt, 1)

                def log_f_sum(step):
                    g = number(step)
                    pe.wait_ge(s_ls, g + 1)
                    pe.matmul(ps_cs, tri[:, :], lsg[:, :, :].rearrange("p j h -> p (j h)"),
                              start=True, stop=True).then_inc(s_cs, 1)

                def turn_a(step):
                    g = number(step)
                    pe.wait_ge(s_a, g + 1)
                    pe.transpose(ps_aT, acol[:, step[1], :], ident[:, :]).then_inc(s_aT, 1)

                def turn_max(step):
                    g = number(step)
                    pe.wait_ge(s_run, g + 1)
                    pe.sem_inc(s_held, 1)
                    pe.transpose(ps_ab, arun[:, :], ident[0:G, 0:G]).then_inc(s_ab, 1)

                def scores(step, j):
                    g = number(step)
                    pe.wait_ge(s_cm, g * SB + j + 1)
                    for u in range(KC):
                        for n, (a, b) in enumerate(HALVES):
                            for k in range(HG):
                                r = slice(DH * k, DH * k + DH)
                                ins = pe.matmul(ps_s[:, k, u * P:(u + 1) * P], qkT[r, step[1], j, a, KC + u, :],
                                                qkT[r, step[1], j, b, u, :], start=(n == 0), stop=(n == 2))
                    ins.then_inc(s_s, 1)

                def times_v(step, j):
                    g = number(step)
                    pe.wait_ge(s_cm, g * SB + j + 2)
                    pe.wait_ge(s_hev, g * SB + j + 1)
                    for u in range(KC):
                        for k in range(HG):
                            h = u * HG + k
                            ins = pe.matmul(ps_pv[j % 2][:, h * (DH + 1):(h + 1) * (DH + 1)], E[:, j, k * KC + u, :],
                                            vaug[:, step[1], j, h, :], start=True, stop=True)
                    ins.then_inc(s_pv, 1)

                def turn_xf(step, r):
                    g = number(step)
                    pe.wait_ge(s_xf, g * SB + 2 * r + 2)
                    pe.wait_ge(s_xe, g * (SB // 2) + r + 1)
                    for j in range(2):
                        for c in range(KC):
                            ins = pe.transpose(ps_x[:, (j * KC + c) * P:(j * KC + c + 1) * P],
                                               normed[:, 2 * r + j, c * P:(c + 1) * P], ident[:, :])
                    ins.then_inc(s_xt, 1)

                def logits(step):
                    g = number(step)
                    pe.wait_ge(s_xe, g * (SB // 2) + SB // 2 + 1)
                    for j in range(SB):
                        for c in range(KC):
                            ins = pe.matmul(ps_log[:, j, :], xT[:, j, c, :], gw[:, c, :],
                                            start=(c == 0), stop=(c == KC - 1))
                    ins.then_inc(s_lg, 1)

                def ranks(step):
                    g = number(step)
                    pe.wait_ge(s_mk, g + 1)
                    chosen = mask[:, :, :].rearrange("p j e -> p (j e)")
                    pe.matmul(ps_rank, tri_s[:, :], chosen, start=True, stop=False)
                    for d in range(1, SB):
                        pe.matmul(ps_rank[:, d * NE:], ones[:, :], chosen[:, 0:(SB - d) * NE], start=False,
                                  stop=(d == SB - 1))
                    for j in range(SB):
                        ins = pe.matmul(ps_tot, ones[:, :], mask[:, j, :], start=(j == 0), stop=(j == SB - 1))
                    ins.then_inc(s_rk, 1)

                def prologue(step, nxt):
                    for j in range(SB):
                        turn(step, j, True)
                    gates(step, True)
                    for j in range(SB):
                        turn(nxt, j, True)
                    log_f_sum(step)
                    turn_a(step)
                    turn_max(step)

                def body(last, step, nxt, after_next):
                    if nxt is not None:
                        gates(nxt, False)
                    scores(step, 0)
                    scores(step, 1)
                    if nxt is not None:
                        log_f_sum(nxt)
                    times_v(step, 0)
                    if last is not None:
                        turn_xf(last, 0)
                    if nxt is not None:
                        turn_a(nxt)
                    scores(step, 2)
                    if nxt is not None:
                        turn_max(nxt)
                    if last is not None:
                        turn_xf(last, 1)
                    times_v(step, 1)
                    if last is not None:
                        logits(last)
                    scores(step, 3)
                    times_v(step, 2)
                    times_v(step, 3)
                    if after_next is not None:
                        for j in range(SB):
                            turn(after_next, j, False)
                    if last is not None:
                        ranks(last)

                def epilogue(step):
                    turn_xf(step, 0)
                    turn_xf(step, 1)
                    logits(step)
                    ranks(step)

                pe.sem_inc(s_lg, 1)
                run_steps(pe, prologue, body, epilogue)

            @block.vector
            def _(dve):
                for s, n in ((s_cm, 1), (s_hev, 1), (s_xe, 1)):
                    dve.sem_inc(s, n)
                dve.wait_ge(s_cp, 10)
                dve.wait_ge(s_wt, 1)
                c_cd = Chain(sem("dve_setup"), 0)
                c_cd.inc(dve.tensor_copy(wgr[:, :, :], ps_x[:, 0:16 * 3 * KC].rearrange("p (c o) -> p c o", c=3 * KC)))
                for a in range(2):
                    c_cd.inc(dve.tensor_copy(gbias[:, a, :].rearrange("p (k u) -> p k u", u=KC),
                                             graw[:, a, :].rearrange("p (u k) -> p k u", u=KC)))
                c_cd.inc(dve.tensor_copy(b1T[:, :, :], ps_x[:, 256:256 + NE * FC].rearrange("p (e c) -> p e c", e=NE)))
                c_cd.inc(dve.tensor_copy(revidx[:, :, :], it_rev[:, :, :]))
                c_cd.inc(dve.tensor_copy(ebase[:, :], it_base[:, :]))
                c_cd.inc(dve.tensor_copy(fill[:, :], it_base[:, :]))
                c_cd.inc(dve.tensor_copy(tok[:, :], it_tok[:, :]))
                c_cd.wait(dve)
                c_cd.link(dve, dve.tensor_tensor(wgr[:, KC:2 * KC, :], wgr[:, KC:2 * KC, :],
                                                 wgr[:, 2 * KC:3 * KC, :], ALU.add))
                c_cd.link(dve, dve.tensor_scalar(wg[:, 0, :, :], wgr[:, 0:2 * KC, :], W_SCALE, None, ALU.mult))
                c_cd.link(dve, dve.scalar_tensor_tensor(out=wg[:, 1, :, :], in0=wgr[:, 0:2 * KC, :], scalar=W_SCALE,
                                                        in1=wg[:, 0, :, :], op0=ALU.mult, op1=ALU.subtract))
                dve.sem_inc(s_cd, 1)

                def refine(c, var, y, t):
                    c.link(dve, dve.tensor_tensor(t, y, y, ALU.mult))
                    c.link(dve, dve.scalar_tensor_tensor(out=t, in0=t, scalar=-0.5, in1=var, op0=ALU.mult, op1=ALU.mult))
                    c.link(dve, dve.scalar_tensor_tensor(out=y, in0=t, scalar=1.5, in1=y, op0=ALU.add, op1=ALU.mult))

                def stats(c, src, parts, mean_var, var_eps, ready):
                    for j in range(SB):
                        c.inc(dve.bn_stats(parts[:, j, :], src[:, j, :]))
                    c.wait(dve)
                    dve.sem_inc(s_held, 1)
                    for j in range(SB):
                        c.inc(dve.bn_aggr(mean_var[:, j, :], parts[:, j, :]))
                    c.wait(dve)
                    dve.tensor_scalar(var_eps[:, :], mean_var[:, :, 1], LN_EPS, None, ALU.add).then_inc(ready, 1)

                def next_stats(step):
                    c_dn.begin(number(step))
                    dve.wait_ge(s_x, (number(step) + 1) * 16)
                    stats(c_dn, xin[:, :, :], st, mv, ve, s_ve)

                def next_norm(step):
                    g = number(step)
                    dve.wait_ge(s_rs, g + 1)
                    refine(c_dn, ve[:, :], rs[:, :], nt1[:, :])
                    dve.scalar_tensor_tensor(out=nb[:, :], in0=mv[:, :, 0], scalar=-1.0, in1=rs[:, :],
                                             op0=ALU.mult, op1=ALU.mult).then_inc(s_nb, 1)
                    c_dn.end()

                def centre_v(step):
                    ctx_h = ctxb[:, :, :].rearrange("p j (h e) -> p (j h) e", h=NH)
                    vs = vsum[:, :, :].rearrange("p j h -> p (j h)")
                    dve.tensor_reduce(vs, ctx_h, AX, ALU.add).then_inc(s_vs, 1)
                    dve.wait_ge(s_vs, number(step) + 1)
                    v = vaug[:, step[1], :, :, :].rearrange("p j h e -> p (j h) e")[:, :, 0:DH]
                    dve.scalar_tensor_tensor(out=v, in0=vs.unsqueeze(2).broadcast_to([P, G, DH]), scalar=-1.0 / DH,
                                             in1=ctx_h, op0=ALU.mult, op1=ALU.add).then_inc(s_vc, 1)

                def q_low(step, j):
                    dve.wait_ge(s_te, number(step) * SB + j + 1)
                    hi, lo = (qkT[:, step[1], j, a, :, :].rearrange("p c t -> p (c t)") for a in range(2))
                    dve.tensor_tensor(lo, ps_s[:, j, :], hi, ALU.subtract).then_inc(s_ql, 1)

                def gate_bias(step):
                    g = number(step)
                    c_dg.begin(g)
                    f = gs[:, :, 1, :]
                    dve.wait_ge(s_gt, g + 1)
                    bias = gbias[:, :, :].rearrange("p a h -> p (a h)").unsqueeze(1).broadcast_to([P, SB, 2 * NH])
                    c_dg.link(dve, dve.scalar_tensor_tensor(
                        out=gs[:, :, :, :].rearrange("p j a h -> p j (a h)"),
                        in0=ps_gate.rearrange("p j a h -> p j (a h)"), scalar=1.0 / W_SCALE, in1=bias,
                        op0=ALU.mult, op1=ALU.add))
                    dve.scalar_tensor_tensor(out=nabs[:, :, :], in0=f, scalar=-1.0, in1=f, op0=ALU.mult,
                                             op1=ALU.min).then_inc(s_na, 1)

                def log_f(step):
                    g = number(step)
                    f = gs[:, :, 1, :]
                    dve.wait_ge(s_ln, g + 1)
                    dve.scalar_tensor_tensor(out=lsg[:, :, :], in0=f, scalar=0.0, in1=lsg[:, :, :], op0=ALU.min,
                                             op1=ALU.subtract).then_inc(s_ls, 1)

                def next_a(step):
                    g = number(step)
                    dve.wait_ge(s_cs, g + 1)
                    c_dg.inc(dve.tensor_copy(csb[:, :], ps_cs))
                    dve.tensor_tensor(acol[:, step[1], :].rearrange("p (j h) -> p j h", j=SB), gs[:, :, 0, :],
                                      ps_cs.rearrange("p (j h) -> p j h", j=SB), ALU.subtract).then_inc(s_a, 1)

                def running_max(step, first):
                    g = number(step)
                    dve.wait_ge(s_aT, g + 1)
                    if not first:
                        dve.wait_ge(s_scan, g * 16)
                        dve.wait_ge(s_en, g)
                    dve.tensor_tensor_scan(arun[:, :], ps_aT, low[:, :].broadcast_to([G, P]), -3e38, ALU.max, ALU.max).then_inc(s_run, 1)

                def max_log_decay(step):
                    g = number(step)
                    dve.wait_ge(s_ab, g + 1)
                    c_dg.wait(dve)
                    dve.tensor_tensor(mld[:, :], csb[:, :], ps_ab, ALU.add).then_inc(s_mld, 1)
                    c_dg.end()

                def weights_low(step, n):
                    g, half, q = number(step), n % 2, n // 2
                    dve.wait_ge(s_hi, g * 4 + n + 1)
                    e, k = g, q
                    if half == 0:
                        hi, lo = (w1s[:, bass.ds(e, 1), a, k, :].rearrange("p a f -> p (a f)") for a in range(2))
                    else:
                        hi, lo = (w2s[:, bass.ds(e, 1), a, k * (FC // 2):(k + 1) * (FC // 2), :].rearrange("p a c d -> p (a c d)")
                                  for a in range(2))
                    dve.scalar_tensor_tensor(out=lo, in0=stage[:, half, :], scalar=W_SCALE, in1=hi, op0=ALU.mult,
                                             op1=ALU.subtract).then_inc(s_lo, 1)

                def c_of(step, j):
                    g = number(step)
                    dve.wait_ge(s_s, g * SB + j + 1)
                    dve.wait_ge(s_ee, g * SB + j + 1)
                    c = E[:, j, :, :].rearrange("p (k u) s -> p k (u s)", u=KC)
                    dve.scalar_tensor_tensor(out=c, in0=ps_s[:, :, 0:KC * P], scalar=QK_SCALE, in1=c,
                                             op0=ALU.mult, op1=ALU.mult).then_inc(s_cm, 1)

                def h_norm(step):
                    g, c = number(step), c_dh
                    c.begin(g)
                    dve.wait_ge(s_hev, g * SB + SB + 1)
                    dve.wait_ge(s_en, g + 1)
                    sq = work[:, :, :].rearrange("p j (h e) -> p (j h) e", h=NH)
                    c.inc(dve.tensor_reduce(ssq[:, :], sq, AX, ALU.add))
                    rows = Hs[:, :, :, DH]
                    c.link(dve, dve.scalar_tensor_tensor(out=nrm[:, :, :], in0=rows, scalar=-1.0, in1=rows,
                                                         op0=ALU.mult, op1=ALU.max))
                    c.link(dve, dve.tensor_tensor(nrm[:, :, :], nrm[:, :, :], en[:, step[1], :, :], ALU.max))
                    n = nrm[:, :, :].rearrange("p j h -> p (j h)")
                    c.link(dve, dve.tensor_scalar(n, n, EPS, None, ALU.add))
                    c.link(dve, dve.reciprocal(rn[:, :], n))
                    c.link(dve, dve.tensor_tensor(hv[:, :], ssq[:, :], rn[:, :], ALU.mult))
                    c.link(dve, dve.scalar_tensor_tensor(out=hv[:, :], in0=hv[:, :], scalar=1.0 / DH, in1=rn[:, :],
                                                         op0=ALU.mult, op1=ALU.mult))
                    dve.tensor_scalar(hv[:, :], hv[:, :], LN_EPS, None, ALU.add).then_inc(s_hve, 1)

                def h_scaled(step):
                    g, c = number(step), c_dh
                    sq = work[:, :, :].rearrange("p j (h e) -> p (j h) e", h=NH)
                    dve.wait_ge(s_hy, g + 1)
                    refine(c, hv[:, :], hy[:, :], ht[:, :])
                    c.link(dve, dve.tensor_tensor(hy[:, :], hy[:, :], rn[:, :], ALU.mult))
                    h = Hs[:, :, :, :].rearrange("p j h e -> p (j h) e")[:, :, 0:DH]
                    dve.tensor_tensor(sq, h, hy[:, :].unsqueeze(2).broadcast_to([P, G, DH]), ALU.mult).then_inc(s_ho, 1)
                    c.end()

                def x1_stats(step):
                    g, c = number(step), c_dl
                    c.begin(g)
                    dve.wait_ge(s_x1, g + 1)
                    stats(c, xres[:, :, :], st, mv, ve, s_ve2)

                def x1_norm(step):
                    g, c = number(step), c_dl
                    dve.wait_ge(s_rs2, g + 1)
                    dve.scalar_tensor_tensor(out=nb[:, :], in0=mv[:, :, 0], scalar=-1.0, in1=rs[:, :],
                                             op0=ALU.mult, op1=ALU.mult).then_inc(s_xb, 1)

                def wide(ap):
                    return ap.unsqueeze(2).broadcast_to([P, SB, NE])

                def choose(step):
                    g, c = number(step), c_dl
                    dve.wait_ge(s_lg, g + 2)
                    c.link(dve, dve.tensor_reduce(m1[:, :], ps_log, AX, ALU.max))
                    c.link(dve, dve.tensor_tensor(dl[:, :, :], ps_log, wide(m1[:, :]), ALU.subtract))
                    c.link(dve, dve.scalar_tensor_tensor(out=key[:, :, :], in0=dl[:, :, :], scalar=0.0,
                                                         in1=revidx[:, :, :], op0=ALU.is_equal, op1=ALU.mult))
                    c.link(dve, dve.tensor_reduce(kmax[:, :], key[:, :, :], AX, ALU.max))
                    c.link(dve, dve.tensor_tensor(oh1[:, :, :], key[:, :, :], wide(kmax[:, :]), ALU.is_equal))
                    c.link(dve, dve.scalar_tensor_tensor(out=dl2[:, :, :], in0=oh1[:, :, :], scalar=-BIG,
                                                         in1=dl[:, :, :], op0=ALU.mult, op1=ALU.add))
                    dve.tensor_reduce(m2[:, :], dl2[:, :, :], AX, ALU.max).then_inc(s_m2, 1)
                    dve.wait_ge(s_m2, g + 1)
                    c.link(dve, dve.tensor_tensor(key[:, :, :], dl2[:, :, :], wide(m2[:, :]), ALU.is_equal))
                    c.link(dve, dve.tensor_tensor(key[:, :, :], key[:, :, :], revidx[:, :, :], ALU.mult))
                    c.link(dve, dve.tensor_reduce(kmax[:, :], key[:, :, :], AX, ALU.max))
                    c.link(dve, dve.tensor_tensor(oh2[:, :, :], key[:, :, :], wide(kmax[:, :]), ALU.is_equal))
                    dve.tensor_tensor(mask[:, :, :], oh1[:, :, :], oh2[:, :, :], ALU.add).then_inc(s_mk, 1)

                def records(step):
                    g, c = number(step), c_dl
                    dve.wait_ge(s_rf, g + 1)
                    recf = rec[:, :, :, :].bitcast(F32)
                    dve.wait_ge(s_p2, g + 1)
                    c.link(dve, dve.tensor_scalar(den[:, :], p2[:, :], 1.0, None, ALU.add))
                    c.link(dve, dve.reciprocal(den[:, :], den[:, :]))
                    c.inc(dve.tensor_copy(recf[:, :, 0, 1], den[:, :]))
                    c.inc(dve.tensor_tensor(recf[:, :, 1, 1], den[:, :], p2[:, :], ALU.mult))
                    for k in range(2):
                        c.inc(dve.tensor_copy(rec[:, :, k, 0], tok[:, :]))
                    c.wait(dve)
                    dve.wait_ge(s_rk, g + 1)
                    c.inc(dve.tensor_scalar(tok[:, :], tok[:, :], float(SB * S), None, ALU.add))
                    c.link(dve, dve.tensor_tensor(rsum[:, :, :], ps_rank.rearrange("p (j e) -> p j e", j=SB),
                                                  fill[:, :].unsqueeze(1).broadcast_to([P, SB, NE]), ALU.add))
                    c.inc(dve.tensor_tensor(fill[:, :], fill[:, :], ps_tot, ALU.add))
                    for oh, t in ((oh1, tmp1), (oh2, tmp2)):
                        c.inc(dve.tensor_tensor(t[:, :, :], oh[:, :, :], rsum[:, :, :], ALU.mult))
                    c.wait(dve)
                    for k, t in enumerate((tmp1, tmp2)):
                        c.inc(dve.tensor_reduce(slotf[:, :, k], t[:, :, :], AX, ALU.add))
                    c.wait(dve)
                    dve.tensor_copy(sloti[:, :, :], slotf[:, :, :]).then_inc(s_rec, 1)
                    c.end()

                def turned_low(step):
                    for j in range(SB):
                        q_low(step, j)

                def prologue(step, nxt):
                    next_stats(step)
                    next_norm(step)
                    turned_low(step)
                    centre_v(step)
                    next_stats(nxt)
                    next_norm(nxt)
                    gate_bias(step)
                    turned_low(nxt)
                    log_f(step)
                    next_a(step)
                    running_max(step, True)
                    max_log_decay(step)

                def body(last, step, nxt, after_next):
                    if nxt is not None:
                        gate_bias(nxt)
                    c_of(step, 0)
                    if nxt is not None:
                        log_f(nxt)
                    if last is not None:
                        x1_stats(last)
                        weights_low(last, 3)
                        x1_norm(last)
                    weights_low(step, 0)
                    c_of(step, 1)
                    if nxt is not None:
                        next_a(nxt)
                        centre_v(nxt)
                    if nxt is not None:
                        running_max(nxt, False)
                    c_of(step, 2)
                    if nxt is not None:
                        max_log_decay(nxt)
                    weights_low(step, 1)
                    if after_next is not None:
                        next_stats(after_next)
                        next_norm(after_next)
                    weights_low(step, 2)
                    c_of(step, 3)
                    if last is not None:
                        choose(last)
                    h_norm(step)
                    if after_next is not None:
                        q_low(after_next, 0)
                        q_low(after_next, 1)
                    h_scaled(step)
                    if after_next is not None:
                        q_low(after_next, 2)
                        q_low(after_next, 3)
                    if last is not None:
                        records(last)

                def epilogue(step):
                    weights_low(step, 3)
                    x1_stats(step)
                    x1_norm(step)
                    choose(step)
                    records(step)

                run_steps(dve, prologue, body, epilogue)

        b2r = qkT[:, 0, :, :, :, :].rearrange("p j w c t -> p (j w c t)").bitcast(F32).rearrange(
            "p (e d) -> p e d", e=NE)
        xg = ctxb
        hf = E[:, 0:2, :, :].rearrange("p a c t -> p a (c t)")
        hh = E[:, 2:4, :, :].rearrange("p a c t -> p a (c t)").bitcast(F16).rearrange(
            "p a (w c t) -> p a w c t", w=2, c=FC)
        xh = normed[:, 0:2, :].bitcast(F16).rearrange("p a (w c t) -> p a w c t", w=2, c=KC)
        yo = work
        ps_xt = ps_t
        ps_l1 = ps_s[:, :, :].rearrange("p (a b) n -> p a b n", a=2)
        ps_y = (ps_h, ps_m)

        s_b2 = sem("b2_in")
        s_tl = sem("tiles_listed")
        s_ij = sem("tile_numbers")
        c_tl = Chain(sem("tile_list_steps"), 0)
        s_ig = [sem(f"gather_ids_in{k}") for k in range(4)]
        s_is = [sem(f"scatter_ids_in{k}") for k in range(4)]
        s_xg0 = sem("rows_cleared")
        s_gx = [sem(f"rows_in{k}") for k in range(4)]
        s_xT = sem("rows_turned")
        s_xhi = sem("rows_high")
        s_xh = sem("row_halves")
        s_l1 = sem("layer1_half")
        s_ge = sem("gelu_half")
        s_hhi = sem("gelu_high")
        s_hh = sem("gelu_halves")
        s_l2 = sem("layer2")
        s_yb = sem("rows_with_bias")
        s_y = sem("rows_gated")
        s_add = sem("rows_added")
        s_af = sem("scatter_ids_free")
        GE0, HH0, L20, Y0, FREE0 = 1, 1, 1, 4, 3

        class Turn:

            def __init__(self, i, u):
                self.i, self.u = i, u
                self.t = u if isinstance(i, int) and i == 0 else i * 4 + u

            def slot(self, ahead):
                return (self.u + ahead) % 4

            def landed(self, ahead):
                return (self.i + ((self.u + ahead) // 4 + 1)) * 16

        def run_turns(eng, turn):
            turn(Turn(0, 0), True, NT)
            with eng.Fori(0, LOOP_TURNS) as i:
                for u in range(1, 5):
                    turn(Turn(i, u), False, NT)
            for t in range(4 * LOOP_TURNS + 1, NT + 1):
                turn(Turn(0, t), False, NT - t)

        with nc.Block() as block:

            @block.sync
            def _(sp):
                sp.dma_start(b2r, b2.partition_broadcast(P)).then_inc(s_b2, 16)
                sp.wait_ge(s_tl, 2)

                def ids(tr, ahead, dst, sems, wait=None):
                    row = sp.value_load(rowi[0:1, bass.ds(tr.t + ahead, 1)], min_val=0, max_val=PAD_ROW)
                    if wait is not None:
                        wait()
                    sp.dma_start(dst[:, tr.slot(ahead), :], table[bass.ds(row, P), :])\
                      .then_inc(sems[tr.slot(ahead)], 16)

                def turn(tr, first, left):
                    if first:
                        for k in range(4):
                            ids(tr, k, ids_g, s_ig)
                        ids(tr, 0, ids_s, s_is)
                    if left > 4:
                        ids(tr, 4, ids_g, s_ig, lambda: sp.wait_ge(s_gx[tr.slot(0)], tr.landed(0)))
                    if left > 1:
                        ids(tr, 1, ids_s, s_is, None if first else
                            lambda: sp.wait_ge(s_af, tr.t + (FREE0 - 2)))

                run_turns(sp, turn)
                for n in (NT, NT + 1):
                    sp.wait_ge(s_ig[n % 4], (n // 4 + 1) * 16)

            @block.gpsimd
            def _(pool):
                pool.sem_inc(s_af, FREE0)
                pool.iota(it_j, [[1, NL]], base=0, channel_multiplier=0).then_inc(s_ij, 1)
                pool.memset(xg[:, :, :], 0.0).then_inc(s_xg0, 1)
                pool.wait_ge(s_xg0, 1)

                def gather(tr, ahead):
                    k = tr.slot(ahead)
                    pool.wait_ge(s_ig[k], tr.landed(ahead))
                    pool.sem_inc(s_held, 1)
                    pool.indirect_dma_start(xg[:, k, :], None, xf_dram,
                                            bass.IndirectOffsetOnAxis(ap=ids_g[:, k, 0:1], axis=0),
                                            bounds_check=T - 1, oob_is_err=False).then_inc(s_gx[k], 16)

                def add_rows(tr):
                    k = tr.slot(-1)
                    pool.wait_ge(s_y, tr.t + Y0)
                    pool.sem_inc(s_held, 1)
                    pool.indirect_dma_start(out_rows, bass.IndirectOffsetOnAxis(ap=ids_s[:, k, 0:1], axis=0),
                                            yo[:, k, :], None, bounds_check=T - 1, oob_is_err=False,
                                            compute_op=ALU.add).then_inc(s_add, 16)
                    pool.wait_ge(s_add, tr.t * 16)
                    pool.sem_inc(s_af, 1)

                def turn(tr, first, left):
                    if first:
                        for ahead in range(3):
                            gather(tr, ahead)
                    if left > 3:
                        if not first:
                            pool.wait_ge(s_xT, tr.t)
                        gather(tr, 3)
                    if not first:
                        add_rows(tr)

                run_turns(pool, turn)
                pool.wait_ge(s_gx[NT % 4], (NT // 4 + 1) * 16)

            @block.tensor
            def _(pe):
                def turn_rows(tr, ahead):
                    pe.wait_ge(s_gx[tr.slot(ahead)], tr.landed(ahead))
                    for c in range(KC):
                        ins = pe.transpose(ps_xt[:, c * P:(c + 1) * P], xg[:, tr.slot(ahead), c * P:(c + 1) * P],
                                           ident[:, :])
                    ins.then_inc(s_xT, 1)

                def layer1(tr, expert):
                    half = FC // 2
                    for f in range(FC):
                        o = ps_l1[:, tr.slot(0) % 2, f // half, (f % half) * P:(f % half + 1) * P]
                        parts = [(a, b, k) for a, b in ((0, 0), (0, 1), (1, 0)) for k in range(KC)]
                        for n, (a, b, k) in enumerate(parts):
                            w = w1s[:, bass.ds(expert, 1), a, k, f * P:(f + 1) * P].rearrange("p a f -> p (a f)")
                            ins = pe.matmul(o, w, xh[:, tr.slot(0) % 2, b, k, :], start=(n == 0),
                                            stop=(n == len(parts) - 1))
                        if f % half == half - 1:
                            ins.then_inc(s_l1, 1)

                def layer2(tr, expert):
                    k = tr.slot(-1)
                    for f in range(FC):
                        if f % (FC // 2) == 0:
                            pe.wait_ge(s_hh, tr.t * 2 + (f // (FC // 2) + HH0 - 1))
                        for n, (a, b) in enumerate(((0, 0), (0, 1), (1, 0))):
                            w = w2s[:, bass.ds(expert, 1), b, f, :].rearrange("p a d -> p (a d)")
                            ins = pe.matmul(ps_y[k % 2][:, 0:D], hh[:, k % 2, a, f, :], w,
                                            start=(f == 0 and n == 0), stop=(f == FC - 1 and n == 2))
                    ins.then_inc(s_l2, 1)

                pe.sem_inc(s_l2, L20)
                pe.wait_ge(s_tl, 2)

                def turn(tr, first, left):
                    if first:
                        turn_rows(tr, 0)
                    else:
                        last = pe.value_load(exi[0:1, bass.ds(tr.t - 1, 1)], min_val=0, max_val=NE - 1)
                    if left > 0:
                        expert = pe.value_load(exi[0:1, bass.ds(tr.t, 1)], min_val=0, max_val=NE - 1)
                        pe.wait_ge(s_xh, tr.t + 1)
                        if left > 1:
                            turn_rows(tr, 1)
                        if not first:
                            pe.wait_ge(s_ge, tr.t * 2 + (GE0 - 2))
                        layer1(tr, expert)
                    if not first:
                        pe.wait_ge(s_y, tr.t + (Y0 - 2))
                        layer2(tr, last)

                run_turns(pe, turn)

            @block.scalar
            def _(act):
                act.sem_inc(s_ge, GE0)
                act.wait_ge(s_tl, 2)

                def turn(tr, first, left):
                    if not left > 0:
                        return
                    expert = act.value_load(exi[0:1, bass.ds(tr.t, 1)], min_val=0, max_val=NE - 1)
                    k, w = tr.slot(0) % 2, FC // 2
                    if not first:
                        act.wait_ge(s_hh, tr.t * 2 + (HH0 - 2))
                    for half in range(2):
                        act.wait_ge(s_l1, tr.t * 2 + (half + 1))
                        for q in range(w):
                            f = half * w + q
                            ins = act.activation(hf[:, k, f * P:(f + 1) * P], ps_l1[:, k, half, q * P:(q + 1) * P],
                                                 ACT.Gelu, bias=b1T[:, bass.ds(expert, 1), f], scale=1.0 / W_SCALE)
                        ins.then_inc(s_ge, 1)

                run_turns(act, turn)

            @block.vector
            def _(dve):
                dve.sem_inc(s_y, Y0)
                dve.sem_inc(s_hh, HH0)
                one, c, NJ = slice(0, 1), c_tl, NL
                dve.wait_ge(s_ij, 1)
                c.inc(dve.tensor_copy(jf, it_j))
                c.inc(dve.memset(zer[:, :], 0.0))
                c.link(dve, dve.tensor_tensor(cntf[:, :], fill[one, :], ebase[one, :], ALU.subtract))
                c.link(dve, dve.tensor_scalar(cnti[:, :], cntf[:, :], float(P - 1), None, ALU.add))
                c.link(dve, dve.tensor_scalar(cnti[:, :], cnti[:, :], P.bit_length() - 1, None,
                                              ALU.logical_shift_right))
                c.link(dve, dve.tensor_copy(ntf[:, :], cnti[:, :]))
                c.link(dve, dve.tensor_tensor_scan(endf[:, :], ntf[:, :], zer[:, :], 0.0, ALU.add, ALU.add))
                jw = jf[:, :].unsqueeze(2).broadcast_to([1, NJ, NE])
                ew = endf[:, :].unsqueeze(1).broadcast_to([1, NJ, NE])
                nw = ntf[:, :].unsqueeze(1).broadcast_to([1, NJ, NE])
                c.link(dve, dve.tensor_tensor(cmpf[:, :, :], jw, ew, ALU.is_ge))
                c.link(dve, dve.tensor_reduce(exf[:, :], cmpf[:, :, :], AX, ALU.add))
                c.link(dve, dve.tensor_tensor(cmpf[:, :, :], cmpf[:, :, :], nw, ALU.mult))
                c.link(dve, dve.tensor_reduce(pastf[:, :], cmpf[:, :, :], AX, ALU.add))
                c.link(dve, dve.tensor_tensor(rowf[:, :], jf[:, :], pastf[:, :], ALU.subtract))
                c.link(dve, dve.tensor_scalar(pastf[:, :], exf[:, :], float(NE), float(P), ALU.is_lt, ALU.mult))
                c.link(dve, dve.tensor_tensor(rowf[:, :], rowf[:, :], pastf[:, :], ALU.mult))
                c.link(dve, dve.scalar_tensor_tensor(out=rowf[:, :], in0=exf[:, :], scalar=float(T), in1=rowf[:, :],
                                                     op0=ALU.mult, op1=ALU.add))
                dve.tensor_copy(rowi[:, :], rowf[:, :]).then_inc(s_tl, 1)
                dve.tensor_scalar(exi[:, :], exf[:, :], float(NE - 1), None, ALU.min).then_inc(s_tl, 1)
                dve.wait_ge(s_tl, 2)
                dve.wait_ge(s_b2, 16)

                def split_rows(tr, ahead):
                    dve.wait_ge(s_xT, tr.t + (ahead + 1))
                    src = ps_xt[:, 0:D].rearrange("p (c t) -> p c t", c=KC)
                    hi, lo = (xh[:, tr.slot(ahead) % 2, w, :, :] for w in range(2))
                    dve.tensor_copy(hi, src).then_inc(s_xhi, 1)
                    dve.wait_ge(s_xhi, tr.t + (ahead + 1))
                    dve.tensor_tensor(lo, src, hi, ALU.subtract).then_inc(s_xh, 1)

                def split_gelu(tr, half):
                    w, k = FC // 2, tr.slot(0) % 2
                    dve.wait_ge(s_ge, tr.t * 2 + (half + 1 + GE0))
                    src = hf[:, k, half * w * P:(half + 1) * w * P].rearrange("p (c t) -> p c t", c=w)
                    hi, lo = (hh[:, k, a, half * w:(half + 1) * w, :] for a in range(2))
                    dve.tensor_copy(hi, src).then_inc(s_hhi, 1)
                    dve.wait_ge(s_hhi, tr.t * 2 + (half + 1))
                    dve.tensor_tensor(lo, src, hi, ALU.subtract).then_inc(s_hh, 1)

                def gate_rows(tr, expert):
                    k = tr.slot(-1)
                    dve.wait_ge(s_is[k], tr.landed(-1))
                    dve.wait_ge(s_l2, tr.t + L20)
                    dve.scalar_tensor_tensor(
                        out=yo[:, k, :], in0=ps_y[k % 2][:, 0:D], scalar=1.0 / W_SCALE,
                        in1=b2r[:, bass.ds(expert, 1), :].rearrange("p a d -> p (a d)"), op0=ALU.mult,
                        op1=ALU.add).then_inc(s_yb, 1)
                    dve.wait_ge(s_yb, tr.t)
                    dve.tensor_scalar(yo[:, k, :], yo[:, k, :], ids_s[:, k, 1:2].bitcast(F32), None,
                                      ALU.mult).then_inc(s_y, 1)

                def turn(tr, first, left):
                    if first:
                        split_rows(tr, 0)
                    else:
                        expert = dve.value_load(exi[0:1, bass.ds(tr.t - 1, 1)], min_val=0, max_val=NE - 1)
                    if left > 1:
                        if not first:
                            dve.wait_ge(s_l1, tr.t * 2)
                        split_rows(tr, 1)
                    if left > 0:
                        if not first:
                            dve.wait_ge(s_l2, tr.t + (L20 - 1))
                        split_gelu(tr, 0)
                        split_gelu(tr, 1)
                    if not first:
                        gate_rows(tr, expert)

                run_turns(dve, turn)


_INS = ["x", "ctx_1024", "L0_xattn_igate_w", "L0_xattn_igate_b", "L0_xattn_fgate_w", "L0_xattn_fgate_b",
        "L0_xattn_out_w", "L0_ffn_gate_w", "L0_ffn_w1", "L0_ffn_b1", "L0_ffn_w2", "L0_ffn_b2"]


def kernel(**inputs):
    import numpy as np
    import concourse.bacc as bacc
    from concourse.bass_utils import run_bass_kernel_spmd

    nc = bacc.Bacc("TRN2", target_bir_lowering=False, num_devices=1)
    arrays, args = {}, []
    for name in _INS:
        a = np.ascontiguousarray(inputs[name])
        arrays[f"in_{name}"] = a
        args.append(nc.dram_tensor(f"in_{name}", a.shape, mybir.dt.from_np(a.dtype), kind="ExternalInput").ap())
    shape = arrays["in_x"].shape
    args.append(nc.dram_tensor("out_rows", shape, F32, kind="ExternalOutput").ap())
    build(nc, *args)
    r = run_bass_kernel_spmd(nc, [arrays], core_ids=[0])
    return r.results[0]["out_rows"]
```

```python
from contextlib import ExitStack

import concourse.bass as bass
from concourse import mybir

ALU = mybir.AluOpType
ACT = mybir.ActivationFunctionType
AX = mybir.AxisListType.X
F32 = mybir.dt.float32
F16 = mybir.dt.float16
BF16 = mybir.dt.bfloat16
I32 = mybir.dt.int32

P = 128
R = 2 * P
EPS = 1e-6
LN_EPS = 1e-5
BIG = 1e30
W_SCALE = 64.0


class Chain:

    def __init__(self, sem, per_step):
        self.sem, self.per_step, self.base, self.n = sem, per_step, 0, 0

    def begin(self, step):
        self.base, self.n = step * self.per_step, 0

    def inc(self, ins):
        self.n += 1
        ins.then_inc(self.sem, 1)

    def wait(self, eng):
        eng.wait_ge(self.sem, self.base + self.n)

    def link(self, eng, ins):
        self.inc(ins)
        self.wait(eng)

    def end(self):
        assert self.n == self.per_step, (self.n, self.per_step)


def build(nc, x, ctx_in, igate_w, igate_b, fgate_w, fgate_b, out_w, gate_w, w1, b1, w2, b2, out):
    NB, S, D = x.shape
    NH = igate_b.shape[0]
    DH = D // NH
    HG = P // DH
    KC = D // P
    NE, _, F = w1.shape
    FC = F // P
    SB = 4
    NSTEP = NB // SB
    T = NB * S
    G = SB * NH
    QK_SCALE = float(DH) ** -0.5
    assert S == P and D == KC * P and NH == KC * HG and NSTEP % 2 == 0
    NT = (2 * T + NE * (R - 1)) // R
    NBIG = max((2 * T - k * (P + 1)) // R + k for k in range(NE + 1))
    NV = 2 * NE
    PAD_ROW = NE * T
    TABLE = NE * T + R
    TB = TABLE // P
    LOOP_TURNS = (NBIG - 3) // 4

    HALVES = ((0, 0), (0, 1), (1, 0))

    DVE_NEXT, DVE_GATES, DVE_HERE, DVE_LAST, ACT_NEXT, ACT_HERE, ACT_LAST = 11, 2, 11, 31, 1, 1, 1

    xs_dram = x.rearrange("(g j) s d -> g s j d", j=SB)
    ctx_dram = ctx_in.rearrange("(g j) s d -> g s j d", j=SB)
    out_dram = out.rearrange("(g j) s d -> g s j d", j=SB)
    out_rows = out.rearrange("b s d -> (b s) d")
    xf_dram = nc.dram_tensor("xf_rows", (T, D), F32, kind="Internal").ap()
    xf_step = xf_dram.rearrange("(g j s) d -> g s j d", j=SB, s=S)
    scan_dram = nc.dram_tensor("scan_rows", (NSTEP, G, P), F32, kind="Internal").ap()
    table = nc.dram_tensor("expert_table", (TABLE, 2), I32, kind="Internal").ap()
    w1_dram = w1.rearrange("e (k p) f -> (e k) p f", p=P)
    w2_dram = w2.rearrange("e (h c p) d -> (e h) p c d", h=2, p=P)
    NPIECE = NE * 4
    PW = 1024
    assert NPIECE == NB and F == PW and FC * D == 2 * PW

    with ExitStack() as ctx:
        def sb(name, shape, dt=F32):
            return ctx.enter_context(nc.sbuf_tensor(name, shape, dt))

        def sem(name):
            return ctx.enter_context(nc.semaphore(name))

        w1s = sb("w1_halves", [P, NE, 2, KC, F], F16)
        w2s = sb("w2_halves", [P, NE, 2, FC, D], F16)
        xbuf = sb("x_slots", [P, 2, SB, D])
        xin = xbuf[:, 0, :, :]
        xres = xbuf[:, 1, :, :]
        ctxb = sb("ctx_slots", [P, SB, D])
        normed = sb("normed", [P, SB, D])
        vaug = sb("v_centred_and_one", [P, 2, SB, NH, DH + 1])
        qkT = sb("q_and_k_halves", [P, 2, SB, 2, 2 * KC, P], F16)
        E = sb("decay_slots", [P, SB, NH, P])
        Hs = sb("h_slots", [P, SB, NH, DH + 1])
        work = sb("work", [P, SB, D])
        stage = sb("weight_stage", [P, 2, PW])
        ident = sb("ident", [P, P])
        tri = sb("tri", [P, P])
        tri_s = sb("tri_strict", [P, P], BF16)
        ones = sb("ones", [P, P], BF16)
        low = sb("low", [G, 1])
        outw = sb("out_w_rows", [P, D])
        gbias = sb("gate_bias_rows", [P, 2, NH])
        wraw = E[0:2 * NH, 0, :, :].rearrange("p a c -> p (a c)")[:, 0:3 * D]
        wgr = E[:, 2, 0, 0:6 * KC * NH].rearrange("p (c o) -> p c o", c=3 * KC)
        graw = E[:, 3, 0, 0:2 * NH].rearrange("p (a h) -> p a h", a=2)
        b1raw = E[0:NE * FC, 1, 0, :]
        gwr = E[:, 3, 1, 0:KC * NE].rearrange("p (k e) -> p k e", k=KC)
        wg = sb("gate_w_halves", [P, 2, 2 * KC, 2 * NH], F16)
        gw = sb("router_w_halves", [P, 2, KC, NE], F16)
        b1T = sb("b1_turned", [P, NE, FC])
        revidx = sb("rev_index", [P, SB, NE])
        ebase = sb("expert_base", [P, NE])
        tok = sb("token_ids", [P, SB])
        h_flat = sb("routing_work", [P, 5 * SB * NE])
        dl, key, oh1, oh2, dl2 = (
            h_flat[:, n * SB * NE:(n + 1) * SB * NE].rearrange("p (j e) -> p j e", j=SB) for n in range(5))
        rsum, tmp1, tmp2 = dl, key, dl2
        it_rev, it_base, it_tok = dl.bitcast(I32), key[:, 0, :].bitcast(I32), oh1[:, 0, 0:SB].bitcast(I32)
        v_flat = vaug[0:1, :, :, :, :].rearrange("p a j h e -> p (a j h e)")
        exf, pastf, rowf, jf, it_j, rowi, exi, lastf = (v_flat[:, n * NT:(n + 1) * NT] for n in range(8))
        it_j, rowi, exi = (a.bitcast(I32) for a in (it_j, rowi, exi))
        xT = ctxb[:, :, :].rearrange("p j d -> p (j d)").bitcast(F16).rearrange(
            "p (w j c t) -> p w j c t", w=2, j=SB, c=KC)
        b2r = qkT[:, 0, :, :, :, :].rearrange("p j w c t -> p (j w c t)").bitcast(F32).rearrange(
            "p (e d) -> p e d", e=NE)
        st = sb("bn_parts", [P, SB, 6])
        mv = sb("mean_var", [P, SB, 2])
        ve = sb("var_eps", [P, SB])
        lnv = sb("ln_var", [P, SB])
        rs = sb("rstd", [P, SB])
        nt1 = sb("newton", [P, SB])
        nb = sb("minus_mean_rstd", [P, SB])
        vsum = sb("v_sum", [P, SB, NH])
        gs = sb("gates", [P, SB, 2, NH])
        nabs = sb("minus_abs_f", [P, SB, NH])
        ex1 = sb("exp_f", [P, SB, NH])
        lsg = sb("log_sigmoid", [P, SB, NH])
        csb = sb("log_f_sum", [P, G])
        acol = sb("i_minus_sum", [P, 2, G])
        arun = sb("running_max", [G, P])
        mld = sb("max_log_d", [P, G])
        en = sb("exp_minus_max", [P, 2, SB, NH])
        ssq = sb("square_sum", [P, G])
        nrm = sb("normalizer", [P, SB, NH])
        rn = sb("one_over_norm", [P, G])
        hv = sb("h_var", [P, G])
        hln = ssq
        ht = nabs[:, :, :].rearrange("p j h -> p (j h)")
        hy = sb("h_rstd", [P, G])
        m1 = sb("top1", [P, SB])
        kmax = sb("key_max", [P, SB])
        m2 = sb("top2", [P, SB])
        mask = sb("chosen", [P, SB, NE], BF16)
        p2 = sb("exp_top2", [P, SB])
        den = sb("gate_sum", [P, SB])
        slotf = sb("slot_f", [P, SB, 2])
        sloti = sb("slot_i", [P, SB, 2], I32)
        rec = sb("record", [P, SB, 2, 2], I32)
        fill = sb("expert_fill", [P, NE])
        ids_g = sb("ids_for_gather", [P, 4, R // P, 2], I32)
        ids_s = sb("ids_for_scatter", [P, 4, R // P, 2], I32)
        ntf, zer, endf, basef, deltaf, cntf, totf, cnti, toti = (
            v_flat[:, 8 * NT + n * (NV + 1):8 * NT + (n + 1) * (NV + 1)] for n in range(9))
        cnti, toti = cnti.bitcast(I32), toti.bitcast(I32)
        cmpf = Hs[0:1, :, :, :].rearrange("p j h e -> p (j h e)")[:, 0:NT * NV].rearrange(
            "p (t v) -> p t v", v=NV)

        ps_s = ctx.enter_context(nc.psum_tensor("scores", [P, HG, 512], F32))
        ps_h = ctx.enter_context(nc.psum_tensor("pv", [P, 512], F32))
        ps_m = ctx.enter_context(nc.psum_tensor("gate_bank", [P, 512], F32))
        ps_x = ctx.enter_context(nc.psum_tensor("route_bank", [P, 512], F32))
        ps_t = ctx.enter_context(nc.psum_tensor("pv_odd", [P, 512], F32))
        ps_pv = (ps_h, ps_t)
        ps_gate = ps_m[:, 0:G * 2].rearrange("p (j a h) -> p j a h", j=SB, a=2)
        ps_cs = ps_m[:, 64:64 + G]
        ps_aT = ps_m[0:G, 128:128 + P]
        ps_ab = ps_m[:, 256:256 + G]
        ps_log = ps_x[:, 0:SB * NE].rearrange("p (j e) -> p j e", j=SB)
        ps_rank = ps_x[:, 64:64 + SB * NE]
        ps_tot = ps_x[:, 128:128 + NE]

        s_held = sem("held")
        s_const = sem("const_in")
        s_b2 = sem("b2_in")
        s_tl = sem("tiles_listed")
        s_ij = sem("tile_numbers")
        c_tl = Chain(sem("tile_list_steps"), 0)
        s_c0 = sem("zeroed")
        s_cp = sem("pool_consts")
        s_tab0 = sem("table_fill")
        s_tab = sem("table_written")
        s_wt = sem("gate_w_transposed")
        s_cd = sem("dve_consts")
        s_x = sem("x_in")
        s_xr = sem("x_residual_in")
        s_ctx = sem("ctx_in")
        s_w = [sem(f"weights_in{p}") for p in range(2)]
        s_hi = sem("weights_high")
        s_lo = sem("weights_low")
        c_dn = Chain(sem("dve_next"), DVE_NEXT)
        c_dh = Chain(sem("dve_here"), DVE_HERE)
        c_an = Chain(sem("act_next"), ACT_NEXT)
        c_ah = Chain(sem("act_here"), ACT_HERE)
        c_dl = Chain(sem("dve_last"), DVE_LAST)
        c_al = Chain(sem("act_last"), ACT_LAST)
        c_ax = Chain(sem("act_log_f"), 1)
        c_dg = Chain(sem("dve_gates"), DVE_GATES)
        s_ve = sem("var_ready")
        s_rs = sem("rstd_guess")
        s_nb = sem("q_scale_ready")
        s_vs = sem("v_summed")
        s_xb = sem("xf_scale_ready")
        s_ho = sem("h_scaled")
        s_hw = sem("h_weighted")
        s_qn = sem("q_normed")
        s_vc = sem("v_ready")
        s_tq = sem("qk_turned")
        s_te = sem("qk_high")
        s_ql = sem("qk_halves")
        s_gt = sem("gates_summed")
        s_na = sem("f_abs_ready")
        s_ln = sem("ln_ready")
        s_ls = sem("log_sigmoid_ready")
        s_cs = sem("log_f_summed")
        s_a = sem("a_ready")
        s_aT = sem("a_turned")
        s_run = sem("running_max_ready")
        s_ab = sem("running_max_turned")
        s_mld = sem("max_log_d_ready")
        s_en = sem("exp_minus_max_ready")
        s_scan = sem("scan_written")
        s_e = [sem(f"running_max_in{j}") for j in range(SB)]
        s_em = sem("masked")
        s_ee = sem("decay_ready")
        s_s = sem("scores_ready")
        s_cm = sem("c_ready")
        s_pv = sem("pv_ready")
        s_hev = sem("h_in_sbuf")
        s_hve = sem("h_var_ready")
        s_hy = sem("h_rstd_guess")
        s_ve2 = sem("var2_ready")
        s_rs2 = sem("rstd2_guess")
        s_x1 = sem("x1_ready")
        s_xf = sem("xf_ready")
        s_xo = sem("x1_written")
        s_xfo = sem("xf_written")
        s_xt = sem("xf_turned")
        s_xe = sem("xf_high")
        s_xl = sem("xf_halves")
        s_lg = sem("logits_ready")
        s_m2 = sem("top2_ready")
        s_p2 = sem("exp_top2_ready")
        s_mk = sem("chosen_ready")
        s_rk = sem("rank_ready")
        s_rec = sem("records_ready")
        s_sc = sem("table_scattered")
        s_rf = sem("records_free")

        def number(step):
            return step[0] * 2 + step[1]

        def run_steps(eng, prologue, body, epilogue):
            end = NSTEP // 2 - 1
            prologue((0, 0), (0, 1))
            body(None, (0, 0), (0, 1), (1, 0))
            with eng.Fori(0, end - 1) as i:
                body((i, 0), (i, 1), (i + 1, 0), (i + 1, 1))
                body((i, 1), (i + 1, 0), (i + 1, 1), (i + 2, 0))
            body((end - 1, 0), (end - 1, 1), (end, 0), (end, 1))
            body((end - 1, 1), (end, 0), (end, 1), None)
            body((end, 0), (end, 1), None, None)
            epilogue((end, 1))

        with nc.Block() as block:

            @block.sync
            def _(sp):
                sp.dma_start(xin[:, :, :], xs_dram[0]).then_inc(s_x, 16)
                sp.dma_start(ctxb[:, :, :], ctx_dram[0]).then_inc(s_ctx, 16)
                sp.dma_start(xres[:, :, :], xs_dram[0]).then_inc(s_xr, 16)
                sp.dma_start(gwr, gate_w.rearrange("(k p) e -> p k e", p=P)).then_inc(s_const, 16)
                sp.dma_start(outw[:, :], out_w.partition_broadcast(P)).then_inc(s_const, 16)
                for a, gate in ((0, igate_b), (1, fgate_b)):
                    sp.dma_start(graw[:, a, :], gate.partition_broadcast(P)).then_inc(s_const, 16)
                sp.wait_ge(s_tab0, 2)
                sp.sem_inc(s_held, 1)
                sp.dma_start(table.rearrange("(p n) w -> p n w", p=P),
                             stage[:, 0, 0:2 * TB].bitcast(I32).rearrange("p (n w) -> p n w", w=2)).then_inc(s_tab, 16)
                sp.wait_ge(s_tab, 16)

                def weights(n_half, half):
                    src = (w1_dram, w2_dram)[half]
                    dst = stage[:, half, :]
                    if half:
                        dst = dst.rearrange("p (c d) -> p c d", d=D)
                    sp.dma_start(dst, src[n_half]).then_inc(s_w[half], 16)

                def write_scan(step):
                    g = number(step)
                    sp.wait_ge(s_run, g + 1)
                    sp.sem_inc(s_held, 1)
                    sp.dma_start(scan_dram[g], arun[:, :]).then_inc(s_scan, 16)

                def read_scan(step, free, places):
                    g = number(step)
                    sp.wait_ge(s_scan, (g + 1) * 16)
                    sp.sem_inc(s_held, 1)
                    for j in places:
                        if free:
                            sp.wait_ge(s_pv, g * SB + (j + 1 - SB))
                        sp.sem_inc(s_held, 1)
                        sp.dma_start(E[:, j, :, :],
                                     scan_dram[g, j * NH:j * NH + NH, :].partition_broadcast(P)).then_inc(s_e[j], 16)

                def load_x(step):
                    g = number(step)
                    sp.wait_ge(s_qn, g * SB)
                    sp.sem_inc(s_held, 1)
                    sp.dma_start(xin[:, :, :], xs_dram[g]).then_inc(s_x, 16)

                def load_ctx(step, first):
                    g = number(step)
                    sp.wait_ge(s_tq, g * SB)
                    sp.sem_inc(s_held, 1)
                    sp.wait_ge(s_vc, g)
                    sp.sem_inc(s_held, 1)
                    if not first:
                        sp.wait_ge(s_lg, g - 1)
                    sp.sem_inc(s_held, 1)
                    sp.dma_start(ctxb[:, :, :], ctx_dram[g]).then_inc(s_ctx, 16)

                def write_xf(step):
                    g = number(step)
                    sp.wait_ge(s_xf, (g + 1) * SB)
                    sp.sem_inc(s_held, 1)
                    sp.dma_start(xf_step[g], normed[:, :, :]).then_inc(s_xfo, 16)

                def write_x1(step):
                    g = number(step)
                    sp.wait_ge(s_x1, g + 1)
                    sp.sem_inc(s_held, 1)
                    sp.dma_start(out_dram[g], xres[:, :, :]).then_inc(s_xo, 16)

                def prologue(step, nxt):
                    weights(0, 0)
                    weights(0, 1)
                    load_x(nxt)
                    load_ctx(nxt, True)
                    write_scan(step)
                    read_scan(step, False, range(SB))
                    load_x((1, 0))

                def body(last, step, nxt, after_next):
                    g = number(step)
                    if last is not None:
                        write_xf(last)
                        sp.wait_ge(s_xo, g * 16)
                        sp.sem_inc(s_held, 1)
                        sp.dma_start(xres[:, :, :], xs_dram[g]).then_inc(s_xr, 16)
                    if nxt is not None:
                        write_scan(nxt)
                        read_scan(nxt, True, range(1))
                    if last is not None:
                        sp.wait_ge(s_lo, g * SB)
                        sp.sem_inc(s_held, 1)
                        weights(g * 2, 1)
                    if nxt is not None:
                        read_scan(nxt, True, range(1, 2))
                    if after_next is not None:
                        load_ctx(after_next, False)
                    sp.wait_ge(s_lo, g * SB + 1)
                    sp.sem_inc(s_held, 1)
                    weights(g * 2 + 1, 0)
                    if nxt is not None:
                        read_scan(nxt, True, range(2, 3))
                    sp.wait_ge(s_lo, g * SB + 2)
                    sp.sem_inc(s_held, 1)
                    weights(g * 2 + 1, 1)
                    if nxt is not None:
                        read_scan(nxt, True, range(3, SB))
                        sp.wait_ge(s_lo, g * SB + 3)
                        sp.sem_inc(s_held, 1)
                        weights(g * 2 + 2, 0)
                    write_x1(step)
                    if after_next is not None and not (isinstance(g, int) and g + 3 == NSTEP):
                        load_x((after_next[0] + after_next[1], 1 - after_next[1]))

                run_steps(sp, prologue, body, write_xf)
                sp.wait_ge(s_s, (NSTEP - 1) * SB)
                sp.dma_start(b2r, b2.partition_broadcast(P)).then_inc(s_b2, 16)
                sp.wait_ge(s_xo, 16 * NSTEP)
                sp.wait_ge(s_xfo, 16 * (NSTEP + 1))

            @block.gpsimd
            def _(pool):
                pool.sem_inc(s_rf, 1)
                pool.sem_inc(s_xfo, 16)
                tab0 = stage[:, 0, 0:2 * TB].rearrange("p (n w) -> p n w", w=2)
                pool.iota(tab0[:, :, 0:1].bitcast(I32), [[0, TB]], base=T, channel_multiplier=0).then_inc(s_tab0, 1)
                pool.memset(tab0[:, :, 1:2], 0.0).then_inc(s_tab0, 1)
                pool.memset(ident[:, :], 0.0).then_inc(s_c0, 1)
                pool.memset(tri[:, :], 1.0).then_inc(s_c0, 1)
                pool.memset(tri_s[:, :], 1.0).then_inc(s_c0, 1)
                pool.wait_ge(s_c0, 3)
                pool.affine_select(out=ident[:, :], in_=ident[:, :], compare_op=ALU.not_equal, fill=1.0,
                                   base=0, pattern=[[-1, P]], channel_multiplier=1).then_inc(s_cp, 1)
                pool.affine_select(out=tri[:, :], in_=tri[:, :], compare_op=ALU.is_ge, fill=0.0,
                                   base=0, pattern=[[1, P]], channel_multiplier=-1).then_inc(s_cp, 1)
                pool.affine_select(out=tri_s[:, :], in_=tri_s[:, :], compare_op=ALU.is_ge, fill=0.0,
                                   base=-1, pattern=[[1, P]], channel_multiplier=-1).then_inc(s_cp, 1)
                pool.memset(ones[:, :], 1.0).then_inc(s_cp, 1)
                pool.memset(low[:, :], -3e38).then_inc(s_cp, 1)
                for p in range(2):
                    pool.memset(vaug[:, p, :, :, DH:DH + 1], 1.0).then_inc(s_cp, 1)
                pool.iota(it_rev[:, :, :], [[0, SB], [-1, NE]], base=NE, channel_multiplier=0).then_inc(s_cp, 1)
                pool.iota(it_base[:, :], [[T, NE]], base=0, channel_multiplier=0).then_inc(s_cp, 1)
                pool.iota(it_tok[:, :], [[S, SB]], base=0, channel_multiplier=1).then_inc(s_cp, 1)
                pool.wait_ge(s_tab, 16)

                big = pool.to_reg(BIG)

                def masks(step):
                    g = number(step)
                    for j in range(SB):
                        pool.wait_ge(s_e[j], (g + 1) * 16)
                        pool.sem_inc(s_held, 1)
                        pool.affine_select(out=E[:, j, :, :], in_=E[:, j, :, :], compare_op=ALU.is_ge, fill=big,
                                           base=0, pattern=[[0, NH], [1, P]], channel_multiplier=-1).then_inc(s_em, 1)

                def prologue(step, nxt):
                    masks(step)

                def x1_of(step):
                    g = number(step)
                    pool.wait_ge(s_ho, g + 1)
                    pool.sem_inc(s_held, 1)
                    pool.tensor_tensor(work[:, :, :], work[:, :, :],
                                       outw[:, :].unsqueeze(1).broadcast_to([P, SB, D]), ALU.mult).then_inc(s_hw, 1)
                    pool.wait_ge(s_hw, g + 1)
                    pool.wait_ge(s_xr, (g + 1) * 16)
                    pool.sem_inc(s_held, 1)
                    pool.tensor_tensor(xres[:, :, :], xres[:, :, :], work[:, :, :], ALU.add).then_inc(s_x1, 1)

                def scatter(step):
                    g = number(step)
                    pool.wait_ge(s_rec, g + 1)
                    pool.sem_inc(s_held, 1)
                    for j in range(SB):
                        for k in range(2):
                            pool.indirect_dma_start(
                                table, bass.IndirectOffsetOnAxis(ap=sloti[:, j, k:k + 1], axis=0),
                                rec[:, j, k, :], None, bounds_check=TABLE - 1,
                                oob_is_err=False).then_inc(s_sc, 16)
                    pool.wait_ge(s_sc, (g + 1) * (2 * SB * 16))
                    pool.sem_inc(s_rf, 1)

                def body(last, step, nxt, after_next):
                    if nxt is not None:
                        masks(nxt)
                        x1_of(step)
                    if last is not None:
                        scatter(last)

                def epilogue(step):
                    pool.wait_ge(s_pv, NSTEP * SB)
                    pool.iota(it_j, [[1, NT]], base=0, channel_multiplier=0).then_inc(s_ij, 1)
                    scatter(step)

                run_steps(pool, prologue, body, epilogue)

            @block.scalar
            def _(act):
                act.preload_act_table_set("natural_log_exp_and_others")
                for o, gate in ((0, igate_w), (NH, fgate_w)):
                    for r in range(HG):
                        act.dma_start(wraw[o + KC * r:o + KC * r + KC, :], gate[r::HG, :]).then_inc(s_const, 16)
                act.dma_start(b1raw, b1.rearrange("e (c p) -> (e c) p", p=P)).then_inc(s_const, 16)

                def rsqrt_guess(var, ln, y, chain, ready, done, count):
                    act.wait_ge(ready, count)
                    chain.link(act, act.activation(ln, var, ACT.Ln))
                    act.activation(y, ln, ACT.Exp, scale=-0.5).then_inc(done, 1)

                def next_guess(step):
                    c_an.begin(number(step))
                    rsqrt_guess(ve[:, :], lnv[:, :], rs[:, :], c_an, s_ve, s_rs, number(step) + 1)

                def normalize(src, done):
                    for j in range(SB):
                        act.activation(normed[:, j, :], src[:, j, :], ACT.Identity, scale=rs[:, j:j + 1],
                                       bias=nb[:, j:j + 1]).then_inc(done, 1)

                def next_normed(step, first):
                    g = number(step)
                    act.wait_ge(s_nb, g + 1)
                    if not first:
                        act.wait_ge(s_xfo, (g - 1) * 16)
                        act.wait_ge(s_lg, g - 1)
                    act.wait_ge(s_ctx, (g + 1) * 16)
                    normalize(xin, s_qn)

                def x1_normed(step, last):
                    g = number(step)
                    act.wait_ge(s_xb, g + 1)
                    if not last:
                        act.wait_ge(s_tq, (g + 3) * SB)
                    normalize(xres, s_xf)

                def turned(step, j):
                    g = number(step)
                    act.wait_ge(s_tq, g * SB + j + 1)
                    act.activation(qkT[:, step[1], j, 0, :, :].rearrange("p c t -> p (c t)"), ps_s[:, j, :],
                                   ACT.Copy).then_inc(s_te, 1)

                def log_sigmoid(step):
                    g = number(step)
                    act.wait_ge(s_na, g + 1)
                    c_ax.begin(g)
                    c_ax.link(act, act.activation(ex1[:, :, :], nabs[:, :, :], ACT.Exp))
                    act.activation(lsg[:, :, :], ex1[:, :, :], ACT.Ln, bias=1.0).then_inc(s_ln, 1)
                    c_ax.end()

                def exp_minus_max(step):
                    g = number(step)
                    act.wait_ge(s_mld, g + 1)
                    for j in range(SB):
                        ins = act.activation(
                            en[:, step[1], j, :].rearrange("p (u k) -> p k u", u=KC),
                            mld[:, j * NH:(j + 1) * NH].rearrange("p (k u) -> p k u", u=KC), ACT.Exp, scale=-1.0)
                    ins.then_inc(s_en, 1)

                def decay(step, j):
                    g = number(step)
                    act.wait_ge(s_em, g * SB + j + 1)
                    act.wait_ge(s_a, g + 1)
                    for c in range(NH):
                        ins = act.activation(E[:, j, c, :], E[:, j, c, :], ACT.Exp, scale=-1.0,
                                             bias=acol[:, step[1], j * NH + c:j * NH + c + 1])
                    ins.then_inc(s_ee, 1)

                def weights_high(step, n):
                    g, half, q = number(step), n % 2, n // 2
                    act.wait_ge(s_w[half], (g * 2 + (q + 1)) * 16)
                    if half == 0:
                        dst = w1s[:, bass.ds(g, 1), 0, q, :].rearrange("p a f -> p (a f)")
                    else:
                        dst = w2s[:, bass.ds(g, 1), 0, q * (FC // 2):(q + 1) * (FC // 2), :].rearrange(
                            "p a c d -> p (a c d)")
                    act.activation(dst, stage[:, half, :], ACT.Copy, scale=W_SCALE).then_inc(s_hi, 1)

                def h_out(step, j, first=False):
                    g = number(step)
                    act.wait_ge(s_pv, g * SB + j + 1)
                    if j == 0 and not first:
                        act.wait_ge(s_x1, g)
                    h = ps_pv[j % 2][:, 0:NH * (DH + 1)].rearrange("p (h e) -> p h e", h=NH)
                    act.activation(Hs[:, j, :, :], h, ACT.Copy)
                    act.activation(work[:, j, :].rearrange("p (h e) -> p h e", h=NH), h[:, :, 0:DH],
                                   ACT.Square).then_inc(s_hev, 1)

                def h_guess(step):
                    c_ah.begin(number(step))
                    rsqrt_guess(hv[:, :], hln[:, :], hy[:, :], c_ah, s_hve, s_hy, number(step) + 1)
                    c_ah.end()

                def x1_guess(step):
                    c_al.begin(number(step))
                    rsqrt_guess(ve[:, :], lnv[:, :], rs[:, :], c_al, s_ve2, s_rs2, number(step) + 1)
                    c_al.end()

                def xf_turned(step, r, last=False):
                    g = number(step)
                    vc = NSTEP if last else g + 3
                    act.wait_ge(s_xt, g * (SB // 2) + r + 1)
                    if r == 0:
                        act.wait_ge(s_vc, vc)
                    act.activation(xT[:, 0, 2 * r:2 * r + 2, :, :].rearrange("p j c t -> p (j c t)"), ps_x[:, :],
                                   ACT.Copy).then_inc(s_xe, 1)

                def second_gate(step):
                    act.wait_ge(s_m2, number(step) + 1)
                    act.activation(p2[:, :], m2[:, :], ACT.Exp, scale=1.0 / W_SCALE).then_inc(s_p2, 1)

                def prologue(step, nxt):
                    next_guess(step)
                    c_an.end()
                    next_normed(step, True)
                    for j in range(SB):
                        turned(step, j)
                    log_sigmoid(step)
                    next_guess(nxt)
                    c_an.end()
                    next_normed(nxt, True)
                    exp_minus_max(step)
                    for j in range(SB):
                        turned(nxt, j)
                    for j in range(SB - 2):
                        decay(step, j)

                def body(last, step, nxt, after_next):
                    if nxt is not None:
                        log_sigmoid(nxt)
                    if last is not None:
                        weights_high(last, 3)
                    weights_high(step, 0)
                    if last is not None:
                        x1_guess(last)
                        x1_normed(last, nxt is None)
                    decay(step, 2)
                    h_out(step, 0, last is None)
                    if last is not None:
                        xf_turned(last, 0, nxt is None)
                    decay(step, 3)
                    if last is not None:
                        xf_turned(last, 1)
                    h_out(step, 1)
                    if nxt is not None:
                        exp_minus_max(nxt)
                    if after_next is not None:
                        next_guess(after_next)
                        c_an.end()
                    weights_high(step, 1)
                    if after_next is not None:
                        next_normed(after_next, False)
                    h_out(step, 2)
                    weights_high(step, 2)
                    h_out(step, 3)
                    if last is not None:
                        second_gate(last)
                    if after_next is not None:
                        turned(after_next, 0)
                        turned(after_next, 1)
                    h_guess(step)
                    if after_next is not None:
                        turned(after_next, 2)
                        turned(after_next, 3)
                    if nxt is not None:
                        decay(nxt, 0)
                        decay(nxt, 1)

                def epilogue(step):
                    weights_high(step, 3)
                    x1_guess(step)
                    x1_normed(step, True)
                    xf_turned(step, 0, True)
                    xf_turned(step, 1)
                    second_gate(step)

                run_steps(act, prologue, body, epilogue)

            @block.tensor
            def _(pe):
                pe.wait_ge(s_cp, 10)
                def turn(step, j, first):
                    g = number(step)
                    pe.wait_ge(s_qn, g * SB + j + 1)
                    if not first:
                        pe.wait_ge(s_cm, (g - 1) * SB + 1)
                    for c in range(KC):
                        pe.transpose(ps_s[:, j, c * P:(c + 1) * P], normed[:, j, c * P:(c + 1) * P], ident[:, :])
                    for c in range(KC):
                        ins = pe.transpose(ps_s[:, j, (KC + c) * P:(KC + c + 1) * P],
                                           ctxb[:, j, c * P:(c + 1) * P], ident[:, :])
                    ins.then_inc(s_tq, 1)

                def gates(step, first):
                    g = number(step)
                    if not first:
                        pe.wait_ge(s_mld, g)
                    pe.wait_ge(s_cd, 1)
                    pe.wait_ge(s_ql, g * SB + SB)
                    for j in range(SB):
                        for c in range(2 * KC):
                            for n, (a, b) in enumerate(HALVES):
                                ins = pe.matmul(ps_m[:, j * 2 * NH:(j + 1) * 2 * NH], qkT[:, step[1], j, a, c, :],
                                                wg[:, b, c, :], start=(c == 0 and n == 0),
                                                stop=(c == 2 * KC - 1 and n == 2))
                    ins.then_inc(s_gt, 1)

                def log_f_sum(step):
                    g = number(step)
                    pe.wait_ge(s_ls, g + 1)
                    pe.matmul(ps_cs, tri[:, :], lsg[:, :, :].rearrange("p j h -> p (j h)"),
                              start=True, stop=True).then_inc(s_cs, 1)

                def turn_a(step):
                    g = number(step)
                    pe.wait_ge(s_a, g + 1)
                    pe.transpose(ps_aT, acol[:, step[1], :], ident[:, :]).then_inc(s_aT, 1)

                def turn_max(step):
                    g = number(step)
                    pe.wait_ge(s_run, g + 1)
                    pe.sem_inc(s_held, 1)
                    pe.transpose(ps_ab, arun[:, :], ident[0:G, 0:G]).then_inc(s_ab, 1)

                def scores(step, j):
                    g = number(step)
                    pe.wait_ge(s_cm, g * SB + j + 1)
                    for u in range(KC):
                        for n, (a, b) in enumerate(HALVES):
                            for k in range(HG):
                                r = slice(DH * k, DH * k + DH)
                                ins = pe.matmul(ps_s[:, k, u * P:(u + 1) * P], qkT[r, step[1], j, a, KC + u, :],
                                                qkT[r, step[1], j, b, u, :], start=(n == 0), stop=(n == 2))
                    ins.then_inc(s_s, 1)

                def times_v(step, j):
                    g = number(step)
                    pe.wait_ge(s_cm, g * SB + j + 2)
                    pe.wait_ge(s_hev, g * SB + j + 1)
                    for u in range(KC):
                        for k in range(HG):
                            h = u * HG + k
                            ins = pe.matmul(ps_pv[j % 2][:, h * (DH + 1):(h + 1) * (DH + 1)], E[:, j, k * KC + u, :],
                                            vaug[:, step[1], j, h, :], start=True, stop=True)
                    ins.then_inc(s_pv, 1)

                def turn_xf(step, r):
                    g = number(step)
                    pe.wait_ge(s_xf, g * SB + 2 * r + 2)
                    pe.wait_ge(s_xl, g * (SB // 2) + r + 1)
                    for j in range(2):
                        for c in range(KC):
                            ins = pe.transpose(ps_x[:, (j * KC + c) * P:(j * KC + c + 1) * P],
                                               normed[:, 2 * r + j, c * P:(c + 1) * P], ident[:, :])
                    ins.then_inc(s_xt, 1)

                def logits(step):
                    g = number(step)
                    pe.wait_ge(s_xl, g * (SB // 2) + SB // 2 + 1)
                    for j in range(SB):
                        for c in range(KC):
                            for n, (a, b) in enumerate(HALVES):
                                ins = pe.matmul(ps_log[:, j, :], xT[:, a, j, c, :], gw[:, b, c, :],
                                                start=(c == 0 and n == 0), stop=(c == KC - 1 and n == 2))
                    ins.then_inc(s_lg, 1)

                def ranks(step):
                    g = number(step)
                    pe.wait_ge(s_mk, g + 1)
                    chosen = mask[:, :, :].rearrange("p j e -> p (j e)")
                    pe.matmul(ps_rank, tri_s[:, :], chosen, start=True, stop=False)
                    for d in range(1, SB):
                        pe.matmul(ps_rank[:, d * NE:], ones[:, :], chosen[:, 0:(SB - d) * NE], start=False,
                                  stop=(d == SB - 1))
                    for j in range(SB):
                        ins = pe.matmul(ps_tot, ones[:, :], mask[:, j, :], start=(j == 0), stop=(j == SB - 1))
                    ins.then_inc(s_rk, 1)

                def turn_weights():
                    pe.wait_ge(s_const, 16 * (2 * HG + 5))
                    for c in range(3 * KC):
                        ins = pe.transpose(ps_x[:, 16 * c:16 * c + 16], wraw[:, c * P:(c + 1) * P],
                                           ident[0:2 * NH, 0:2 * NH])
                    ins = pe.transpose(ps_x[:, 256:256 + NE * FC], b1raw, ident[0:NE * FC, 0:NE * FC])
                    ins.then_inc(s_wt, 1)

                def prologue(step, nxt):
                    for j in range(SB):
                        turn(step, j, True)
                    turn_weights()
                    gates(step, True)
                    log_f_sum(step)
                    turn_a(step)
                    turn_max(step)
                    for j in range(SB):
                        turn(nxt, j, True)

                def body(last, step, nxt, after_next):
                    if nxt is not None:
                        gates(nxt, False)
                    scores(step, 0)
                    scores(step, 1)
                    if nxt is not None:
                        log_f_sum(nxt)
                    times_v(step, 0)
                    if last is not None:
                        turn_xf(last, 0)
                    if nxt is not None:
                        turn_a(nxt)
                    scores(step, 2)
                    if nxt is not None:
                        turn_max(nxt)
                    if last is not None:
                        turn_xf(last, 1)
                    times_v(step, 1)
                    if last is not None:
                        logits(last)
                    scores(step, 3)
                    times_v(step, 2)
                    times_v(step, 3)
                    if after_next is not None:
                        for j in range(SB):
                            turn(after_next, j, False)
                    if last is not None:
                        ranks(last)

                def epilogue(step):
                    turn_xf(step, 0)
                    turn_xf(step, 1)
                    logits(step)
                    ranks(step)

                pe.sem_inc(s_lg, 1)
                run_steps(pe, prologue, body, epilogue)

            @block.vector
            def _(dve):
                for s, n in ((s_cm, 1), (s_hev, 2), (s_xl, 1)):
                    dve.sem_inc(s, n)
                dve.wait_ge(s_cp, 10)
                def refine(c, var, y, t):
                    c.link(dve, dve.tensor_tensor(t, y, y, ALU.mult))
                    c.link(dve, dve.scalar_tensor_tensor(out=t, in0=t, scalar=-0.5, in1=var, op0=ALU.mult, op1=ALU.mult))
                    c.link(dve, dve.scalar_tensor_tensor(out=y, in0=t, scalar=1.5, in1=y, op0=ALU.add, op1=ALU.mult))

                def stats(c, src, parts, mean_var, var_eps, ready):
                    for j in range(SB):
                        c.inc(dve.bn_stats(parts[:, j, :], src[:, j, :]))
                    c.wait(dve)
                    dve.sem_inc(s_held, 1)
                    for j in range(SB):
                        c.inc(dve.bn_aggr(mean_var[:, j, :], parts[:, j, :]))
                    c.wait(dve)
                    dve.tensor_scalar(var_eps[:, :], mean_var[:, :, 1], LN_EPS, None, ALU.add).then_inc(ready, 1)

                def next_stats(step):
                    c_dn.begin(number(step))
                    dve.wait_ge(s_x, (number(step) + 1) * 16)
                    stats(c_dn, xin[:, :, :], st, mv, ve, s_ve)

                def next_norm(step):
                    g = number(step)
                    dve.wait_ge(s_rs, g + 1)
                    refine(c_dn, ve[:, :], rs[:, :], nt1[:, :])
                    dve.scalar_tensor_tensor(out=nb[:, :], in0=mv[:, :, 0], scalar=-1.0, in1=rs[:, :],
                                             op0=ALU.mult, op1=ALU.mult).then_inc(s_nb, 1)
                    c_dn.end()

                def centre_v(step):
                    ctx_h = ctxb[:, :, :].rearrange("p j (h e) -> p (j h) e", h=NH)
                    vs = vsum[:, :, :].rearrange("p j h -> p (j h)")
                    dve.wait_ge(s_ctx, (number(step) + 1) * 16)
                    dve.tensor_reduce(vs, ctx_h, AX, ALU.add).then_inc(s_vs, 1)
                    dve.wait_ge(s_vs, number(step) + 1)
                    v = vaug[:, step[1], :, :, :].rearrange("p j h e -> p (j h) e")[:, :, 0:DH]
                    dve.scalar_tensor_tensor(out=v, in0=vs.unsqueeze(2).broadcast_to([P, G, DH]), scalar=-1.0 / DH,
                                             in1=ctx_h, op0=ALU.mult, op1=ALU.add).then_inc(s_vc, 1)

                def q_low(step, j):
                    dve.wait_ge(s_te, number(step) * SB + j + 1)
                    hi, lo = (qkT[:, step[1], j, a, :, :].rearrange("p c t -> p (c t)") for a in range(2))
                    dve.tensor_tensor(lo, ps_s[:, j, :], hi, ALU.subtract).then_inc(s_ql, 1)

                def gate_bias(step):
                    g = number(step)
                    c_dg.begin(g)
                    f = gs[:, :, 1, :]
                    dve.wait_ge(s_gt, g + 1)
                    bias = gbias[:, :, :].rearrange("p a h -> p (a h)").unsqueeze(1).broadcast_to([P, SB, 2 * NH])
                    c_dg.link(dve, dve.scalar_tensor_tensor(
                        out=gs[:, :, :, :].rearrange("p j a h -> p j (a h)"),
                        in0=ps_gate.rearrange("p j a h -> p j (a h)"), scalar=1.0 / W_SCALE, in1=bias,
                        op0=ALU.mult, op1=ALU.add))
                    dve.scalar_tensor_tensor(out=nabs[:, :, :], in0=f, scalar=-1.0, in1=f, op0=ALU.mult,
                                             op1=ALU.min).then_inc(s_na, 1)

                def log_f(step):
                    g = number(step)
                    f = gs[:, :, 1, :]
                    dve.wait_ge(s_ln, g + 1)
                    dve.scalar_tensor_tensor(out=lsg[:, :, :], in0=f, scalar=0.0, in1=lsg[:, :, :], op0=ALU.min,
                                             op1=ALU.subtract).then_inc(s_ls, 1)

                def next_a(step):
                    g = number(step)
                    dve.wait_ge(s_cs, g + 1)
                    c_dg.inc(dve.tensor_copy(csb[:, :], ps_cs))
                    dve.tensor_tensor(acol[:, step[1], :].rearrange("p (j h) -> p j h", j=SB), gs[:, :, 0, :],
                                      ps_cs.rearrange("p (j h) -> p j h", j=SB), ALU.subtract).then_inc(s_a, 1)

                def running_max(step, first):
                    g = number(step)
                    dve.wait_ge(s_aT, g + 1)
                    if not first:
                        dve.wait_ge(s_scan, g * 16)
                        dve.wait_ge(s_en, g)
                    dve.tensor_tensor_scan(arun[:, :], ps_aT, low[:, :].broadcast_to([G, P]), -3e38, ALU.max, ALU.max).then_inc(s_run, 1)

                def max_log_decay(step):
                    g = number(step)
                    dve.wait_ge(s_ab, g + 1)
                    c_dg.wait(dve)
                    dve.tensor_tensor(mld[:, :], csb[:, :], ps_ab, ALU.add).then_inc(s_mld, 1)
                    c_dg.end()

                def weights_low(step, n):
                    g, half, q = number(step), n % 2, n // 2
                    dve.wait_ge(s_hi, g * 4 + n + 1)
                    e, k = g, q
                    if half == 0:
                        hi, lo = (w1s[:, bass.ds(e, 1), a, k, :].rearrange("p a f -> p (a f)") for a in range(2))
                    else:
                        hi, lo = (w2s[:, bass.ds(e, 1), a, k * (FC // 2):(k + 1) * (FC // 2), :].rearrange("p a c d -> p (a c d)")
                                  for a in range(2))
                    dve.scalar_tensor_tensor(out=lo, in0=stage[:, half, :], scalar=W_SCALE, in1=hi, op0=ALU.mult,
                                             op1=ALU.subtract).then_inc(s_lo, 1)

                def c_of(step, j):
                    g = number(step)
                    dve.wait_ge(s_s, g * SB + j + 1)
                    dve.wait_ge(s_ee, g * SB + j + 1)
                    c = E[:, j, :, :].rearrange("p (k u) s -> p k (u s)", u=KC)
                    dve.scalar_tensor_tensor(out=c, in0=ps_s[:, :, 0:KC * P], scalar=QK_SCALE, in1=c,
                                             op0=ALU.mult, op1=ALU.mult).then_inc(s_cm, 1)

                def h_norm(step):
                    g, c = number(step), c_dh
                    c.begin(g)
                    dve.wait_ge(s_hev, g * SB + SB + 2)
                    dve.wait_ge(s_en, g + 1)
                    sq = work[:, :, :].rearrange("p j (h e) -> p (j h) e", h=NH)
                    c.inc(dve.tensor_reduce(ssq[:, :], sq, AX, ALU.add))
                    rows = Hs[:, :, :, DH]
                    c.link(dve, dve.scalar_tensor_tensor(out=nrm[:, :, :], in0=rows, scalar=-1.0, in1=rows,
                                                         op0=ALU.mult, op1=ALU.max))
                    c.link(dve, dve.tensor_tensor(nrm[:, :, :], nrm[:, :, :], en[:, step[1], :, :], ALU.max))
                    n = nrm[:, :, :].rearrange("p j h -> p (j h)")
                    c.link(dve, dve.tensor_scalar(n, n, EPS, None, ALU.add))
                    c.link(dve, dve.reciprocal(rn[:, :], n))
                    c.link(dve, dve.tensor_tensor(hv[:, :], ssq[:, :], rn[:, :], ALU.mult))
                    c.link(dve, dve.scalar_tensor_tensor(out=hv[:, :], in0=hv[:, :], scalar=1.0 / DH, in1=rn[:, :],
                                                         op0=ALU.mult, op1=ALU.mult))
                    dve.tensor_scalar(hv[:, :], hv[:, :], LN_EPS, None, ALU.add).then_inc(s_hve, 1)

                def h_scaled(step, last):
                    g, c = number(step), c_dh
                    sq = work[:, :, :].rearrange("p j (h e) -> p (j h) e", h=NH)
                    dve.wait_ge(s_hy, g + 1)
                    refine(c, hv[:, :], hy[:, :], ht[:, :])
                    c.link(dve, dve.tensor_tensor(hy[:, :], hy[:, :], rn[:, :], ALU.mult))
                    h = Hs[:, :, :, :].rearrange("p j h e -> p (j h) e")[:, :, 0:DH]
                    dve.tensor_tensor(sq, h, hy[:, :].unsqueeze(2).broadcast_to([P, G, DH]), ALU.mult).then_inc(s_ho, 1)
                    if last:
                        dve.wait_ge(s_ho, g + 1)
                        dve.tensor_tensor(work[:, :, :], work[:, :, :],
                                          outw[:, :].unsqueeze(1).broadcast_to([P, SB, D]), ALU.mult).then_inc(s_hw, 1)
                        dve.wait_ge(s_hw, g + 1)
                        dve.wait_ge(s_xr, (g + 1) * 16)
                        dve.tensor_tensor(xres[:, :, :], xres[:, :, :], work[:, :, :], ALU.add).then_inc(s_x1, 1)
                    c.end()

                def x1_stats(step):
                    g, c = number(step), c_dl
                    c.begin(g)
                    dve.wait_ge(s_x1, g + 1)
                    stats(c, xres[:, :, :], st, mv, ve, s_ve2)

                def x1_norm(step):
                    g, c = number(step), c_dl
                    dve.wait_ge(s_rs2, g + 1)
                    dve.scalar_tensor_tensor(out=nb[:, :], in0=mv[:, :, 0], scalar=-1.0, in1=rs[:, :],
                                             op0=ALU.mult, op1=ALU.mult).then_inc(s_xb, 1)

                def wide(ap):
                    return ap.unsqueeze(2).broadcast_to([P, SB, NE])

                def xf_low(step, r):
                    dve.wait_ge(s_xe, number(step) * (SB // 2) + r + 1)
                    hi, lo = (xT[:, a, 2 * r:2 * r + 2, :, :].rearrange("p j c t -> p (j c t)") for a in range(2))
                    dve.tensor_tensor(lo, ps_x[:, :], hi, ALU.subtract).then_inc(s_xl, 1)

                def choose(step):
                    g, c = number(step), c_dl
                    dve.wait_ge(s_lg, g + 2)
                    c.link(dve, dve.tensor_reduce(m1[:, :], ps_log, AX, ALU.max))
                    c.link(dve, dve.tensor_tensor(dl[:, :, :], ps_log, wide(m1[:, :]), ALU.subtract))
                    c.link(dve, dve.scalar_tensor_tensor(out=key[:, :, :], in0=dl[:, :, :], scalar=0.0,
                                                         in1=revidx[:, :, :], op0=ALU.is_equal, op1=ALU.mult))
                    c.link(dve, dve.tensor_reduce(kmax[:, :], key[:, :, :], AX, ALU.max))
                    c.link(dve, dve.tensor_tensor(oh1[:, :, :], key[:, :, :], wide(kmax[:, :]), ALU.is_equal))
                    c.link(dve, dve.scalar_tensor_tensor(out=dl2[:, :, :], in0=oh1[:, :, :], scalar=-BIG,
                                                         in1=dl[:, :, :], op0=ALU.mult, op1=ALU.add))
                    dve.tensor_reduce(m2[:, :], dl2[:, :, :], AX, ALU.max).then_inc(s_m2, 1)
                    dve.wait_ge(s_m2, g + 1)
                    c.link(dve, dve.tensor_tensor(key[:, :, :], dl2[:, :, :], wide(m2[:, :]), ALU.is_equal))
                    c.link(dve, dve.tensor_tensor(key[:, :, :], key[:, :, :], revidx[:, :, :], ALU.mult))
                    c.link(dve, dve.tensor_reduce(kmax[:, :], key[:, :, :], AX, ALU.max))
                    c.link(dve, dve.tensor_tensor(oh2[:, :, :], key[:, :, :], wide(kmax[:, :]), ALU.is_equal))
                    dve.tensor_tensor(mask[:, :, :], oh1[:, :, :], oh2[:, :, :], ALU.add).then_inc(s_mk, 1)

                def records(step):
                    g, c = number(step), c_dl
                    dve.wait_ge(s_rf, g + 1)
                    recf = rec[:, :, :, :].bitcast(F32)
                    dve.wait_ge(s_p2, g + 1)
                    c.link(dve, dve.tensor_scalar(den[:, :], p2[:, :], 1.0, None, ALU.add))
                    c.link(dve, dve.reciprocal(den[:, :], den[:, :]))
                    c.inc(dve.tensor_copy(recf[:, :, 0, 1], den[:, :]))
                    c.inc(dve.tensor_tensor(recf[:, :, 1, 1], den[:, :], p2[:, :], ALU.mult))
                    for k in range(2):
                        c.inc(dve.tensor_copy(rec[:, :, k, 0], tok[:, :]))
                    c.wait(dve)
                    dve.wait_ge(s_rk, g + 1)
                    c.inc(dve.tensor_scalar(tok[:, :], tok[:, :], float(SB * S), None, ALU.add))
                    c.link(dve, dve.tensor_tensor(rsum[:, :, :], ps_rank.rearrange("p (j e) -> p j e", j=SB),
                                                  fill[:, :].unsqueeze(1).broadcast_to([P, SB, NE]), ALU.add))
                    c.inc(dve.tensor_tensor(fill[:, :], fill[:, :], ps_tot, ALU.add))
                    for oh, t in ((oh1, tmp1), (oh2, tmp2)):
                        c.inc(dve.tensor_tensor(t[:, :, :], oh[:, :, :], rsum[:, :, :], ALU.mult))
                    c.wait(dve)
                    for k, t in enumerate((tmp1, tmp2)):
                        c.inc(dve.tensor_reduce(slotf[:, :, k], t[:, :, :], AX, ALU.add))
                    c.wait(dve)
                    dve.tensor_copy(sloti[:, :, :], slotf[:, :, :]).then_inc(s_rec, 1)
                    c.end()

                def turned_low(step):
                    for j in range(SB):
                        q_low(step, j)

                def constants():
                    dve.wait_ge(s_wt, 1)
                    c_cd = Chain(sem("dve_setup"), 0)
                    c_cd.inc(dve.tensor_copy(wgr[:, :, :], ps_x[:, 0:16 * 3 * KC].rearrange("p (c o) -> p c o", c=3 * KC)))
                    for a in range(2):
                        c_cd.inc(dve.tensor_copy(gbias[:, a, :].rearrange("p (k u) -> p k u", u=KC),
                                                 graw[:, a, :].rearrange("p (u k) -> p k u", u=KC)))
                    c_cd.inc(dve.tensor_copy(b1T[:, :, :], ps_x[:, 256:256 + NE * FC].rearrange("p (e c) -> p e c", e=NE)))
                    c_cd.inc(dve.tensor_copy(revidx[:, :, :], it_rev[:, :, :]))
                    c_cd.inc(dve.tensor_copy(ebase[:, :], it_base[:, :]))
                    c_cd.inc(dve.tensor_copy(fill[:, :], it_base[:, :]))
                    c_cd.inc(dve.tensor_copy(tok[:, :], it_tok[:, :]))
                    c_cd.wait(dve)
                    c_cd.link(dve, dve.tensor_tensor(wgr[:, KC:2 * KC, :], wgr[:, KC:2 * KC, :],
                                                     wgr[:, 2 * KC:3 * KC, :], ALU.add))
                    c_cd.link(dve, dve.tensor_scalar(wg[:, 0, :, :], wgr[:, 0:2 * KC, :], W_SCALE, None, ALU.mult))
                    c_cd.link(dve, dve.scalar_tensor_tensor(out=wg[:, 1, :, :], in0=wgr[:, 0:2 * KC, :], scalar=W_SCALE,
                                                            in1=wg[:, 0, :, :], op0=ALU.mult, op1=ALU.subtract))
                    c_cd.link(dve, dve.tensor_scalar(gw[:, 0, :, :], gwr, W_SCALE, None, ALU.mult))
                    c_cd.link(dve, dve.scalar_tensor_tensor(out=gw[:, 1, :, :], in0=gwr, scalar=W_SCALE,
                                                            in1=gw[:, 0, :, :], op0=ALU.mult, op1=ALU.subtract))
                    dve.sem_inc(s_cd, 1)

                def prologue(step, nxt):
                    next_stats(step)
                    next_norm(step)
                    centre_v(step)
                    turned_low(step)
                    constants()
                    gate_bias(step)
                    next_stats(nxt)
                    log_f(step)
                    next_a(step)
                    next_norm(nxt)
                    running_max(step, True)
                    max_log_decay(step)
                    turned_low(nxt)

                def body(last, step, nxt, after_next):
                    if nxt is not None:
                        gate_bias(nxt)
                    c_of(step, 0)
                    if nxt is not None:
                        log_f(nxt)
                    if last is not None:
                        x1_stats(last)
                        weights_low(last, 3)
                        x1_norm(last)
                    weights_low(step, 0)
                    c_of(step, 1)
                    if nxt is not None:
                        next_a(nxt)
                        centre_v(nxt)
                    if nxt is not None:
                        running_max(nxt, False)
                    if last is not None:
                        xf_low(last, 0)
                    c_of(step, 2)
                    if nxt is not None:
                        max_log_decay(nxt)
                    if last is not None:
                        xf_low(last, 1)
                    if after_next is not None:
                        next_stats(after_next)
                        next_norm(after_next)
                    weights_low(step, 1)
                    c_of(step, 3)
                    if last is not None:
                        choose(last)
                    weights_low(step, 2)
                    h_norm(step)
                    if after_next is not None:
                        turned_low(after_next)
                    h_scaled(step, nxt is None)
                    if last is not None:
                        records(last)

                def epilogue(step):
                    weights_low(step, 3)
                    x1_stats(step)
                    x1_norm(step)
                    xf_low(step, 0)
                    xf_low(step, 1)
                    choose(step)
                    records(step)

                run_steps(dve, prologue, body, epilogue)

                one, c = slice(0, 1), c_tl
                big, small = slice(0, NE), slice(NE, NV)
                dve.wait_ge(s_ij, 1)
                c.inc(dve.tensor_copy(jf, it_j))
                c.inc(dve.memset(zer, 0.0))
                c.link(dve, dve.tensor_tensor(cntf[:, big], fill[one, :], ebase[one, :], ALU.subtract))
                c.link(dve, dve.tensor_scalar(cnti[:, big], cntf[:, big], float(P - 1), None, ALU.add))
                c.inc(dve.tensor_scalar(toti[:, big], cnti[:, big], P.bit_length() - 1, None,
                                        ALU.logical_shift_right))
                c.link(dve, dve.tensor_scalar(toti[:, small], cnti[:, big], R.bit_length() - 1, None,
                                              ALU.logical_shift_right))
                c.inc(dve.tensor_copy(ntf[:, big], toti[:, small]))
                c.link(dve, dve.tensor_copy(totf[:, big], toti[:, big]))
                c.inc(dve.scalar_tensor_tensor(out=ntf[:, small], in0=ntf[:, big], scalar=-2.0, in1=totf[:, big],
                                               op0=ALU.mult, op1=ALU.add))
                c.inc(dve.tensor_copy(basef[:, big], ebase[one, :]))
                c.inc(dve.scalar_tensor_tensor(out=basef[:, small], in0=ntf[:, big], scalar=float(R),
                                               in1=ebase[one, :], op0=ALU.mult, op1=ALU.add))
                c.link(dve, dve.memset(basef[:, NV:NV + 1], float(PAD_ROW)))
                c.inc(dve.tensor_tensor(deltaf[:, 0:NV], basef[:, 1:NV + 1], basef[:, 0:NV], ALU.subtract))
                c.link(dve, dve.tensor_tensor_scan(endf[:, 0:NV], ntf[:, 0:NV], zer[:, 0:NV], 0.0, ALU.add, ALU.add))
                jw = jf[:, :].unsqueeze(2).broadcast_to([1, NT, NV])
                ew, nw, dw = (a[:, 0:NV].unsqueeze(1).broadcast_to([1, NT, NV]) for a in (endf, ntf, deltaf))
                wide_t = ctxb[0:1, :, :].rearrange("p j d -> p (j d)")[:, 0:NT * NV].rearrange("p (t v) -> p t v", v=NV)
                c.link(dve, dve.tensor_tensor(cmpf[:, :, :], jw, ew, ALU.is_ge))
                c.inc(dve.tensor_tensor(wide_t, cmpf[:, :, :], nw, ALU.mult))
                c.link(dve, dve.tensor_reduce(exf[:, :], cmpf[:, :, :], AX, ALU.add))
                c.link(dve, dve.tensor_reduce(pastf[:, :], wide_t, AX, ALU.add))
                c.link(dve, dve.tensor_tensor(cmpf[:, :, :], cmpf[:, :, :], dw, ALU.mult))
                c.inc(dve.tensor_reduce(rowf[:, :], cmpf[:, :, :], AX, ALU.add))
                c.inc(dve.tensor_tensor(jf[:, :], jf[:, :], pastf[:, :], ALU.subtract))
                c.link(dve, dve.tensor_scalar(lastf[:, :], exf[:, :], float(NV), float(R), ALU.is_lt, ALU.mult))
                c.inc(dve.tensor_scalar(pastf[:, :], exf[:, :], float(NE), float(-NE), ALU.is_ge, ALU.mult))
                c.link(dve, dve.tensor_tensor(jf[:, :], jf[:, :], lastf[:, :], ALU.mult))
                dve.tensor_tensor(rowi[:, :], rowf[:, :], jf[:, :], ALU.add).then_inc(s_tl, 1)
                c.link(dve, dve.tensor_tensor(exf[:, :], exf[:, :], pastf[:, :], ALU.add))
                dve.tensor_scalar(exi[:, :], exf[:, :], float(NE - 1), None, ALU.min).then_inc(s_tl, 1)

        xg = xbuf[:, :, :, :].rearrange("p a (q b) d -> p (a q) b d", q=2)
        hf = E[:, 0:2, :, :].rearrange("p a c t -> p (a c t)")
        hh = [x.rearrange("p (w c t) -> p w c t", w=2, c=FC) for x in (
            E[:, 2:4, :, :].rearrange("p a c t -> p (a c t)").bitcast(F16),
            qkT[:, 1, :, :, :, :].rearrange("p j w c t -> p (j w c t)"))]
        xh = normed[:, :, :].rearrange("p (a b) d -> p a (b d)", a=2).bitcast(F16).rearrange(
            "p a (w c t) -> p a w c t", w=2, c=KC)
        yo = [x[:, 2 * b:2 * b + 2, :] for x in (ctxb, work) for b in range(2)]
        ps_xt = ps_t
        ps_y = (ps_h, ps_m)
        FQ = FC // 4

        s_ig = [sem(f"gather_ids_in{k}") for k in range(4)]
        s_is = [sem(f"scatter_ids_in{k}") for k in range(4)]
        s_gx = [sem(f"rows_in{k}") for k in range(4)]
        s_xT = sem("rows_turned")
        s_xhi = sem("rows_high")
        s_xh = sem("row_halves")
        s_l1 = sem("layer1_quarter")
        s_ge = sem("gelu_quarter")
        s_hhi = sem("gelu_high")
        s_hh = sem("gelu_halves")
        s_l2 = sem("layer2")
        s_yb = sem("rows_with_bias")
        s_y = sem("rows_gated")
        s_add = sem("rows_added")
        s_af = sem("scatter_ids_free")
        L20, Y0, FREE0 = 1, 4, 3

        class Turn:

            def __init__(self, i, u):
                self.i, self.u = i, u
                self.t = u if isinstance(i, int) and i == 0 else i * 4 + u

            def rows(self, ahead):
                return P if isinstance(self.t, int) and self.t + ahead >= NBIG else R

            def slot(self, ahead):
                return (self.u + ahead) % 4

            def landed(self, ahead, dmas=1):
                return (self.i + ((self.u + ahead) // 4 + 1)) * (16 * dmas)

        def run_turns(eng, turn):
            turn(Turn(0, 0), True, NT)
            with eng.Fori(0, LOOP_TURNS) as i:
                for u in range(1, 5):
                    turn(Turn(i, u), False, NT)
            for t in range(4 * LOOP_TURNS + 1, NT + 1):
                turn(Turn(0, t), False, NT - t)

        with nc.Block() as block:

            @block.sync
            def _(sp):
                sp.wait_ge(s_tl, 2)

                def ids(tr, ahead, dst, sems, wait=None):
                    row = sp.value_load(rowi[0:1, bass.ds(tr.t + ahead, 1)], min_val=0, max_val=PAD_ROW)
                    if wait is not None:
                        wait()
                    sp.dma_start(dst[:, tr.slot(ahead), :, :],
                                 table[bass.ds(row, R), :].rearrange("(b p) w -> p b w", p=P))\
                      .then_inc(sems[tr.slot(ahead)], 16)

                def turn(tr, first, left):
                    if first:
                        for k in range(4):
                            ids(tr, k, ids_g, s_ig)
                        ids(tr, 0, ids_s, s_is)
                    if left > 4:
                        ids(tr, 4, ids_g, s_ig, lambda: sp.wait_ge(s_gx[tr.slot(0)], tr.landed(0, 2)))
                    if left > 1:
                        ids(tr, 1, ids_s, s_is, None if first else
                            lambda: sp.wait_ge(s_af, tr.t + (FREE0 - 2)))

                run_turns(sp, turn)

            @block.gpsimd
            def _(pool):
                pool.sem_inc(s_af, FREE0)

                def gather(tr, ahead):
                    k = tr.slot(ahead)
                    pool.wait_ge(s_ig[k], tr.landed(ahead))
                    pool.sem_inc(s_held, 1)
                    for b in range(R // P):
                        pool.indirect_dma_start(xg[:, k, b, :], None, xf_dram,
                                                bass.IndirectOffsetOnAxis(ap=ids_g[:, k, b, 0:1], axis=0),
                                                bounds_check=T - 1, oob_is_err=False).then_inc(s_gx[k], 16)

                def add_rows(tr):
                    k = tr.slot(-1)
                    for b in range(R // P):
                        pool.wait_ge(s_y, tr.t * 2 + (Y0 - 1 + b))
                        pool.sem_inc(s_held, 1)
                        pool.indirect_dma_start(out_rows, bass.IndirectOffsetOnAxis(ap=ids_s[:, k, b, 0:1], axis=0),
                                                yo[k][:, b, :], None, bounds_check=T - 1, oob_is_err=False,
                                                compute_op=ALU.add).then_inc(s_add, 16)
                    pool.wait_ge(s_add, tr.t * (16 * 2))
                    pool.sem_inc(s_af, 1)

                def turn(tr, first, left):
                    if first:
                        for ahead in range(3):
                            gather(tr, ahead)
                    if left > 3:
                        if not first:
                            pool.wait_ge(s_xT, tr.t)
                        gather(tr, 3)
                    if not first:
                        add_rows(tr)

                run_turns(pool, turn)

            @block.tensor
            def _(pe):
                def turn_rows(tr, ahead):
                    pe.wait_ge(s_gx[tr.slot(ahead)], tr.landed(ahead, 2))
                    for c in range(KC):
                        for b in range(tr.rows(ahead) // P):
                            ins = pe.transpose(ps_xt[:, c * R + b * P:c * R + b * P + P],
                                               xg[:, tr.slot(ahead), b, c * P:(c + 1) * P], ident[:, :])
                    ins.then_inc(s_xT, 1)

                def layer1(tr, expert, first):
                    for f in range(FC):
                        if f % FQ == 0 and not first:
                            pe.wait_ge(s_ge, tr.t * 4 + (f // FQ - 3))
                        o = ps_s[:, f // FQ, (f % FQ) * R:(f % FQ) * R + tr.rows(0)]
                        n = 0
                        for a, parts in ((0, (0, 1)), (1, (0,))):
                            for k in range(KC):
                                w = w1s[:, bass.ds(expert, 1), a, k, f * P:(f + 1) * P].rearrange("p a f -> p (a f)")
                                for b in parts:
                                    ins = pe.matmul(o, w, xh[:, tr.slot(0) % 2, b, k, 0:tr.rows(0)], start=(n == 0),
                                                    stop=(n == 3 * KC - 1))
                                    n += 1
                        if f % FQ == FQ - 1:
                            ins.then_inc(s_l1, 1)

                def layer2(tr, expert):
                    k = tr.slot(-1)
                    for f in range(FC):
                        if f % FQ == 0:
                            pe.wait_ge(s_hh, tr.t * 4 + (f // FQ - 3))
                        for n, (a, b) in enumerate(HALVES):
                            w = w2s[:, bass.ds(expert, 1), b, f, :].rearrange("p a d -> p (a d)")
                            for c in range(tr.rows(-1) // P):
                                ins = pe.matmul(ps_y[k % 2][:, c * D:(c + 1) * D],
                                                hh[k % 2][:, a, f, c * P:(c + 1) * P], w,
                                                start=(f == 0 and n == 0 and c == 0),
                                                stop=(f == FC - 1 and n == 2 and c == tr.rows(-1) // P - 1))
                    ins.then_inc(s_l2, 1)

                pe.sem_inc(s_l2, L20)
                pe.wait_ge(s_tl, 2)

                def turn(tr, first, left):
                    if first:
                        turn_rows(tr, 0)
                    else:
                        last = pe.value_load(exi[0:1, bass.ds(tr.t - 1, 1)], min_val=0, max_val=NE - 1)
                    if left > 0:
                        expert = pe.value_load(exi[0:1, bass.ds(tr.t, 1)], min_val=0, max_val=NE - 1)
                        pe.wait_ge(s_xh, tr.t + 1)
                        if left > 1:
                            turn_rows(tr, 1)
                        layer1(tr, expert, first)
                    if not first:
                        pe.wait_ge(s_y, tr.t * 2 + (Y0 - 4))
                        layer2(tr, last)

                run_turns(pe, turn)

            @block.scalar
            def _(act):
                act.preload_act_table_set("gelu_and_others")
                act.wait_ge(s_tl, 2)

                def turn(tr, first, left):
                    if not left > 0:
                        return
                    expert = act.value_load(exi[0:1, bass.ds(tr.t, 1)], min_val=0, max_val=NE - 1)
                    for q in range(4):
                        if not first:
                            act.wait_ge(s_hh, tr.t * 4 + (q - 3))
                        act.wait_ge(s_l1, tr.t * 4 + (q + 1))
                        for n in range(FQ):
                            f = q * FQ + n
                            ins = act.activation(hf[:, f * R:f * R + tr.rows(0)],
                                                 ps_s[:, q, n * R:n * R + tr.rows(0)],
                                                 ACT.Gelu, bias=b1T[:, bass.ds(expert, 1), f], scale=1.0 / W_SCALE)
                        ins.then_inc(s_ge, 1)

                run_turns(act, turn)

            @block.vector
            def _(dve):
                dve.sem_inc(s_y, Y0)
                dve.wait_ge(s_tl, 2)
                dve.wait_ge(s_b2, 16)

                def split_rows(tr, ahead):
                    dve.wait_ge(s_xT, tr.t + (ahead + 1))
                    n = tr.rows(ahead)
                    src = ps_xt[:, :].rearrange("p (c t) -> p c t", c=KC)[:, :, 0:n]
                    hi, lo = (xh[:, tr.slot(ahead) % 2, w, :, 0:n] for w in range(2))
                    dve.tensor_copy(hi, src).then_inc(s_xhi, 1)
                    dve.wait_ge(s_xhi, tr.t + (ahead + 1))
                    dve.tensor_tensor(lo, src, hi, ALU.subtract).then_inc(s_xh, 1)

                def split_gelu(tr, q):
                    dve.wait_ge(s_ge, tr.t * 4 + (q + 1))
                    src = hf[:, q * FQ * R:(q + 1) * FQ * R].rearrange("p (c t) -> p c t", c=FQ)
                    src = src[:, :, 0:tr.rows(0)]
                    hi, lo = (hh[tr.slot(0) % 2][:, a, q * FQ:(q + 1) * FQ, 0:tr.rows(0)] for a in range(2))
                    dve.tensor_copy(hi, src).then_inc(s_hhi, 1)
                    dve.wait_ge(s_hhi, tr.t * 4 + (q + 1))
                    dve.tensor_tensor(lo, src, hi, ALU.subtract).then_inc(s_hh, 1)

                def gate_rows(tr, expert):
                    k = tr.slot(-1)
                    dve.wait_ge(s_is[k], tr.landed(-1))
                    dve.wait_ge(s_l2, tr.t + L20)
                    for b in range(tr.rows(-1) // P):
                        dve.scalar_tensor_tensor(
                            out=yo[k][:, b, :], in0=ps_y[k % 2][:, b * D:(b + 1) * D], scalar=1.0 / W_SCALE,
                            in1=b2r[:, bass.ds(expert, 1), :].rearrange("p a d -> p (a d)"), op0=ALU.mult,
                            op1=ALU.add).then_inc(s_yb, 1)
                    for b in range(tr.rows(-1) // P):
                        dve.wait_ge(s_yb, tr.t * 2 + (b - 1))
                        dve.tensor_scalar(yo[k][:, b, :], yo[k][:, b, :], ids_s[:, k, b, 1:2].bitcast(F32), None,
                                          ALU.mult).then_inc(s_y, 1)
                    if tr.rows(-1) < R:
                        dve.sem_inc(s_yb, 1)
                        dve.wait_ge(s_y, tr.t * 2 + (Y0 - 1))
                        dve.sem_inc(s_y, 1)

                def turn(tr, first, left):
                    if first:
                        split_rows(tr, 0)
                    else:
                        expert = dve.value_load(exi[0:1, bass.ds(tr.t - 1, 1)], min_val=0, max_val=NE - 1)
                    if left > 1:
                        if not first:
                            dve.wait_ge(s_l1, tr.t * 4)
                        split_rows(tr, 1)
                    if left > 0:
                        if not first:
                            dve.wait_ge(s_l2, tr.t + (L20 - 1))
                        for q in range(4):
                            split_gelu(tr, q)
                    if not first:
                        gate_rows(tr, expert)

                run_turns(dve, turn)


_INS = ["x", "ctx_1024", "L0_xattn_igate_w", "L0_xattn_igate_b", "L0_xattn_fgate_w", "L0_xattn_fgate_b",
        "L0_xattn_out_w", "L0_ffn_gate_w", "L0_ffn_w1", "L0_ffn_b1", "L0_ffn_w2", "L0_ffn_b2"]


def kernel(**inputs):
    import numpy as np
    import concourse.bacc as bacc
    from concourse.bass_utils import run_bass_kernel_spmd

    nc = bacc.Bacc("TRN2", target_bir_lowering=False, num_devices=1)
    arrays, args = {}, []
    for name in _INS:
        a = np.ascontiguousarray(inputs[name])
        arrays[f"in_{name}"] = a
        args.append(nc.dram_tensor(f"in_{name}", a.shape, mybir.dt.from_np(a.dtype), kind="ExternalInput").ap())
    shape = arrays["in_x"].shape
    args.append(nc.dram_tensor("out_rows", shape, F32, kind="ExternalOutput").ap())
    build(nc, *args)
    r = run_bass_kernel_spmd(nc, [arrays], core_ids=[0])
    return r.results[0]["out_rows"]
```
